# Optimizing a Trainium2 kernel written in Bass

```python
import numpy as np
import jax
import jax.numpy as jnp

def _softmax(x, axis=-1):
    return jax.nn.softmax(x, axis=axis)

def _gelu(x):
    return jax.nn.gelu(x, approximate=True)

def _silu(x):
    return jax.nn.silu(x)

def _sigmoid(x):
    return jax.nn.sigmoid(x)

def _layernorm(x, axis=-1, eps=1e-05):
    m = jnp.mean(x, axis=axis, keepdims=True)
    v = jnp.var(x, axis=axis, keepdims=True)
    return (x - m) / jnp.sqrt(v + eps)

def _scatter_add(tgt, idx, src, axis=0):
    return tgt.at[idx].add(src)

def _segment_sum(src, seg, n):
    return jax.ops.segment_sum(src, seg, n)
kernel_name = 'mk_recurrent_d1_jaxref_r4_85f685'

def setup_inputs(seed: int=0):
    np.random.seed(seed)
    _w = jnp.asarray

    def _L0_attn_setup():
        import jax, jax.numpy as jnp
        import numpy as np
        B, S, D, H = (2, 512, 512, 16)
        HD = D // H
        NEG = jnp.float32(-1000000000.0)
        key = jax.random.key(seed)
        ks = jax.random.split(key, 6)
        slopes = np.array([2 ** (-8.0 * (i + 1) / H) for i in range(H)], dtype=np.float32)
        return {'hidden_states': jax.random.normal(ks[0], (B, S, D), jnp.float32), 'qkv_w': jax.random.normal(ks[1], (3 * D, D), jnp.float32) * (1.0 / np.sqrt(D)), 'qkv_b': jax.random.normal(ks[2], (3 * D,), jnp.float32) * 0.01, 'out_w': jax.random.normal(ks[3], (D, D), jnp.float32) * (1.0 / np.sqrt(D)), 'out_b': jax.random.normal(ks[4], (D,), jnp.float32) * 0.01, 'alibi_slopes': jnp.asarray(slopes)}
    _L0_attn_in = _L0_attn_setup()

    def _L0_ffn_setup():
        import jax, jax.numpy as jnp
        import numpy as np
        B, S, H, E, K, I = (2, 256, 512, 32, 8, 192)
        key = jax.random.key(seed)
        ks = jax.random.split(key, 5)
        scaled = lambda k, shp, fan: jax.random.normal(k, shp, jnp.float32) * fan ** (-0.5)
        return {'hidden_states': jax.random.normal(ks[0], (B, S, H), jnp.float32), 'router_w': scaled(ks[1], (E, H), H), 'w_gate': scaled(ks[2], (E, H, I), H), 'w_up': scaled(ks[3], (E, H, I), H), 'w_down': scaled(ks[4], (E, I, H), I)}
    _L0_ffn_in = _L0_ffn_setup()
    _d = {'L0_attn_hidden_states': _L0_attn_in['hidden_states'], 'L0_attn_qkv_w': _L0_attn_in['qkv_w'], 'L0_attn_qkv_b': _L0_attn_in['qkv_b'], 'L0_attn_out_w': _L0_attn_in['out_w'], 'L0_attn_out_b': _L0_attn_in['out_b'], 'L0_attn_alibi_slopes': _L0_attn_in['alibi_slopes'], 'L0_ffn_router_w': _L0_ffn_in['router_w'], 'L0_ffn_w_gate': _L0_ffn_in['w_gate'], 'L0_ffn_w_up': _L0_ffn_in['w_up'], 'L0_ffn_w_down': _L0_ffn_in['w_down']}
    _x0 = _d['L0_attn_hidden_states']
    _d['L0_attn_hidden_states'] = jax.random.normal(jax.random.fold_in(jax.random.key(seed), 1), (2, 1024, 512), dtype=_x0.dtype)
    del _x0
    return _d

def reference(L0_attn_hidden_states, L0_attn_qkv_w, L0_attn_qkv_b, L0_attn_out_w, L0_attn_out_b, L0_attn_alibi_slopes, L0_ffn_router_w, L0_ffn_w_gate, L0_ffn_w_up, L0_ffn_w_down):

    def _L0_attn_ref(hidden_states, qkv_w, qkv_b, out_w, out_b, alibi_slopes):
        import jax, jax.numpy as jnp
        import numpy as np
        B, S, D, H = (2, 512, 512, 16)
        HD = D // H
        NEG = jnp.float32(-1000000000.0)
        b, s, d = hidden_states.shape
        qkv = hidden_states @ qkv_w.T + qkv_b
        q, k, v = jnp.split(qkv, 3, axis=-1)
        q = q.reshape(b, s, H, HD)
        k = k.reshape(b, s, H, HD)
        v = v.reshape(b, s, H, HD)
        scale = 1.0 / np.sqrt(HD)
        scores = jnp.einsum('bqhd,bkhd->bhqk', q, k) * scale
        pos = jnp.arange(s)
        rel = (pos[None, :] - pos[:, None]).astype(jnp.float32)
        bias = alibi_slopes[:, None, None] * rel
        causal = pos[None, :] <= pos[:, None]
        scores = jnp.where(causal[None, None], scores + bias[None], NEG)
        attn = jax.nn.softmax(scores, axis=-1)
        out = jnp.einsum('bhqk,bkhd->bqhd', attn, v).reshape(b, s, d)
        out = out @ out_w.T + out_b
        return out

    def _L0_ffn_ref(hidden_states, router_w, w_gate, w_up, w_down):
        import jax, jax.numpy as jnp
        import numpy as np
        B, S, H, E, K, I = (2, 256, 512, 32, 8, 192)
        Bq, Sq, Hd = hidden_states.shape
        x = hidden_states.reshape(-1, Hd)
        logits = x @ router_w.T
        probs = jax.nn.softmax(logits.astype(jnp.float32), axis=-1)
        rw, sel = jax.lax.top_k(probs, K)
        rw = rw / jnp.sum(rw, axis=-1, keepdims=True)
        rw = rw.astype(x.dtype)

        def body(acc, operand):
            e, wg, wu, wd = operand
            w_e = jnp.sum(jnp.where(sel == e, rw, jnp.zeros_like(rw)), axis=-1)
            h = jax.nn.silu(x @ wg) * (x @ wu)
            return (acc + h @ wd * w_e[:, None], None)
        acc0 = jnp.zeros_like(x)
        acc, _ = jax.lax.scan(body, acc0, (jnp.arange(E), w_gate, w_up, w_down))
        return acc.reshape(Bq, Sq, Hd)
    x = L0_attn_hidden_states
    xn = _layernorm(x, axis=-1)
    s = _L0_attn_ref(xn, L0_attn_qkv_w, L0_attn_qkv_b, L0_attn_out_w, L0_attn_out_b, L0_attn_alibi_slopes)
    g = _silu(_L0_ffn_ref(xn, L0_ffn_router_w, L0_ffn_w_gate, L0_ffn_w_up, L0_ffn_w_down))
    x = x + s * g
    return x

_drawn_inputs = setup_inputs


def setup_inputs(seed=0):
    import zlib

    import numpy as np

    out = dict(_drawn_inputs(seed))
    spreads = {}
    factors = {'L0_attn_qkv_b': 40.9, 'L0_attn_out_b': 44.5}
    for name, (base, spread) in spreads.items():
        noise = np.random.default_rng([zlib.crc32(name.encode()), seed]).standard_normal(out[name].shape)
        drawn = base * np.exp(spread * noise) if base else spread * noise
        out[name] = jnp.asarray(drawn.astype(out[name].dtype))
    for name, factor in factors.items():
        out[name] = (out[name] * factor).astype(out[name].dtype)
    return out
```

```python
from contextlib import ExitStack

import concourse.bass as bass
from concourse import mybir

ALU = mybir.AluOpType
ACT = mybir.ActivationFunctionType
AX_X = mybir.AxisListType.X
F32 = mybir.dt.float32
F16 = mybir.dt.float16

SX = 16.0
SW = 64.0
UNSCALE = 1.0 / (SX * SW)


def attention_times_moe_kernel(nc, x, qkv_w, qkv_b, out_w, out_b, slopes, router_w, w_gate, w_up, w_down, out):
    B, S, D = x.shape
    H = slopes.shape[0]
    HD = D // H
    E, _, I = w_gate.shape
    P = 128
    T = B * S
    NT = T // P
    C = D // P
    QT = S // P
    RQ = 3 * D // P
    RO = D // P
    NTOK = 512
    TG = T // NTOK
    SUB = NTOK // P
    IA, IB = P, I - P
    EPS = 1e-5
    SS = SX * SX
    assert IB == 64 and TG == 4 and C == 4 and QT == 8 and B == 2

    x_t = x.rearrange("b (t p) d -> p (b t) d", p=P)
    out_t = out.rearrange("b (t p) d -> p (b t) d", p=P)
    qkvw_t = qkv_w.rearrange("(r p) d -> p r d", p=P)
    outw_t = out_w.rearrange("(r p) d -> p r d", p=P)
    qk_dram = nc.dram_tensor("qk_parts", [2, 2 * D, T], F16, kind="Internal").ap()

    with ExitStack() as ctx:
        def sb(name, shape, dt=F32):
            return ctx.enter_context(nc.sbuf_tensor(name, shape, dt))

        def sem(name):
            return ctx.enter_context(nc.semaphore(name))

        bank = ctx.enter_context(nc.psum_tensor("bank", [P, 8, 512], F32))

        ident = sb("ident", [P, P])
        wT = [sb(f"wT{i}", [P, C, RQ + RO, P], F16) for i in range(2)]
        rT = [sb(f"rT{i}", [P, C, E], F16) for i in range(2)]
        xT = [sb(f"xT{i}", [P, C, NT, P], F16) for i in range(2)]
        v_sb = sb("v_sb", [P, NT, H, HD + 1])
        acc = v_sb[:, :, :, :].rearrange("p t h d -> p (t h d)")[:, 0:NT * D].rearrange("p (t d) -> p t d", t=NT)
        o_all = sb("o_all", [P, NT, D])
        route = sb("route", [P, NT, E])
        qk_scale = sb("qk_scale", [P, 8])
        qk_bias = sb("qk_bias", [P, 8])
        v_bias = sb("v_bias", [P, D])
        o_bias = sb("o_bias", [P, D])
        slope = sb("slope", [P, H])
        rwst = sb("rwst", [E, D])
        scratch = sb("scratch", [P, 11264])
        mvs = sb("mvs", [P, NT, 2])
        stats = sb("stats", [P, NT, 6])
        rstd = sb("rstd", [P, NT])
        small = sb("small", [P, 4, NT])
        top8 = sb("top8", [P, NT, 8])
        mn = sb("mn", [P, 2])
        rd = sb("rd", [P, 2])

        def carve(at, shape, dt=F32):
            n = 1
            for d in shape[1:]:
                n *= d
            words = n if dt == F32 else n // 2
            v = scratch[:, at:at + words]
            if dt != F32:
                v = v.bitcast(dt)
            if len(shape) == 3:
                v = v.rearrange("p (a b) -> p a b", a=shape[1])
            return v, at + words

        at = 0
        wst, xn, qk_f, qk_p = [], [], [], [[], []]
        for i in range(4):
            v, at = carve(at, [P, D]); wst.append(v)
        for i in range(2):
            v, at = carve(at, [P, D]); xn.append(v)
        for i in range(4):
            v, at = carve(at, [P, NTOK]); qk_f.append(v)
        for j in range(2):
            for i in range(4):
                v, at = carve(at, [P, NTOK], F16); qk_p[j].append(v)
        rl, at = carve(at, [P, NT, E])
        rr, at = carve(at, [P, NT, E])
        at = 0
        qs, ks, tb, pr, pt, alibi = [], [], [], [], [], []
        for i in range(2):
            v, at = carve(at, [P, S], F16); qs.append(v)
            v, at = carve(at, [P, S], F16); ks.append(v)
        for i in range(2):
            v, at = carve(at, [P, S]); tb.append(v)
        for i in range(2):
            v, at = carve(at, [P, S]); pr.append(v)
        for i in range(2):
            v, at = carve(at, [P, QT, P]); pt.append(v)
        for i in range(2):
            v, at = carve(at, [P, S]); alibi.append(v)
        rel, at = carve(at, [P, S])
        assert at <= 11264, at
        at = 0
        wg_raw, wu_raw, wda_raw, wdb_raw, wgu16, wda16, wdb16 = ([] for _ in range(7))
        for i in range(1):
            v, at = carve(at, [P, C, I]); wg_raw.append(v)
            v, at = carve(at, [P, C, I]); wu_raw.append(v)
            v, at = carve(at, [P, D]); wda_raw.append(v)
            v, at = carve(at, [P, D]); wdb_raw.append(v)
        for i in range(2):
            w, d, b = [], [], []
            for j in range(2):
                v, at = carve(at, [P, C * 3, P], F16); w.append(v.rearrange("p (c m) q -> p c m q", c=C))
                v, at = carve(at, [P, D], F16); d.append(v)
                v, at = carve(at, [P, D], F16); b.append(v)
            wgu16.append(w); wda16.append(d); wdb16.append(b)
        tA, at = carve(at, [P, NTOK])
        tB, at = carve(at, [P, NTOK])
        aA = tA
        aB = tB
        h_f, at = carve(at, [P, 2, NTOK])
        assert at <= 11264, at
        h16 = sb("h16", [P, 2, 3, NTOK], F16)
        hA = [[h16[:, i, 0, :], h16[:, i, 1, :]] for i in range(2)]
        hB = [h16[:, i, 2, :] for i in range(2)]
        at = 0
        ost, oT, xr, th, ga, fin = [], [], [], [], [], []
        for i in range(2):
            v, at = carve(at, [P, D]); ost.append(v)
            v, at = carve(at, [P, C, P], F16)
            w, at = carve(at, [P, C, P], F16); oT.append([v, w])
            v, at = carve(at, [P, D]); xr.append(v)
            v, at = carve(at, [P, D]); th.append(v)
            v, at = carve(at, [P, D]); ga.append(v)
            v, at = carve(at, [P, D]); fin.append(v)

        const_ld = [sem(f"const_ld{i}") for i in range(6)]
        x_ld = [sem(f"x_ld{i}") for i in range(4)]
        wst_ld = [sem(f"wst_ld{i}") for i in range(4)]
        ident_ok = sem("ident_ok")
        tp_full = sem("tp_full")
        tp_hi = sem("tp_hi")
        tp_lo = sem("tp_lo")
        var_ok = sem("var_ok")
        std_ok = sem("std_ok")
        rstd_ok = sem("rstd_ok")
        bias_ok = sem("bias_ok")
        xn_ok = sem("xn_ok")
        proj_full = sem("proj_full")
        proj_free = sem("proj_free")
        qkf_free = sem("qkf_free")
        qk_hi = sem("qk_hi")
        qk_st = [sem(f"qk_st{i}") for i in range(4)]
        logits_ok = sem("logits_ok")
        ev_act = sem("ev_act")
        dch = sem("dch")
        pch = sem("pch")
        qk_in = [sem(f"qk_in{i}") for i in range(2)]
        slope_rel = sem("slope_rel")
        alibi_ok = sem("alibi_ok")
        s_full = sem("s_full")
        scores_seen = sem("scores_seen")
        slope_seen = sem("slope_seen")
        s_free = sem("s_free")
        p_ok = sem("p_ok")
        pt_full = sem("pt_full")
        pt_out = [sem("pt_out_act"), sem("pt_out_dve")]
        o_full = sem("o_full")
        o_out = sem("o_out")
        wraw_ld = sem("wraw_ld")
        w16_hi = sem("w16_hi")
        w16_lo = sem("w16_lo")
        gu_full = [sem(f"gu_full{i}") for i in range(3)]
        tanh_ok = sem("tanh_ok")
        aA_ok = sem("aA_ok")
        aB_ok = sem("aB_ok")
        hf_ok = sem("hf_ok")
        h_hi = sem("h_hi")
        hA_lo = sem("hA_lo")
        hB_lo = sem("hB_lo")
        y_full = sem("y_full")
        y_free = sem("y_free")
        acc_zero = sem("acc_zero")
        ost_ok = sem("ost_ok")
        ot_full = sem("ot_full")
        ot_hi = sem("ot_hi")
        ot_lo = sem("ot_lo")
        s_out = sem("s_out")
        th_ok = sem("th_ok")
        fin_ok = sem("fin_ok")
        xr_ld = [sem(f"xr_ld{i}") for i in range(2)]
        out_st = [sem(f"out_st{i}") for i in range(2)]

        block = ctx.enter_context(nc.Block())

        NI_W = RQ + RO
        NI_R = NI_W + 1
        NI = NI_R + NT
        NPROJ = 8 * TG
        Q_TILES = B * H * QT
        GROUPS = [(hh, b, i) for hh in range(2) for b in range(B) for i in range(QT)]
        NG = len(GROUPS)

        def pt_groups(i):
            return [range(0, min(4, i + 1))] + ([range(4, i + 1)] if i >= 4 else [])

        PT_HEAD = sum(len(pt_groups(i)) for i in range(QT))
        PT_ENG = [g % 2 for g in range(PT_HEAD)]
        PT_CNT = [[PT_ENG[:g + 1].count(e) for e in range(2)] for g in range(PT_HEAD)]
        assert PT_HEAD % 2 == 0

        @block.sync
        def _(sp):
            for s in range(TG):
                sp.sem_inc(qk_st[s], 16)
            for s in range(2):
                sp.sem_inc(out_st[s], 16)
            for i in range(4):
                sp.dma_start(o_all[:, 4 * i:4 * i + 4, :], x_t[:, 4 * i:4 * i + 4, :]).then_inc(x_ld[i], 16)
            sp.dma_start(qk_bias[:, :], qkv_b[0:2 * D].rearrange("(r p) -> p r", p=P),
                         allow_slow_non_contiguous=True).then_inc(const_ld[0], 16)
            sp.dma_start(v_bias[:, :], qkv_b[2 * D:3 * D].partition_broadcast(P)).then_inc(const_ld[1], 16)
            sp.dma_start(o_bias[:, :], out_b.partition_broadcast(P)).then_inc(const_ld[2], 16)
            sp.dma_start(slope[:, :], slopes.partition_broadcast(P)).then_inc(const_ld[3], 16)
            sp.dma_start(rwst[:, :], router_w).then_inc(const_ld[4], 16)
            for s in range(4):
                sp.dma_start(wst[s], qkvw_t[:, s, :]).then_inc(wst_ld[s], 16)
            with sp.Fori(0, RQ // 4 - 1) as g:
                for s in range(4):
                    sp.wait_ge(tp_full, g * 4 + (s + 1))
                    sp.dma_start(wst[s], qkvw_t[:, bass.ds(g * 4 + (s + 4), 1), :].rearrange("p r d -> p (r d)"))\
                        .then_inc(wst_ld[s], 16)
            for s in range(RO):
                sp.wait_ge(tp_full, RQ + s - 3)
                sp.dma_start(wst[s], outw_t[:, s, :]).then_inc(wst_ld[s], 16)
            with sp.Fori(0, 8) as r:
                for s in range(TG):
                    sp.wait_ge(qkf_free, r * 4 + (s + 5))
                    for j in range(2):
                        sp.dma_start(qk_dram[j, bass.ds(r * P, P), s * NTOK:(s + 1) * NTOK],
                                     qk_p[j][s]).then_inc(qk_st[s], 16)
            for s in range(TG):
                sp.wait_ge(qk_st[s], 8 * 2 * 16 + 16)
            sp.wait_ge(alibi_ok, 1)

            def load_head(row, b):
                tok = slice(b * S, (b + 1) * S)
                for k, j in enumerate((0, 0, 1)):
                    sp.dma_start(qs[b][HD * k:HD * (k + 1), :],
                                 qk_dram[j, bass.ds(row, HD), tok]).then_inc(qk_in[b], 16)
                for k, j in enumerate((0, 1, 0)):
                    sp.dma_start(ks[b][HD * k:HD * (k + 1), :],
                                 qk_dram[j, bass.ds(row + D, HD), tok]).then_inc(qk_in[b], 16)

            for b in range(B):
                load_head(0, b)
            with sp.Fori(0, H - 1) as h:
                for b in range(B):
                    sp.wait_ge(s_full, h * (B * QT) + (b + 1) * QT)
                    load_head(h * HD + HD, b)
            sp.wait_ge(o_out, Q_TILES + 2)
            with sp.Fori(0, E) as e:
                sp.wait_ge(w16_lo, e + 1)
                sp.dma_start(wg_raw[0], w_gate[bass.ds(e, 1), :, :].rearrange("e (c p) i -> p (e c) i", p=P))\
                    .then_inc(wraw_ld, 16)
                sp.dma_start(wu_raw[0], w_up[bass.ds(e, 1), :, :].rearrange("e (c p) i -> p (e c) i", p=P))\
                    .then_inc(wraw_ld, 16)
                sp.dma_start(wda_raw[0], w_down[bass.ds(e, 1), 0:IA, :].rearrange("e p d -> p (e d)"))\
                    .then_inc(wraw_ld, 16)
                for k in range(2):
                    sp.dma_start(wdb_raw[0][IB * k:IB * (k + 1), :],
                                 w_down[bass.ds(e, 1), IA:I, :].rearrange("e p d -> p (e d)"))\
                        .then_inc(wraw_ld, 16)
            sp.wait_ge(y_free, 4 + E * NT)
            with sp.Fori(0, NT // 2) as g:
                for s in range(2):
                    sp.wait_ge(fin_ok, g * 2 + 2)
                    sp.dma_start(xr[s], x_t[:, bass.ds(g * 2 + s, 1), :].rearrange("p t d -> p (t d)")).then_inc(xr_ld[s], 16)
                for s in range(2):
                    sp.wait_ge(fin_ok, g * 2 + (s + 3))
                    sp.dma_start(out_t[:, bass.ds(g * 2 + s, 1), :].rearrange("p t d -> p (t d)"), fin[s]).then_inc(out_st[s], 16)
            for s in range(2):
                sp.wait_ge(out_st[s], NT // 2 * 16 + 16)

        @block.tensor
        def _(pe):
            pe.sem_inc(pt_full, 3)
            pe.sem_inc(o_full, 2)
            pe.sem_inc(y_full, 8)
            pe.sem_inc(s_out, 2)
            pe.sem_inc(ot_full, 2)
            pe.wait_ge(ident_ok, 1)

            def turn(src, rows, n_bank):
                view = bank[:, n_bank, :].rearrange("p (c q) -> p c q", c=C)
                for c in range(C):
                    last = pe.transpose(view[:, c, 0:rows], src[0:rows, c * P:(c + 1) * P], ident[0:rows, 0:rows])
                return last.then_inc(tp_full, 1)

            with pe.Fori(0, RQ // 4) as g:
                for s in range(4):
                    pe.wait_ge(wst_ld[s], g * 16 + 16)
                    pe.wait_ge(tp_lo, g * 4 + (s + 1))
                    turn(wst[s], P, s % 2)
            for s in range(RO):
                pe.wait_ge(wst_ld[s], (RQ // 4 + 1) * 16)
                pe.wait_ge(tp_lo, RQ + s + 1)
                turn(wst[s], P, s % 2)
            pe.wait_ge(const_ld[4], 16)
            pe.wait_ge(tp_lo, NI_W + 1)
            turn(rwst, E, 0)
            with pe.Fori(0, NT // 2) as g:
                for s in range(2):
                    pe.wait_ge(xn_ok, g * 2 + (s + 1))
                    pe.wait_ge(tp_lo, g * 2 + (NI_R + s + 1))
                    turn(xn[s], P, (1 + s) % 2)
            pe.wait_ge(tp_lo, NI + 2)

            def three(o, aT, b, first=True, last=True, **kw):
                for k, (i, j) in enumerate(((0, 0), (0, 1), (1, 0))):
                    ins = pe.matmul(o, aT(i), b(j), start=first and k == 0, stop=last and k == 2, **kw)
                return ins

            with pe.Fori(0, 8) as r:
                for s in range(TG):
                    pe.wait_ge(proj_free, r * 4 + (s + 1))
                    for c in range(C):
                        ins = three(bank[:, s, :],
                                    lambda i: wT[i][:, c, bass.ds(r, 1), :].rearrange("p r q -> p (r q)"),
                                    lambda j: xT[j][:, c, SUB * s:SUB * (s + 1), :].rearrange("p t q -> p (t q)"),
                                    c == 0, c == C - 1)
                    ins.then_inc(proj_full, 1)
            with pe.Fori(0, NT // 4) as g:
                for s in range(4):
                    pe.wait_ge(proj_free, g * 4 + (NPROJ + s + 1))
                    for c in range(C):
                        ins = three(bank[:, s, :],
                                    lambda i: xT[i][:, c, bass.ds(g * 4 + s, 1), :].rearrange("p t q -> p (t q)"),
                                    lambda j: wT[j][:, c, 8:12, :].rearrange("p r q -> p (r q)"),
                                    c == 0, c == C - 1)
                    ins.then_inc(proj_full, 1)
            for t in range(NT):
                for c in range(C):
                    ins = three(bank[:, 4, t * E:(t + 1) * E], lambda i: xT[i][:, c, t, :],
                                lambda j: rT[j][:, c, :], c == 0, c == C - 1)
            ins.then_inc(logits_ok, 1)
            pe.wait_ge(proj_free, NPROJ + NT + 4)
            pe.wait_ge(ev_act, 1)

            def scores(h, b, i, n):
                if i == 0:
                    pe.wait_ge(qk_in[b], h * 96 + 96)
                pe.wait_ge(s_free, n + 1)
                keys = (i + 1) * P
                for a in range(0, keys, 512):
                    w = min(512, keys - a)
                    ins = pe.matmul(bank[:, 2 * (i % 2) + a // 512, 0:w], qs[b][0:3 * HD, i * P:(i + 1) * P],
                                    ks[b][0:3 * HD, a:a + w], start=True, stop=True)
                ins.then_inc(s_full, 1)

            def values(h, b, i, n, half):
                base = sum(len(pt_groups(k)) for k in range(i))
                pe.wait_ge(p_ok, n + 3)
                groups = pt_groups(i)
                for k, blocks in enumerate(groups):
                    g = base + k
                    eng = PT_ENG[g]
                    pe.wait_ge(pt_out[eng], half + PT_CNT[g][eng])
                    for j, kb in enumerate(blocks):
                        ins = pe.transpose(bank[:, 4 + g % 2, j * P:(j + 1) * P], pr[i % 2][:, kb * P:(kb + 1) * P],
                                           ident[:, :])
                    ins.then_inc(pt_full, 1)
                for k, blocks in enumerate(groups):
                    g = base + k
                    eng = PT_ENG[g]
                    pe.wait_ge(pt_out[eng], half + (PT_CNT[g][eng] + 1))
                    if k == 0:
                        pe.wait_ge(o_out, n + 1)
                    for kb in blocks:
                        vv = v_sb[:, b * QT + kb, bass.ds(h, 1), :].rearrange("p h d -> p (h d)")
                        ins = pe.matmul(bank[:, 6 + i % 2, 0:HD + 1], pt[i % 2][:, kb, :], vv,
                                        start=(kb == 0), stop=(kb == i))
                ins.then_inc(o_full, 1)

            with pe.Fori(0, H // 2) as g:
                for q, (hh, b, i) in enumerate(GROUPS):
                    if q == 0:
                        scores(g * 2, b, i, g * NG)
                    if q + 1 < NG:
                        h1, b1, i1 = GROUPS[q + 1]
                        scores(g * 2 + h1, b1, i1, g * NG + (q + 1))
                    values(g * 2 + hh, b, i, g * NG + q, g * (2 * PT_HEAD) + (hh * B + b) * (PT_HEAD // 2))

            pe.wait_ge(o_out, Q_TILES + 2)
            pe.wait_ge(s_free, Q_TILES + 2)

            def gate_up(e, es, tg, n):
                if tg == 0:
                    pe.wait_ge(w16_lo, e + 2)
                for m in range(3):
                    if n is not FIRST:
                        pe.wait_ge(aA_ok, n) if m == 0 else pe.wait_ge(hf_ok, n * 2 + m)
                    for c in range(C):
                        ins = three(bank[:, m, :], lambda i: wgu16[es][i][:, c, m, :],
                                    lambda j: xT[j][:, c, SUB * tg:SUB * (tg + 1), :].rearrange("p t q -> p (t q)"),
                                    c == 0, c == C - 1)
                    ins.then_inc(gu_full[m], 1)

            def down(es, n, k):
                pe.wait_ge(hA_lo, n + 2)
                pe.wait_ge(hB_lo, n + 1)
                for s in range(SUB):
                    cols = slice(s * P, (s + 1) * P)
                    pe.wait_ge(y_free, n * 4 + (s + 1))
                    y = bank[:, 3 + s, :]
                    three(y, lambda i: hA[k][i][:, cols], lambda j: wda16[es][j], True, False)
                    pe.matmul(y, hB[k][:, cols], wdb16[es][0], start=False, stop=False)
                    pe.matmul(y, hB[k][0:IB, cols], wdb16[es][1][0:IB, :], start=False, stop=True)\
                        .then_inc(y_full, 1)

            def expert_pair(g, tail):
                for s in range(8):
                    if s < 7:
                        gate_up(g * 2 + (s + 1) // 4, (s + 1) // 4, (s + 1) % 4, g * 8 + (s + 1))
                    elif not tail:
                        gate_up(g * 2 + 2, 0, 0, g * 8 + 8)
                    down(s // 4, g * 8 + s, s % 2)

            FIRST = None
            gate_up(0, 0, 0, FIRST)
            with pe.Fori(0, E // 2 - 1) as g:
                expert_pair(g, False)
            expert_pair(E // 2 - 1, True)
            pe.wait_ge(y_free, 4 + E * NT)

            with pe.Fori(0, NT // 2) as g:
                for s in range(2):
                    pe.wait_ge(ost_ok, g * 2 + (s + 1))
                    pe.wait_ge(ot_lo, g * 2 + (s + 1))
                    view = bank[:, s, :].rearrange("p (c q) -> p c q", c=C)
                    for c in range(C):
                        ins = pe.transpose(view[:, c, :], ost[s][:, c * P:(c + 1) * P], ident[:, :])
                    ins.then_inc(ot_full, 1)
                for s in range(2):
                    pe.wait_ge(ot_lo, g * 2 + (s + 3))
                    pe.wait_ge(fin_ok, g * 2 + 2)
                    for c in range(C):
                        ins = three(bank[:, 2 + s, :], lambda i: oT[s][i][:, c, :],
                                    lambda j: wT[j][:, c, 12:16, :].rearrange("p r q -> p (r q)"),
                                    c == 0, c == C - 1)
                    ins.then_inc(s_out, 1)

        @block.scalar
        def _(act):
            act.sem_inc(pt_out[0], 1)
            act.sem_inc(p_ok, 2)
            act.wait_ge(var_ok, 1)
            act.activation(small[:, 0, :], small[:, 1, :], ACT.Sqrt).then_inc(std_ok, 1)

            def bank4(n):
                return bank[:, n, :].rearrange("p (c q) -> p c q", c=C)

            with act.Fori(0, (RQ + RO) // 4) as g:
                for s in range(4):
                    act.wait_ge(tp_full, g * 4 + (s + 1))
                    act.activation(wT[0][:, :, bass.ds(g * 4 + s, 1), :].rearrange("p c r q -> p c (r q)"),
                                   bank4(s % 2), ACT.Copy, scale=SW).then_inc(tp_hi, 1)
            act.wait_ge(tp_full, NI_R)
            act.activation(rT[0][:, :, :], bank4(0)[:, :, 0:E], ACT.Copy, scale=SW).then_inc(tp_hi, 1)
            with act.Fori(0, NT // 2) as g:
                for s in range(2):
                    act.wait_ge(tp_full, g * 2 + (NI_R + s + 1))
                    act.activation(xT[0][:, :, bass.ds(g * 2 + s, 1), :].rearrange("p c t q -> p c (t q)"),
                                   bank4((1 + s) % 2), ACT.Copy, scale=SX).then_inc(tp_hi, 1)
            with act.Fori(0, 8) as r:
                for s in range(TG):
                    act.wait_ge(proj_free, r * 4 + (s + 5))
                    act.wait_ge(qk_st[s], r * 32 + 16)
                    act.activation(qk_p[0][s], qk_f[s], ACT.Copy).then_inc(qk_hi, 1)
            act.wait_ge(rstd_ok, 2)
            act.activation(rl, rr, ACT.Exp).then_inc(ev_act, 1)

            PT_OF = [len(pt_groups(i)) for _, _, i in GROUPS]

            def softmax(q, i, n, g):
                act.wait_ge(s_free, n + 3)
                act.wait_ge(pt_full, g * (4 * PT_HEAD) + (sum(PT_OF[:q - 1]) + 3 if q else 3 - PT_OF[-1]))
                keys = (i + 1) * P
                act.activation(pr[i % 2][:, 0:keys], tb[i % 2][:, 0:keys], ACT.Exp, scale=-1.0,
                               bias=mn[:, i % 2:i % 2 + 1]).then_inc(p_ok, 1)

            def empty(i, g, copy):
                first = sum(len(pt_groups(k)) for k in range(i))
                blocks = pt_groups(i)[g - first]
                w = len(blocks) * P
                dst = pt[i % 2][:, blocks[0]:blocks[0] + len(blocks), :].rearrange("p k q -> p (k q)")
                copy(dst, bank[:, 4 + g % 2, 0:w])

            def head_bias(h, hh):
                act.activation(alibi[hh], rel, ACT.Copy, scale=slope[:, bass.ds(h, 1)]).then_inc(slope_rel, 1)

            def pair_softmax(pair, tail):
                for q, (hh, b, i) in enumerate(GROUPS):
                    softmax(q, i, pair * NG + q, pair)
                    base = sum(len(pt_groups(k)) for k in range(i))
                    for g in range(base, base + len(pt_groups(i))):
                        if PT_ENG[g] == 0:
                            act.wait_ge(pt_full, pair * (4 * PT_HEAD) + ((hh * B + b) * PT_HEAD + g + 4))
                            act.wait_ge(o_full, pair * NG + (q + 1))
                            empty(i, g, lambda d, s_: act.activation(d, s_, ACT.Copy).then_inc(pt_out[0], 1))
                    if q % 16 == 15 and not tail:
                        head_bias(pair * 2 + (hh + 2), hh)

            act.wait_ge(alibi_ok, 1)
            for hh in range(2):
                head_bias(hh, hh)
            with act.Fori(0, H // 2 - 1) as pair:
                pair_softmax(pair, False)
            pair_softmax(H // 2 - 1, True)

            def split_hi(e, es, freed):
                act.wait_ge(wraw_ld, e * 80 + 80)
                if freed is not None:
                    act.wait_ge(y_full, freed)
                w = wgu16[es][0]
                act.activation(w[:, :, 0, :], wg_raw[0][:, :, 0:IA], ACT.Copy, scale=SW)
                act.activation(w[:, :, 1, :], wu_raw[0][:, :, 0:IA], ACT.Copy, scale=SW)
                act.activation(w[:, :, 2, 0:IB], wg_raw[0][:, :, IA:I], ACT.Copy, scale=SW)
                act.activation(w[:, :, 2, IB:P], wu_raw[0][:, :, IA:I], ACT.Copy, scale=SW)
                act.activation(wda16[es][0], wda_raw[0], ACT.Copy, scale=SW)
                act.activation(wdb16[es][0], wdb_raw[0], ACT.Copy, scale=SW).then_inc(w16_hi, 1)

            def hidden_act(n, k, used):
                act.wait_ge(gu_full[0], n + 1)
                act.wait_ge(hf_ok, n * 2 + 2)
                act.activation(tA, bank[:, 0, :], ACT.Tanh, scale=0.5 * UNSCALE).then_inc(tanh_ok, 1)
                act.wait_ge(gu_full[2], n + 1)
                act.activation(tB[0:IB, :], bank[0:IB, 2, :], ACT.Tanh, scale=0.5 * UNSCALE).then_inc(tanh_ok, 1)
                act.wait_ge(y_full, used)
                act.wait_ge(hf_ok, n * 2 + 3)
                act.activation(hA[k][0], h_f[:, 0, :], ACT.Copy).then_inc(h_hi, 1)
                act.wait_ge(hf_ok, n * 2 + 4)
                act.activation(hB[k][0:IB, :], h_f[0:IB, 1, :], ACT.Copy).then_inc(h_hi, 1)

            def pair_act(g, tail):
                for s in range(8):
                    hidden_act(g * 8 + s, s % 2, g * 32 + (4 * s + 4))
                    if s == 0:
                        split_hi(g * 2 + 1, 1, g * 32 + 8)
                    if s == 4 and not tail:
                        split_hi(g * 2 + 2, 0, g * 32 + 24)

            split_hi(0, 0, None)
            with act.Fori(0, E // 2 - 1) as g:
                pair_act(g, False)
            pair_act(E // 2 - 1, True)

            with act.Fori(0, NT // 2) as g:
                for s in range(2):
                    act.wait_ge(ot_full, g * 2 + (s + 3))
                    act.wait_ge(s_out, g * 2 + 2)
                    act.activation(oT[s][0], bank4(s), ACT.Copy, scale=SX).then_inc(ot_hi, 1)
                for s in range(2):
                    act.wait_ge(fin_ok, g * 2 + 2)
                    act.activation(th[s], acc[:, bass.ds(g * 2 + s, 1), :].rearrange("p t d -> p (t d)"),
                                   ACT.Tanh, scale=0.5).then_inc(th_ok, 1)

        @block.vector
        def _(dve):
            dve.sem_inc(tp_lo, 2)
            dve.sem_inc(proj_free, 4)
            dve.sem_inc(s_free, 2)
            dve.sem_inc(pt_out[1], 1)
            dve.sem_inc(o_out, 2)
            dve.sem_inc(y_free, 4)
            dve.sem_inc(ot_lo, 2)
            dve.sem_inc(hf_ok, 2)
            dve.sem_inc(w16_lo, 1)
            dve.sem_inc(fin_ok, 2)

            def bank4(n):
                return bank[:, n, :].rearrange("p (c q) -> p c q", c=C)

            for i in range(4):
                dve.wait_ge(x_ld[i], 16)
                for t in range(4 * i, 4 * i + 4):
                    ins = dve.bn_stats(stats[:, t, :], o_all[:, t, :])
            ins.then_inc(dch, 1)
            dve.wait_ge(dch, 1)
            for t in range(NT):
                ins = dve.bn_aggr(mvs[:, t, :], stats[:, t, :])
            ins.then_inc(dch, 1)
            dve.wait_ge(dch, 2)
            dve.tensor_scalar(small[:, 1, :], mvs[:, :, 1], EPS, None, ALU.add).then_inc(var_ok, 1)
            dve.wait_ge(std_ok, 1)
            dve.reciprocal(rstd[:, :], small[:, 0, :]).then_inc(dch, 1)
            dve.wait_ge(dch, 3)
            dve.wait_ge(const_ld[3], 16)
            dve.tensor_scalar(slope[:, :], slope[:, :], SS, None, ALU.mult).then_inc(rstd_ok, 1)
            dve.memset(qk_scale[:, 0:4], UNSCALE * SX * HD ** -0.5)
            dve.memset(qk_scale[:, 4:8], UNSCALE * SX)
            dve.wait_ge(const_ld[0], 16)
            dve.tensor_scalar(qk_bias[:, 0:4], qk_bias[:, 0:4], SX * HD ** -0.5, None, ALU.mult)
            dve.tensor_scalar(qk_bias[:, 4:8], qk_bias[:, 4:8], SX, None, ALU.mult).then_inc(dch, 1)
            dve.wait_ge(dch, 4)

            with dve.Fori(0, (RQ + RO) // 4) as g:
                for s in range(4):
                    hi, lo = (wT[i][:, :, bass.ds(g * 4 + s, 1), :].rearrange("p c r q -> p c (r q)") for i in range(2))
                    dve.wait_ge(tp_hi, g * 4 + (s + 1))
                    dve.scalar_tensor_tensor(out=lo, in0=bank4(s % 2), scalar=SW, in1=hi,
                                             op0=ALU.mult, op1=ALU.subtract).then_inc(tp_lo, 1)
            dve.wait_ge(tp_hi, NI_R)
            dve.scalar_tensor_tensor(out=rT[1][:, :, :], in0=bank4(0)[:, :, 0:E], scalar=SW, in1=rT[0][:, :, :],
                                     op0=ALU.mult, op1=ALU.subtract).then_inc(tp_lo, 1)

            def normalise(t, s):
                dve.wait_ge(tp_full, t + (NI_R - 1))
                dve.tensor_scalar(xn[s], o_all[:, bass.ds(t, 1), :].rearrange("p t d -> p (t d)"),
                                  mvs[:, bass.ds(t, 1), 0:1].rearrange("p t d -> p (t d)"), rstd[:, bass.ds(t, 1)],
                                  ALU.subtract, ALU.mult).then_inc(xn_ok, 1)

            def x_lo(t, s):
                hi, lo = (xT[i][:, :, bass.ds(t, 1), :].rearrange("p c t q -> p c (t q)") for i in range(2))
                dve.wait_ge(tp_hi, t + (NI_R + 1))
                dve.scalar_tensor_tensor(out=lo, in0=bank4((1 + s) % 2), scalar=SX, in1=hi,
                                         op0=ALU.mult, op1=ALU.subtract).then_inc(tp_lo, 1)

            normalise(0, 0)
            with dve.Fori(0, NT // 2 - 1) as g:
                for s in range(2):
                    normalise(g * 2 + (s + 1), (s + 1) % 2)
                    x_lo(g * 2 + s, s)
            normalise(NT - 1, 1)
            x_lo(NT - 2, 0)
            x_lo(NT - 1, 1)
            with dve.Fori(0, 8) as r:
                for s in range(TG):
                    dve.wait_ge(proj_full, r * 4 + (s + 1))
                    dve.wait_ge(qkf_free, r * 4 + (s + 1))
                    dve.tensor_scalar(qk_f[s], bank[:, s, :], qk_scale[:, bass.ds(r, 1)], qk_bias[:, bass.ds(r, 1)],
                                      ALU.mult, ALU.add).then_inc(proj_free, 1)
            dve.wait_ge(const_ld[1], 16)
            with dve.Fori(0, NT // 4) as g:
                for s in range(4):
                    dve.wait_ge(proj_full, g * 4 + (NPROJ + s + 1))
                    dve.scalar_tensor_tensor(
                        out=v_sb[:, bass.ds(g * 4 + s, 1), :, 0:HD].rearrange("p t h d -> p (t h) d"),
                        in0=bank[:, s, :].rearrange("p (h d) -> p h d", h=H), scalar=UNSCALE,
                        in1=v_bias[:, :].rearrange("p (h d) -> p h d", h=H),
                        op0=ALU.mult, op1=ALU.add).then_inc(proj_free, 1)
            dve.wait_ge(logits_ok, 1)
            lg = bank[:, 4, :].rearrange("p (t e) -> p t e", e=E)
            dve.tensor_scalar(rl, lg, UNSCALE, None, ALU.mult).then_inc(dch, 1)
            dve.wait_ge(dch, 5)
            dve.tensor_reduce(small[:, 2, :], rl, AX_X, ALU.max).then_inc(dch, 1)
            dve.wait_ge(dch, 6)
            dve.tensor_tensor(rr, rl, small[:, 2, :].unsqueeze(2).broadcast_to([P, NT, E]), ALU.subtract)\
                .then_inc(rstd_ok, 1)
            dve.wait_ge(ev_act, 1)
            for t in range(NT):
                ins = dve.max(top8[:, t, :], rl[:, t, :])
            ins.then_inc(dch, 1)
            dve.wait_ge(dch, 7)
            for t in range(NT):
                dve.match_replace(rr[:, t, :], top8[:, t, :], rl[:, t, :], 0.0)
            dve.tensor_reduce(small[:, 3, :], top8[:, :, :], AX_X, ALU.add).then_inc(dch, 1)
            dve.wait_ge(dch, 8)
            dve.tensor_scalar(small[:, 2, :], small[:, 3, :], 1.0 / UNSCALE, None, ALU.mult).then_inc(dch, 1)
            dve.tensor_tensor(rr, rl, rr, ALU.subtract).then_inc(dch, 1)
            dve.wait_ge(dch, 10)
            dve.reciprocal(small[:, 3, :], small[:, 2, :]).then_inc(dch, 1)
            dve.wait_ge(dch, 11)
            dve.tensor_tensor(route[:, :, :], rr, small[:, 3, :].unsqueeze(2).broadcast_to([P, NT, E]), ALU.mult)\
                .then_inc(rstd_ok, 1)

            def take_output(h, b, i, n):
                dve.wait_ge(o_full, n + 3)
                o = bank[:, 6 + i % 2, :]
                dve.reciprocal(rd[:, i % 2:i % 2 + 1], o[:, HD:HD + 1]).then_inc(dch, 1)
                dve.wait_ge(dch, n + 12)
                dve.tensor_scalar(o_all[:, b * QT + i, bass.ds(h * HD, HD)], o[:, 0:HD], rd[:, i % 2:i % 2 + 1],
                                  None, ALU.mult).then_inc(o_out, 1)

            def empty_dve(g2, hh, b, i, q):
                base = sum(len(pt_groups(k)) for k in range(i))
                for g in range(base, base + len(pt_groups(i))):
                    if PT_ENG[g] == 1:
                        dve.wait_ge(pt_full, g2 * (4 * PT_HEAD) + ((hh * B + b) * PT_HEAD + g + 4))
                        dve.wait_ge(o_full, g2 * NG + (q + 1))
                        blocks = pt_groups(i)[g - base]
                        dve.tensor_copy(
                            pt[i % 2][:, blocks[0]:blocks[0] + len(blocks), :].rearrange("p k q -> p (k q)"),
                            bank[:, 4 + g % 2, 0:len(blocks) * P]).then_inc(pt_out[1], 1)

            with dve.Fori(0, H // 2) as g2:
                for q, (hh, b, i) in enumerate(GROUPS):
                    keys = (i + 1) * P
                    if q % (B * QT) == 0:
                        dve.wait_ge(alibi_ok, g2 * 2 + (hh + 2))
                    dve.wait_ge(s_full, g2 * NG + (q + 1))
                    dve.wait_ge(p_ok, g2 * NG + (q + 1))
                    dve.sem_inc(scores_seen, 1)
                    dve.tensor_tensor_reduce(
                        tb[i % 2][:, 0:keys],
                        bank[:, 2 * (i % 2):2 * (i % 2) + 2, :].rearrange("p a k -> p (a k)")[:, 0:keys],
                        alibi[hh][:, S - keys:S], -1.0 / SS, 3.0e38, ALU.add, ALU.min,
                        mn[:, i % 2:i % 2 + 1]).then_inc(s_free, 1)
                    for q0 in ([q - 1] if q else []) + ([q] if q == NG - 1 else []):
                        h0, b0, i0 = GROUPS[q0]
                        empty_dve(g2, h0, b0, i0, q0)
                        take_output(g2 * 2 + h0, b0, i0, g2 * NG + q0)

            def split_lo(e, es):
                dve.wait_ge(w16_hi, e + 1)
                hi, lo = wgu16[es]
                for d, raw, h_ in ((lo[:, :, 0, :], wg_raw[0][:, :, 0:IA], hi[:, :, 0, :]),
                                   (lo[:, :, 1, :], wu_raw[0][:, :, 0:IA], hi[:, :, 1, :]),
                                   (lo[:, :, 2, 0:IB], wg_raw[0][:, :, IA:I], hi[:, :, 2, 0:IB]),
                                   (lo[:, :, 2, IB:P], wu_raw[0][:, :, IA:I], hi[:, :, 2, IB:P]),
                                   (wda16[es][1], wda_raw[0], wda16[es][0]),
                                   (wdb16[es][1][0:IB, :], wdb_raw[0][0:IB, :], wdb16[es][0][0:IB, :])):
                    ins = dve.scalar_tensor_tensor(out=d, in0=raw, scalar=SW, in1=h_,
                                                   op0=ALU.mult, op1=ALU.subtract)
                ins.then_inc(w16_lo, 1)

            def hidden(n):
                dve.wait_ge(tanh_ok, n * 2 + 1)
                dve.scalar_tensor_tensor(out=aA, in0=tA, scalar=1.0, in1=bank[:, 0, :],
                                         op0=ALU.add, op1=ALU.mult).then_inc(aA_ok, 1)
                dve.wait_ge(tanh_ok, n * 2 + 2)
                dve.scalar_tensor_tensor(out=aB[0:IB, :], in0=tB[0:IB, :], scalar=1.0, in1=bank[0:IB, 2, :],
                                         op0=ALU.add, op1=ALU.mult).then_inc(aB_ok, 1)
                dve.wait_ge(gu_full[1], n + 1)
                dve.wait_ge(aA_ok, n + 1)
                dve.wait_ge(hA_lo, n + 1)
                s = 0.5 * UNSCALE * UNSCALE * SX
                dve.scalar_tensor_tensor(out=h_f[:, 0, :], in0=bank[:, 1, :], scalar=s, in1=aA,
                                         op0=ALU.mult, op1=ALU.mult).then_inc(hf_ok, 1)
                dve.wait_ge(aB_ok, n + 1)
                dve.scalar_tensor_tensor(out=h_f[0:IB, 1, :], in0=bank[IB:P, 2, :], scalar=s, in1=aB[0:IB, :],
                                         op0=ALU.mult, op1=ALU.mult).then_inc(hf_ok, 1)

            def hidden_lo(n, k):
                dve.wait_ge(h_hi, n * 2 + 2)
                dve.tensor_tensor(hB[k][IB:P, :], h_f[0:IB, 1, :], hB[k][0:IB, :], ALU.subtract).then_inc(hB_lo, 1)

            def combine(e, tg, n):
                for s in range(SUB):
                    t = tg * SUB + s
                    dve.wait_ge(y_full, n * 4 + (s + 9))
                    dve.scalar_tensor_tensor(out=acc[:, t, :], in0=bank[:, 3 + s, :],
                                             scalar=route[:, t, bass.ds(e, 1)] if not isinstance(e, int)
                                             else route[:, t, e:e + 1],
                                             in1=acc[:, t, :], op0=ALU.mult, op1=ALU.add).then_inc(y_free, 1)

            def pair_dve(g, tail):
                for s in range(8):
                    if s < 7 or not tail:
                        hidden(g * 8 + (s + 1))
                    if s == 0:
                        split_lo(g * 2 + 1, 1)
                    if s == 4 and not tail:
                        split_lo(g * 2 + 2, 0)
                    combine(g * 2 + s // 4, s % 4, g * 8 + s)
                    if s < 7 or not tail:
                        hidden_lo(g * 8 + (s + 1), (s + 1) % 2)

            dve.wait_ge(acc_zero, 1)
            split_lo(0, 0)
            hidden(0)
            hidden_lo(0, 0)
            with dve.Fori(0, E // 2 - 1) as g:
                pair_dve(g, False)
            pair_dve(E // 2 - 1, True)

            dve.wait_ge(const_ld[2], 16)
            DB = 11 + Q_TILES
            with dve.Fori(0, NT // 2) as g:
                for s in range(2):
                    dve.wait_ge(ot_hi, g * 2 + (s + 1))
                    dve.scalar_tensor_tensor(out=oT[s][1], in0=bank4(s), scalar=SX, in1=oT[s][0],
                                             op0=ALU.mult, op1=ALU.subtract).then_inc(ot_lo, 1)
                for s in range(2):
                    a = acc[:, bass.ds(g * 2 + s, 1), :].rearrange("p t d -> p (t d)")
                    dve.wait_ge(th_ok, g * 2 + (s + 1))
                    dve.wait_ge(out_st[s], g * 16 + 16)
                    dve.scalar_tensor_tensor(out=ga[s], in0=th[s], scalar=1.0, in1=a, op0=ALU.add, op1=ALU.mult)\
                        .then_inc(dch, 1)
                    dve.wait_ge(s_out, g * 2 + (s + 3))
                    dve.scalar_tensor_tensor(out=fin[s], in0=bank[:, 2 + s, :], scalar=UNSCALE, in1=o_bias[:, :],
                                             op0=ALU.mult, op1=ALU.add).then_inc(dch, 1)
                    dve.wait_ge(dch, g * 6 + (DB + 3 * s + 2))
                    dve.scalar_tensor_tensor(out=ga[s], in0=ga[s], scalar=0.5, in1=fin[s], op0=ALU.mult,
                                             op1=ALU.mult).then_inc(dch, 1)
                    dve.wait_ge(dch, g * 6 + (DB + 3 * s + 3))
                    dve.wait_ge(xr_ld[s], g * 16 + 16)
                    dve.tensor_tensor(fin[s], ga[s], xr[s], ALU.add).then_inc(fin_ok, 1)

        @block.gpsimd
        def _(pool):
            pool.sem_inc(qkf_free, 4)
            pool.sem_inc(hA_lo, 1)
            pool.memset(ident[:, :], 0.0).then_inc(pch, 1)
            pool.wait_ge(pch, 1)
            pool.affine_select(out=ident[:, :], in_=ident[:, :], compare_op=ALU.not_equal, fill=1.0,
                               base=0, pattern=[[-1, P]], channel_multiplier=1).then_inc(ident_ok, 1)
            pool.memset(v_sb[:, :, :, HD:HD + 1], 1.0).then_inc(pch, 1)
            with pool.Fori(0, 8) as r:
                for s in range(TG):
                    pool.wait_ge(qk_hi, r * 4 + (s + 1))
                    pool.tensor_tensor(qk_p[1][s], qk_f[s], qk_p[0][s], ALU.subtract).then_inc(qkf_free, 1)

            pool.wait_ge(rstd_ok, 3)
            for s in range(TG):
                pool.wait_ge(qk_st[s], 8 * 2 * 16 + 16)
            pool.iota(rel, pattern=[[1, S]], base=P - S, channel_multiplier=-1,
                      allow_small_or_imprecise_dtypes=True).then_inc(alibi_ok, 1)
            pool.wait_ge(alibi_ok, 1)
            pool.wait_ge(const_ld[3], 16)

            no_key = pool.to_reg(-1.0e9 * SS)
            with pool.Fori(0, H // 2) as g:
                for hh in range(2):
                    pool.wait_ge(slope_rel, g * 2 + (hh + 1))
                    pool.sem_inc(slope_seen, 1)
                    pool.affine_select(out=alibi[hh], in_=alibi[hh], compare_op=ALU.is_ge, fill=no_key,
                                       base=S - P, pattern=[[-1, S]], channel_multiplier=1).then_inc(alibi_ok, 1)

            def hidden_lo(n, k):
                pool.wait_ge(h_hi, n * 2 + 1)
                pool.tensor_tensor(hA[k][1], h_f[:, 0, :], hA[k][0], ALU.subtract).then_inc(hA_lo, 1)

            pool.wait_ge(o_out, Q_TILES + 2)
            pool.memset(acc, 0.0).then_inc(acc_zero, 1)
            with pool.Fori(0, E * TG // 2) as g:
                for k in range(2):
                    hidden_lo(g * 2 + k, k)

            pool.wait_ge(y_free, 4 + E * NT)
            with pool.Fori(0, NT // 2) as g:
                for s in range(2):
                    pool.wait_ge(ot_full, g * 2 + 2)
                    pool.tensor_copy(ost[s], o_all[:, bass.ds(g * 2 + s, 1), :].rearrange("p t d -> p (t d)"))\
                        .then_inc(ost_ok, 1)


_INS = ['L0_attn_hidden_states', 'L0_attn_qkv_w', 'L0_attn_qkv_b', 'L0_attn_out_w', 'L0_attn_out_b',
        'L0_attn_alibi_slopes', 'L0_ffn_router_w', 'L0_ffn_w_gate', 'L0_ffn_w_up', 'L0_ffn_w_down']
_OUTS = [((2, 1024, 512), 'float32')]


def kernel(**inputs):
    import numpy as _np
    import concourse.bacc as _bacc
    from concourse import mybir as _mybir
    from concourse.bass_utils import run_bass_kernel_spmd as _run

    nc = _bacc.Bacc("TRN2", target_bir_lowering=False, num_devices=1)
    arrays, args = {}, []
    for name in _INS:
        a = _np.ascontiguousarray(inputs[name])
        arrays[f"in_{name}_dram"] = a
        args.append(nc.dram_tensor(f"in_{name}_dram", a.shape, _mybir.dt.from_np(a.dtype), kind="ExternalInput").ap())
    for i, (shape, dtype) in enumerate(_OUTS):
        dt = _mybir.dt.from_np(_np.dtype(dtype))
        args.append(nc.dram_tensor(f"out_{i}_dram", shape, dt, kind="ExternalOutput").ap())
    attention_times_moe_kernel(nc, *args)
    r = _run(nc, [arrays], core_ids=[0])
    got = tuple(r.results[0][f"out_{i}_dram"] for i in range(len(_OUTS)))
    return got[0]
```

```python
from contextlib import ExitStack

import concourse.bass as bass
from concourse import mybir

ALU = mybir.AluOpType
ACT = mybir.ActivationFunctionType
AX_X = mybir.AxisListType.X
F32 = mybir.dt.float32
F16 = mybir.dt.float16
I32 = mybir.dt.int32
U32 = mybir.dt.uint32

SX = 16.0
SW = 64.0
UNSCALE = 1.0 / (SX * SW)
SROUTE = 4096.0


def attention_times_moe_kernel(nc, x, qkv_w, qkv_b, out_w, out_b, slopes, router_w, w_gate, w_up, w_down, out):
    B, S, D = x.shape
    H = slopes.shape[0]
    HD = D // H
    E, _, I = w_gate.shape
    P = 128
    T = B * S
    NT = T // P
    C = D // P
    QT = S // P
    RQ = 3 * D // P
    RO = D // P
    NTOK = 512
    TG = T // NTOK
    SUB = NTOK // P
    IA, IB = P, I - P
    EPS = 1e-5
    SS = SX * SX
    SCRATCH = 12320
    K = 8
    NB = T * K // P + E
    assert NB % 4 == 0 and NB * 3 <= 512
    NW = C * 2 * 2 * I + 4 * D
    WD = C * 2 * 2 * I
    assert IB == 64 and TG == 4 and C == 4 and QT == 8 and B == 2

    x_t = x.rearrange("b (t p) d -> p (b t) d", p=P)
    out_t = out.rearrange("b (t p) d -> p (b t) d", p=P)
    qkvw_t = qkv_w.rearrange("(r p) d -> p r d", p=P)
    outw_t = out_w.rearrange("(r p) d -> p r d", p=P)
    qk_dram = nc.dram_tensor("qk_parts", [2, 2 * D, T], F16, kind="Internal").ap()

    o_dram = nc.dram_tensor("o_sums", [D, T], F32, kind="Internal").ap()
    den_dram = nc.dram_tensor("o_dens", [H, T], F32, kind="Internal").ap()
    rden_dram = nc.dram_tensor("o_rdens", [H, T], F32, kind="Internal").ap()

    x_tab = nc.dram_tensor("x_parts", [T, 2 * D], F16, kind="Internal").ap()
    w_tab = nc.dram_tensor("w_parts", [E, P, NW], F16, kind="Internal").ap()
    y_tab = nc.dram_tensor("y_slots", [NB * P, D], F32, kind="Internal").ap()

    with ExitStack() as ctx:
        def sb(name, shape, dt=F32):
            return ctx.enter_context(nc.sbuf_tensor(name, shape, dt))

        def sem(name):
            return ctx.enter_context(nc.semaphore(name))

        bank = ctx.enter_context(nc.psum_tensor("bank", [P, 8, 512], F32))

        ident = sb("ident", [P, P])
        wT = [sb(f"wT{i}", [P, C, RQ + RO, P], F16) for i in range(2)]
        rT = [sb(f"rT{i}", [P, C, E], F16) for i in range(2)]
        xT_all = sb("xT_all", [P, 2, C, NT, P], F16)
        xT = [xT_all[:, i, :, :, :] for i in range(2)]
        wbuf = xT_all[:, :, :, :, :].rearrange("p i c t q -> p (i c t q)")
        wraw = wbuf[:, 0:8192].bitcast(F32)
        wg_raw, wu_raw = (wraw[:, i * C * I:(i + 1) * C * I].rearrange("p (c i) -> p c i", c=C) for i in range(2))
        wda_raw, wdb_raw = (wraw[:, 2 * C * I + i * D:2 * C * I + (i + 1) * D] for i in range(2))
        w16 = wbuf[:, 8192:8192 + NW]
        w16_gu = w16[:, 0:WD].rearrange("p (c j q) -> p c j q", c=C, j=2)
        w16_d = w16[:, WD:NW].rearrange("p (a j d) -> p a j d", a=2, j=2)
        wslot = wbuf[:, 0:2 * NW].rearrange("p (s f) -> p s f", s=2)
        v_sb = sb("v_sb", [P, NT, H, HD + 1])
        v_flat = v_sb[:, :, :, :].rearrange("p t h d -> p (t h d)")
        yg = [v_flat[:, s * K * D:(s + 1) * K * D].rearrange("p (k d) -> p k d", k=K) for s in range(2)]
        o_all = sb("o_all", [P, NT, D])
        o_T = o_all[:, :, :].rearrange("p t d -> p (t d)").rearrange("p (c k) -> p c k", c=C)
        route = sb("route", [P, NT, E])
        qk_scale = sb("qk_scale", [P, 8])
        qk_bias = sb("qk_bias", [P, 8])
        v_bias = sb("v_bias", [P, D])
        o_bias = sb("o_bias", [P, D])
        slope1 = sb("slope1", [P, H])
        slope = sb("slope", [P, H])
        rwst = sb("rwst", [E, D])
        scratch = sb("scratch", [P, SCRATCH])
        mvs = sb("mvs", [P, NT, 2])
        stats = sb("stats", [P, NT, 6])
        rstd = sb("rstd", [P, NT])
        small = sb("small", [P, 4, NT])
        top8 = sb("top8", [P, NT, 8])
        mn = sb("mn", [P, QT])
        NR = H * T // P
        rden = sb("rden", [P, NR])
        ident16 = sb("ident16", [P, P], F16)
        identh = sb("identh", [P, P], F16)
        later = sb("later", [P, P], F16)
        q_off = sb("q_off", [P, QT, QT])
        k_bias4 = sb("k_bias4", [P, 4])
        k_bias = sb("k_bias", [P, H])
        rows_f = sb("rows_f", [P, QT, QT])
        rows16 = sb("rows16", [P, QT, QT, 3], F16)

        slot_idx = sb("slot_idx", [P, NT, K], I32)
        idx8 = [sb(f"idx8_{i}", [P, K], I32) for i in range(2)]
        tok_idx = sb("tok_idx", [P, NB], I32)
        idx1 = [sb(f"idx1_{i}", [P, 1], I32) for i in range(4)]
        slot_w = sb("slot_w", [P, NB])
        slot_wl = sb("slot_wl", [P, NB])
        expert_of = sb("expert_of", [1, NB], I32)
        slot_wait = sb("slot_wait", [1, E], I32)

        def carve(at, shape, dt=F32):
            n = 1
            for d in shape[1:]:
                n *= d
            words = n if dt == F32 else n // 2
            v = scratch[:, at:at + words]
            if dt != F32:
                v = v.bitcast(dt)
            if len(shape) == 3:
                v = v.rearrange("p (a b) -> p a b", a=shape[1])
            return v, at + words

        at = 0
        wst, xn, qk_f, qk_p = [], [], [], [[], []]
        for i in range(4):
            v, at = carve(at, [P, D]); wst.append(v)
        for i in range(2):
            v, at = carve(at, [P, D]); xn.append(v)
        for i in range(4):
            v, at = carve(at, [P, NTOK]); qk_f.append(v)
        for j in range(2):
            for i in range(4):
                v, at = carve(at, [P, NTOK], F16); qk_p[j].append(v)
        rl, at = carve(at, [P, NT, E])
        rr, at = carve(at, [P, NT, E])
        x16 = []
        for i in range(2):
            v, at = carve(at, [P, 2, D], F16); x16.append(v)
        below, at = carve(at, [P, E, E])
        iota3, at = carve(at, [P, 3, NB])
        thr, at = carve(at, [P, NT])
        tok_id, at = carve(at, [P, NT])
        zero16, at = carve(at, [P, 512], F16)
        tri16, at = carve(at, [P, P], F16)
        ones16, at = carve(at, [P, P], F16)
        assert at <= SCRATCH, at
        xfree = o_all[:, :, :].rearrange("p t d -> p (t d)")
        at = 0

        def carve_x(at, shape, dt=F32):
            n = 1
            for d in shape[1:]:
                n *= d
            words = n if dt != F16 else n // 2
            v = xfree[:, at:at + words]
            if dt != F32:
                v = v.bitcast(dt)
            if len(shape) == 3:
                v = v.rearrange("p (a b) -> p a b", a=shape[1])
            return v, at + words

        mask16, at = carve_x(at, [P, NT, E], F16)
        carry, at = carve_x(at, [P, NT + 1, E])
        val, at = carve_x(at, [P, NT, E])
        over, at = carve_x(at, [P, E, NT])
        nblk, at = carve_x(at, [P, E])
        first, at = carve_x(at, [P, E])
        base, at = carve_x(at, [P, E])
        s8f, at = carve_x(at, [P, NT, K])
        w8, at = carve_x(at, [P, NT, K])
        blk_i, at = carve_x(at, [P, NT * K], I32)
        low_i, at = carve_x(at, [P, NT * K], I32)
        blk_f, at = carve_x(at, [P, NT * K])
        low_f, at = carve_x(at, [P, NT * K])
        tab_f, at = carve_x(at, [P, NB])
        payload, at = carve_x(at, [P, NT * K, 3], F16)
        rhs, oh = [], []
        for i in range(2):
            v, at = carve_x(at, [P, 4, 3 * NB], F16); rhs.append(v)
            v, at = carve_x(at, [P, 4, P], F16); oh.append(v)
        assert at <= NT * D
        eq = v_flat[:, 0:NT * K * E].rearrange("p (t k e) -> p t k e", t=NT, k=K)
        cmp_e = v_flat[0:1, 0:NB * (E - 1)].rearrange("p (b e) -> p b e", b=NB)
        at = 0
        qs, ks, pr, alibi = [], [], [], []
        for i in range(2):
            v, at = carve(at, [P, S], F16); qs.append(v)
            v, at = carve(at, [P, S], F16); ks.append(v)
        tb, at = carve(at, [P, S])
        for i in range(2):
            v, at = carve(at, [P, S]); pr.append(v)
        for i in range(2):
            v, at = carve(at, [P, S]); alibi.append(v)
        rel, at = carve(at, [P, S])
        o_sb, v_cur = [], []
        for i in range(2):
            v, at = carve(at, [P, S]); o_sb.append(v)
        for i in range(2):
            v, at = carve(at, [P, QT, HD + 1]); v_cur.append(v)
        assert at <= SCRATCH, at
        at = 0
        xg, xb, ysb, h16, hT = [], [], [], [], []
        for i in range(4):
            v, at = carve(at, [P, 2 * D], F16); xg.append(v)
        for i in range(2):
            v, at = carve(at, [P, 2 * C, P], F16); xb.append(v)
            v, at = carve(at, [P, D]); ysb.append(v)
            v, at = carve(at, [P, 3, P], F16); h16.append(v)
            v, at = carve(at, [P, 3, P], F16); hT.append(v)
        tA, at = carve(at, [P, I])
        h_f, at = carve(at, [P, I])
        rb = []
        assert at <= SCRATCH - 2 * D, at
        at = SCRATCH - 2 * D
        for i in range(2):
            v, at = carve(at, [P, C, P]); rb.append(v)
        at = 0
        ya = []
        oT, on, xr, th, ga, fin = [], [], [], [], [], []
        for i in range(2):
            v, at = carve(at, [P, C, P], F16)
            w, at = carve(at, [P, C, P], F16); oT.append([v, w])
            v, at = carve(at, [P, C, P]); on.append(v)
            v, at = carve(at, [P, D]); ya.append(v)
            v, at = carve(at, [P, D]); xr.append(v)
            v, at = carve(at, [P, D]); th.append(v)
            v, at = carve(at, [P, D]); ga.append(v)
            v, at = carve(at, [P, D]); fin.append(v)

        const_ld = [sem(f"const_ld{i}") for i in range(6)]
        x_ld = [sem(f"x_ld{i}") for i in range(4)]
        wst_ld = [sem(f"wst_ld{i}") for i in range(4)]
        ident_ok = sem("ident_ok")
        tp_full = sem("tp_full")
        tp_hi = sem("tp_hi")
        tp_lo = sem("tp_lo")
        var_ok = sem("var_ok")
        std_ok = sem("std_ok")
        rstd_ok = sem("rstd_ok")
        bias_ok = sem("bias_ok")
        xn_ok = sem("xn_ok")
        proj_full = sem("proj_full")
        proj_free = sem("proj_free")
        qkf_free = sem("qkf_free")
        qk_hi = sem("qk_hi")
        qk_st = [sem(f"qk_st{i}") for i in range(4)]
        logits_ok = sem("logits_ok")
        ev_act = sem("ev_act")
        rch = sem("rch")
        consts_ok = sem("consts_ok")
        kb_ok = sem("kb_ok")
        dch = sem("dch")
        pch = sem("pch")
        kch = sem("kch")
        qk_in = [sem(f"qk_in{i}") for i in range(2)]
        slope_rel = sem("slope_rel")
        alibi_ok = sem("alibi_ok")
        s_full = sem("s_full")
        scores_seen = sem("scores_seen")
        slope_seen = sem("slope_seen")
        maxima_seen = sem("maxima_seen")
        s_free = sem("s_free")
        rows_ok = sem("rows_ok")
        rows_t = sem("rows_t")
        rows_in = sem("rows_in")
        st_full = sem("st_full")
        p_ok = sem("p_ok")
        pv_done = sem("pv_done")
        o_out = sem("o_out")
        v_ok = sem("v_ok")
        o_st = [sem(f"o_st{i}") for i in range(2)]
        ot_ld = sem("ot_ld")
        den_ld = sem("den_ld")
        rden_ok = sem("rden_ok")
        rden_st = sem("rden_st")
        wraw_ld = sem("wraw_ld")
        w16_hi = sem("w16_hi")
        w16_lo = sem("w16_lo")
        w_st = sem("w_st")
        x_hi = sem("x_hi")
        x_lo_ok = sem("x_lo_ok")
        x16_st = [sem(f"x16_st{i}") for i in range(2)]
        rt = sem("rt")
        mask_ok = sem("mask_ok")
        cnt_ok = sem("cnt_ok")
        go_list = sem("go_list")
        oh_ok = sem("oh_ok")
        rhs_ok = sem("rhs_ok")
        lst_used = sem("lst_used")
        v_free = sem("v_free")
        pq = sem("pq")
        w_ld = sem("w_ld")
        sp_seen = sem("sp_seen")
        ix_ok = sem("ix_ok")
        pl_seen = sem("pl_seen")
        xg_ld = [sem(f"xg_ld{i}") for i in range(4)]
        tp2 = sem("tp2")
        xb_ok = sem("xb_ok")
        gu_ok = sem("gu_ok")
        tanh_ok = sem("tanh_ok")
        a_ok = sem("a_ok")
        hf_ok = sem("hf_ok")
        h_hi = sem("h_hi")
        t2 = sem("t2")
        ht_ok = sem("ht_ok")
        h_lo = sem("h_lo")
        y_full = sem("y_full")
        y_ok = sem("y_ok")
        y_st = [sem(f"y_st{i}") for i in range(2)]
        rb_ld = [sem(f"rb_ld{i}") for i in range(2)]
        yg_ld = [sem(f"yg_ld{i}") for i in range(2)]
        ya_ok = sem("ya_ok")
        on_ok = sem("on_ok")
        ot_hi = sem("ot_hi")
        ot_lo = sem("ot_lo")
        s_out = sem("s_out")
        th_ok = sem("th_ok")
        fin_ok = sem("fin_ok")
        xr_ld = [sem(f"xr_ld{i}") for i in range(2)]
        out_st = [sem(f"out_st{i}") for i in range(2)]

        block = ctx.enter_context(nc.Block())

        NI_W = RQ + RO
        NI_R = NI_W + 1
        NI = NI_R + NT
        NPROJ = 8 * TG
        HEADS = B * H
        PAIR = [(hh, b) for hh in range(2) for b in range(B)]
        NL = len(PAIR)
        AUG = 3 * HD
        KR = AUG + 3 * QT

        @block.sync
        def _(sp):
            for s in range(TG):
                sp.sem_inc(qk_st[s], 16)
            for s in range(2):
                sp.sem_inc(out_st[s], 16)
                sp.sem_inc(o_st[s], 32)
                sp.sem_inc(x16_st[s], 16)
            sp.sem_inc(w_st, 16)
            for i in range(4):
                sp.dma_start(o_all[:, 4 * i:4 * i + 4, :], x_t[:, 4 * i:4 * i + 4, :]).then_inc(x_ld[i], 16)
            sp.dma_start(qk_bias[:, :], qkv_b[0:2 * D].rearrange("(r p) -> p r", p=P),
                         allow_slow_non_contiguous=True).then_inc(const_ld[0], 16)
            sp.dma_start(v_bias[:, :], qkv_b[2 * D:3 * D].partition_broadcast(P)).then_inc(const_ld[1], 16)
            sp.dma_start(o_bias[:, :], out_b.partition_broadcast(P)).then_inc(const_ld[2], 16)
            sp.dma_start(slope[:, :], slopes.partition_broadcast(P)).then_inc(const_ld[3], 16)
            sp.dma_start(rwst[:, :], router_w).then_inc(const_ld[4], 16)
            for s in range(4):
                sp.dma_start(wst[s], qkvw_t[:, s, :]).then_inc(wst_ld[s], 16)
            with sp.Fori(0, RQ // 4 - 1) as g:
                for s in range(4):
                    sp.wait_ge(tp_full, g * 4 + (s + 1))
                    sp.dma_start(wst[s], qkvw_t[:, bass.ds(g * 4 + (s + 4), 1), :].rearrange("p r d -> p (r d)"))\
                        .then_inc(wst_ld[s], 16)
            for s in range(RO):
                sp.wait_ge(tp_full, RQ + s - 3)
                sp.dma_start(wst[s], outw_t[:, s, :]).then_inc(wst_ld[s], 16)
            with sp.Fori(0, NT // 2) as g:
                for s in range(2):
                    sp.wait_ge(x_lo_ok, g * 2 + (s + 3))
                    sp.dma_start(x_tab[bass.ds((g * 2 + s) * P, P), :], x16[s].rearrange("p j d -> p (j d)"))\
                        .then_inc(x16_st[s], 16)
            for s in range(2):
                sp.wait_ge(x16_st[s], NT // 2 * 16 + 16)
            with sp.Fori(0, 8) as r:
                for s in range(TG):
                    sp.wait_ge(qkf_free, r * 4 + (s + 5))
                    for j in range(2):
                        sp.dma_start(qk_dram[j, bass.ds(r * P, P), s * NTOK:(s + 1) * NTOK],
                                     qk_p[j][s]).then_inc(qk_st[s], 16)
            for s in range(TG):
                sp.wait_ge(qk_st[s], 8 * 2 * 16 + 16)
            sp.wait_ge(alibi_ok, 1)

            def load_head(row, b):
                tok = slice(b * S, (b + 1) * S)
                for k, j in enumerate((0, 0, 1)):
                    sp.dma_start(qs[b][HD * k:HD * (k + 1), :],
                                 qk_dram[j, bass.ds(row, HD), tok]).then_inc(qk_in[b], 16)
                for k, j in enumerate((0, 1, 0)):
                    sp.dma_start(ks[b][HD * k:HD * (k + 1), :],
                                 qk_dram[j, bass.ds(row + D, HD), tok]).then_inc(qk_in[b], 16)

            def store_head(h, b):
                tok = slice(b * S, (b + 1) * S)
                sp.wait_ge(o_out, h * 2 + (b + 2))
                sp.dma_start(o_dram[bass.ds(h * HD, HD), tok], o_sb[b][0:HD, :]).then_inc(o_st[b], 16)
                sp.dma_start(den_dram[bass.ds(h, 1), tok], o_sb[b][HD:HD + 1, :]).then_inc(o_st[b], 16)

            def load_weights(e):
                sp.dma_start(wg_raw, w_gate[bass.ds(e, 1), :, :].rearrange("e (c p) i -> p (e c) i", p=P))\
                    .then_inc(wraw_ld, 16)
                sp.dma_start(wu_raw, w_up[bass.ds(e, 1), :, :].rearrange("e (c p) i -> p (e c) i", p=P))\
                    .then_inc(wraw_ld, 16)
                sp.dma_start(wda_raw, w_down[bass.ds(e, 1), 0:IA, :].rearrange("e p d -> p (e d)"))\
                    .then_inc(wraw_ld, 16)
                for k in range(2):
                    sp.dma_start(wdb_raw[IB * k:IB * (k + 1), :],
                                 w_down[bass.ds(e, 1), IA:I, :].rearrange("e p d -> p (e d)"))\
                        .then_inc(wraw_ld, 16)

            def store_weights(e):
                sp.wait_ge(w16_lo, e + 1)
                sp.dma_start(w_tab[bass.ds(e, 1), :, :].rearrange("e p f -> p (e f)"), w16).then_inc(w_st, 16)

            for b in range(B):
                load_head(0, b)
            sp.wait_ge(v_free, NT + 4)
            load_weights(0)
            with sp.Fori(0, H - 1) as h:
                for b in range(B):
                    sp.wait_ge(st_full, h * (B * QT) + (b + 1) * QT)
                    load_head(h * HD + HD, b)
                    store_weights(h * 2 + b)
                    load_weights(h * 2 + (b + 1))
                    store_head(h, b)
            for b in range(B):
                store_weights(E - 2 + b)
                if b == 0:
                    load_weights(E - 1)
                store_head(H - 1, b)
            for b in range(B):
                sp.wait_ge(o_st[b], 32 * H + 32)
            sp.dma_start(o_T, o_dram.rearrange("(c p) t -> p c t", p=P)).then_inc(ot_ld, 16)
            sp.dma_start(rden[:, :], den_dram.rearrange("h (a k) -> (h a) k", k=NR)).then_inc(den_ld, 16)
            sp.wait_ge(o_out, HEADS + 1)
            sp.wait_ge(w_st, E * 16 + 16)
            with sp.Fori(0, E // 2) as g:
                for s in range(2):
                    free_at = sp.value_load(slot_wait[0:1, bass.ds(g * 2 + s, 1)], min_val=1, max_val=NB + 2)
                    sp.wait_ge(y_full, free_at)
                    sp.sem_inc(sp_seen, 1)
                    sp.dma_start(wslot[:, s, :], w_tab[bass.ds(g * 2 + s, 1), :, :].rearrange("e p f -> p (e f)"))\
                        .then_inc(w_ld, 16)
                    sp.wait_ge(w_ld, g * 32 + (16 * s + 16))
                    sp.sem_inc(sp_seen, 1)
            sp.wait_ge(rden_ok, 1)
            sp.dma_start(rden_dram.rearrange("h (a k) -> (h a) k", k=NR), rden[:, :]).then_inc(rden_st, 16)
            sp.wait_ge(rden_st, 16)

            def load_rden(g):
                for s in range(2):
                    sp.wait_ge(on_ok, g * 2 + (s + 1))
                    for q in range(P // HD):
                        rows = rden_dram.rearrange("(c q) t -> q c t", c=C)[q:q + 1, :, bass.ds((g * 2 + s) * P, P)]\
                            .broadcast_to([HD, C, P])
                        sp.dma_start(rb[s][q * HD:(q + 1) * HD, :, :], rows).then_inc(rb_ld[s], 16)

            load_rden(0)
            sp.wait_ge(y_ok, NB + 2)

            def output_dma(g, tail):
                for s in range(2):
                    sp.wait_ge(fin_ok, g * 2 + 2)
                    sp.dma_start(xr[s], x_t[:, bass.ds(g * 2 + s, 1), :].rearrange("p t d -> p (t d)")).then_inc(xr_ld[s], 16)
                if not tail:
                    load_rden(g + 1)
                for s in range(2):
                    sp.wait_ge(fin_ok, g * 2 + (s + 3))
                    sp.dma_start(out_t[:, bass.ds(g * 2 + s, 1), :].rearrange("p t d -> p (t d)"), fin[s]).then_inc(out_st[s], 16)

            with sp.Fori(0, NT // 2 - 1) as g:
                output_dma(g, False)
            output_dma(NT // 2 - 1, True)
            for s in range(2):
                sp.wait_ge(out_st[s], NT // 2 * 16 + 16)

        @block.tensor
        def _(pe):
            pe.sem_inc(rows_t, 1)
            pe.sem_inc(pv_done, 2)
            for given in (y_full, tp2, gu_ok, lst_used, t2):
                pe.sem_inc(given, 2)
            pe.sem_inc(s_out, 2)
            pe.wait_ge(ident_ok, 1)

            def turn(src, rows, n_bank):
                view = bank[:, n_bank, :].rearrange("p (c q) -> p c q", c=C)
                for c in range(C):
                    last = pe.transpose(view[:, c, 0:rows], src[0:rows, c * P:(c + 1) * P], ident[0:rows, 0:rows])
                return last.then_inc(tp_full, 1)

            with pe.Fori(0, RQ // 4) as g:
                for s in range(4):
                    pe.wait_ge(wst_ld[s], g * 16 + 16)
                    pe.wait_ge(tp_lo, g * 4 + (s + 1))
                    turn(wst[s], P, s % 2)
            for s in range(RO):
                pe.wait_ge(wst_ld[s], (RQ // 4 + 1) * 16)
                pe.wait_ge(tp_lo, RQ + s + 1)
                turn(wst[s], P, s % 2)
            pe.wait_ge(const_ld[4], 16)
            pe.wait_ge(tp_lo, NI_W + 1)
            turn(rwst, E, 0)
            with pe.Fori(0, NT // 2) as g:
                for s in range(2):
                    pe.wait_ge(xn_ok, g * 2 + (s + 1))
                    pe.wait_ge(tp_lo, g * 2 + (NI_R + s + 1))
                    turn(xn[s], P, (1 + s) % 2)
            pe.wait_ge(tp_lo, NI + 2)

            def three(o, aT, b, first=True, last=True, **kw):
                for k, (i, j) in enumerate(((0, 0), (0, 1), (1, 0))):
                    ins = pe.matmul(o, aT(i), b(j), start=first and k == 0, stop=last and k == 2, **kw)
                return ins

            for t in range(NT):
                for c in range(C):
                    ins = three(bank[:, 4, t * E:(t + 1) * E], lambda i: xT[i][:, c, t, :],
                                lambda j: rT[j][:, c, :], c == 0, c == C - 1)
            ins.then_inc(logits_ok, 1)

            def qk_tile(r, s):
                pe.wait_ge(proj_free, r * 4 + (s + 1))
                for c in range(C):
                    ins = three(bank[:, s, :],
                                lambda i: wT[i][:, c, bass.ds(r, 1), :].rearrange("p r q -> p (r q)"),
                                lambda j: xT[j][:, c, SUB * s:SUB * (s + 1), :].rearrange("p t q -> p (t q)"),
                                c == 0, c == C - 1)
                ins.then_inc(proj_full, 1)

            def list_step(i, s):
                pe.wait_ge(oh_ok, i + 1)
                pe.wait_ge(rhs_ok, i + 1)
                for q in range(4):
                    ins = pe.matmul(bank[:, 7, 0:3 * NB], oh[s][:, q, :], rhs[s][:, q, :], start=False, stop=False)
                ins.then_inc(lst_used, 1)

            for s in range(TG):
                qk_tile(0, s)
            pe.wait_ge(pch, 4)
            pe.wait_ge(mask_ok, 1)
            m16 = mask16.rearrange("p t e -> p (t e)")
            pe.matmul(bank[:, 5, :], tri16, m16, start=True, stop=True)
            pe.matmul(bank[:, 6, :], ones16, m16, start=True, stop=True).then_inc(cnt_ok, 1)
            pe.matmul(bank[:, 7, :], zero16[:, 0:P], zero16, start=True, stop=False)
            with pe.Fori(0, 3) as r:
                for s in range(TG):
                    qk_tile(r + 1, s)
            with pe.Fori(0, 4) as r:
                for s in range(TG):
                    qk_tile(r + 4, s)
                    list_step(r * 4 + s, s % 2)
            pe.wait_ge(proj_free, NPROJ + 4)
            with pe.Fori(0, NT // 4) as g:
                for s in range(4):
                    pe.wait_ge(v_free, g * 4 + (s + 1))
                    for c in range(C):
                        ins = three(bank[:, s, :],
                                    lambda i: xT[i][:, c, bass.ds(g * 4 + s, 1), :].rearrange("p t q -> p (t q)"),
                                    lambda j: wT[j][:, c, 8:12, :].rearrange("p r q -> p (r q)"),
                                    c == 0, c == C - 1)
                    ins.then_inc(pq, 1)
                    list_step(g * 4 + (NT + s), s % 2)
            pe.matmul(bank[:, 7, :], zero16[:, 0:P], zero16, start=False, stop=True).then_inc(cnt_ok, 1)
            pe.wait_ge(v_free, NT + 4)

            def scores(n, b, k):
                i = QT - 1 - k
                if k == 0:
                    pe.wait_ge(qk_in[b], n[1] * 96 + 96)
                pe.wait_ge(s_free, n[0] * QT + (k + 1))
                if k == 0:
                    pe.wait_ge(rows_in, n[0] + 1)
                keys = (i + 1) * P
                for a in range(0, keys, 512):
                    w = min(512, keys - a)
                    ins = pe.matmul(bank[:, a // 512, 0:w], qs[b][0:AUG, i * P:(i + 1) * P],
                                    ks[b][0:AUG, a:a + w], start=True, stop=True)
                ins.then_inc(s_full, 1)

            def shift_rows(n):
                pe.wait_ge(rows_ok, n + 1)
                t = bank[:, 0, :].bitcast(F16)
                for i in range(QT):
                    ins = pe.transpose(t[0:3 * QT, i * P:(i + 1) * P],
                                       rows16[:, i, :, :].rearrange("p j r -> p (j r)"), identh[:, :])
                ins.then_inc(rows_t, 1)

            def scores_t(n, b, j):
                if j == 0:
                    pe.wait_ge(rows_in, n + 2)
                pe.wait_ge(p_ok, n * QT + (j + 1))
                queries = S - j * P
                for a in range(0, queries, 512):
                    w = min(512, queries - a)
                    ins = pe.matmul(bank[:, 2 + 2 * (j % 2) + a // 512, 0:w], ks[b][0:KR, j * P:(j + 1) * P],
                                    qs[b][0:KR, j * P + a:j * P + a + w], start=True, stop=a > 0)
                    if a == 0:
                        ins = pe.matmul(bank[:, 2 + 2 * (j % 2), 0:P], ident16[:, :], later[:, :],
                                        start=False, stop=True)
                ins.then_inc(st_full, 1)

            def values(n, l, j):
                pe.wait_ge(p_ok, n * QT + (j + 3))
                if j == 0:
                    pe.wait_ge(v_ok, n + 1)
                    pe.wait_ge(o_out, n + 1)
                for half in range(2):
                    a, z = max(j * P, half * 512), (half + 1) * 512
                    if a < z:
                        ins = pe.matmul(bank[0:HD + 1, 6 + half, a - half * 512:512], v_cur[l % 2][:, j, :],
                                        pr[j % 2][:, a - j * P:z - j * P], start=(j == 0),
                                        stop=(j == 4 * half + 3))
                ins.then_inc(pv_done, 1)

            def four_heads(g, tail):
                for l, (hh, b) in enumerate(PAIR):
                    n = g * NL + l
                    more = not (tail and l == NL - 1)
                    nb = PAIR[(l + 1) % NL][1]
                    nh = g * 2 + (hh + b)
                    for j in range(QT):
                        if more and j < QT // 2:
                            for k in (2 * j, 2 * j + 1):
                                scores((n + 1, nh), nb, k)
                        if more and j == 6:
                            shift_rows(n + 1)
                        scores_t(n, b, j)
                        if j:
                            values(n, l, j - 1)
                    values(n, l, QT - 1)

            pe.wait_ge(consts_ok, 1)
            for k in range(QT):
                scores((0, 0), 0, k)
            shift_rows(0)
            with pe.Fori(0, H // 2 - 1) as g:
                four_heads(g, False)
            four_heads(H // 2 - 1, True)
            pe.wait_ge(o_out, HEADS + 1)

            def turn_block(g4, q):
                s = q % 2
                pe.wait_ge(xg_ld[q], g4 * 16 + 16)
                pe.wait_ge(xb_ok, g4 * 4 + (q + 1))
                t = bank[:, s, :].bitcast(F16).rearrange("p (c q) -> p c q", c=2 * C)
                for c in range(2 * C):
                    ins = pe.transpose(t[:, c, :], xg[q][:, c * P:(c + 1) * P], identh[:, :])
                ins.then_inc(tp2, 1)

            def gate_up(b, s, e):
                pe.wait_ge(w_ld, e * 16 + 16)
                pe.wait_ge(xb_ok, b + 3)
                pe.wait_ge(hf_ok, b + 1)
                for c in range(C):
                    ins = three(bank[:, 2 + s, 0:2 * I], lambda i: xb[s][:, i * C + c, :],
                                lambda j: wslot[:, bass.ds(e % 2, 1), (c * 2 + j) * 2 * I:(c * 2 + j + 1) * 2 * I]
                                .rearrange("p s q -> p (s q)"), c == 0, c == C - 1)
                ins.then_inc(gu_ok, 1)

            def turn_hidden(b, s):
                pe.wait_ge(h_lo, b + 1)
                pe.wait_ge(ht_ok, b + 1)
                t = bank[:, 6 + s, :].bitcast(F16).rearrange("p (c q) -> p c q", q=P)
                for m in range(3):
                    ins = pe.transpose(t[:, m, :], h16[s][:, m, :], identh[:, :])
                ins.then_inc(t2, 1)

            def down(b, s, e):
                def wd(a, j, rows):
                    at_ = WD + (a * 2 + j) * D
                    return wslot[0:rows, bass.ds(e % 2, 1), at_:at_ + D].rearrange("p s d -> p (s d)")
                pe.wait_ge(ht_ok, b + 3)
                pe.wait_ge(y_ok, b + 1)
                y = bank[:, 4 + s, :]
                three(y, lambda i: hT[s][:, i, :], lambda j: wd(0, j, P), True, False)
                pe.matmul(y, hT[s][:, 2, :], wd(1, 0, P), start=False, stop=False)
                pe.matmul(y, hT[s][0:IB, 2, :], wd(1, 1, IB), start=False, stop=True).then_inc(y_full, 1)

            def expert(b):
                return pe.value_load(expert_of[0:1, bass.ds(b, 1)], min_val=0, max_val=E - 1)

            def four_blocks(g, tail):
                e = [expert(g * 4 + q) for q in range(2)]
                for q in range(4):
                    b = g * 4 + q
                    if q == 0:
                        turn_block(g, 3)
                    elif not tail:
                        turn_block(g + 1, q - 1)
                    if q < 2 or not tail:
                        e.append(expert(b + 2))
                        gate_up(b + 2, q % 2, e[q + 2])
                    if q < 3 or not tail:
                        turn_hidden(b + 1, (q + 1) % 2)
                    down(b, q % 2, e[q])

            turn_block(0, 0)
            turn_block(0, 1)
            gate_up(0, 0, expert(0))
            turn_block(0, 2)
            gate_up(1, 1, expert(1))
            turn_hidden(0, 0)
            with pe.Fori(0, NB // 4 - 1) as g:
                four_blocks(g, False)
            four_blocks(NB // 4 - 1, True)
            pe.wait_ge(y_ok, NB + 2)

            with pe.Fori(0, NT // 2) as g:
                for s in range(2):
                    pe.wait_ge(ot_lo, g * 2 + (s + 3))
                    pe.wait_ge(fin_ok, g * 2 + 2)
                    for c in range(C):
                        ins = three(bank[:, 2 + s, :], lambda i: oT[s][i][:, c, :],
                                    lambda j: wT[j][:, c, 12:16, :].rearrange("p r q -> p (r q)"),
                                    c == 0, c == C - 1)
                    ins.then_inc(s_out, 1)

        @block.scalar
        def _(act):
            act.sem_inc(rows_in, 1)
            act.sem_inc(p_ok, 2)
            act.sem_inc(xb_ok, 2)
            act.wait_ge(var_ok, 1)
            act.activation(small[:, 0, :], small[:, 1, :], ACT.Sqrt, scale=1.0 / (SX * SX)).then_inc(std_ok, 1)

            def bank4(n):
                return bank[:, n, :].rearrange("p (c q) -> p c q", c=C)

            with act.Fori(0, (RQ + RO) // 4) as g:
                for s in range(4):
                    act.wait_ge(tp_full, g * 4 + (s + 1))
                    act.activation(wT[0][:, :, bass.ds(g * 4 + s, 1), :].rearrange("p c r q -> p c (r q)"),
                                   bank4(s % 2), ACT.Copy, scale=SW).then_inc(tp_hi, 1)
            act.wait_ge(tp_full, NI_R)
            act.activation(rT[0][:, :, :], bank4(0)[:, :, 0:E], ACT.Copy, scale=SW).then_inc(tp_hi, 1)
            with act.Fori(0, NT // 2) as g:
                for s in range(2):
                    act.wait_ge(tp_full, g * 2 + (NI_R + s + 1))
                    act.activation(xT[0][:, :, bass.ds(g * 2 + s, 1), :].rearrange("p c t q -> p c (t q)"),
                                   bank4((1 + s) % 2), ACT.Copy).then_inc(tp_hi, 1)
                    act.wait_ge(x16_st[s], g * 16 + 16)
                    act.activation(x16[s][:, 0, :], xn[s], ACT.Copy).then_inc(x_hi, 1)
            act.wait_ge(rstd_ok, 2)
            act.activation(rl, rr, ACT.Exp).then_inc(ev_act, 1)
            with act.Fori(0, 8) as r:
                for s in range(TG):
                    act.wait_ge(proj_full, r * 4 + (s + 1))
                    act.sem_inc(maxima_seen, 1)
                    act.wait_ge(qkf_free, r * 4 + (s + 1))
                    act.sem_inc(maxima_seen, 1)
                    act.activation(qk_f[s], bank[:, s, :], ACT.Identity, scale=qk_scale[:, bass.ds(r, 1)],
                                   bias=qk_bias[:, bass.ds(r, 1)]).then_inc(proj_free, 1)
                    act.wait_ge(proj_free, r * 4 + (s + 5))
                    act.wait_ge(qk_st[s], r * 32 + 16)
                    act.activation(qk_p[0][s], qk_f[s], ACT.Copy).then_inc(qk_hi, 1)

            def head_bias(h, hh):
                act.activation(alibi[hh], rel, ACT.Copy, scale=slope[:, bass.ds(h, 1)]).then_inc(slope_rel, 1)

            def rows_under_q(n, b):
                act.wait_ge(rows_t, n + 2)
                act.activation(qs[b][AUG:KR, :], bank[0:3 * QT, 0, :].bitcast(F16), ACT.Copy).then_inc(rows_in, 1)

            def lay_values(h, l):
                b = PAIR[l][1]
                act.activation(v_cur[l % 2], v_sb[:, b * QT:(b + 1) * QT, bass.ds(h, 1), :]
                               .rearrange("p j h d -> p j (h d)"), ACT.Copy).then_inc(v_ok, 1)

            def split_hi(e):
                act.wait_ge(wraw_ld, e * 80 + 80)
                act.sem_inc(maxima_seen, 1)
                act.wait_ge(w_st, e * 16 + 16)
                act.sem_inc(maxima_seen, 1)
                act.activation(w16_gu[:, :, 0, 0:I], wg_raw, ACT.Copy, scale=SW)
                act.activation(w16_gu[:, :, 0, I:2 * I], wu_raw, ACT.Copy, scale=SW)
                act.activation(w16_d[:, 0, 0, :], wda_raw, ACT.Copy, scale=SW)
                act.activation(w16_d[:, 1, 0, :], wdb_raw, ACT.Copy, scale=SW).then_inc(w16_hi, 1)

            def softmax(n, l, j):
                act.wait_ge(st_full, n * QT + (j + 1))
                act.wait_ge(pv_done, n * QT + (j + 1))
                act.activation(pr[j % 2][:, 0:S - j * P],
                               bank[:, 2 + 2 * (j % 2):4 + 2 * (j % 2), :].rearrange("p a k -> p (a k)")[:, 0:S - j * P],
                               ACT.Exp, scale=1.0 / SS, bias=k_bias4[:, l:l + 1]).then_inc(p_ok, 1)

            def four_heads(g, tail):
                for l, (hh, b) in enumerate(PAIR):
                    n = g * NL + l
                    if b == 1 and not tail:
                        act.wait_ge(s_free, n * QT + (QT + 1))
                        act.sem_inc(maxima_seen, 1)
                        head_bias(g * 2 + (hh + 2), hh)
                    for j in range(QT):
                        if j == 6 and not (tail and l == NL - 1):
                            rows_under_q(n + 1, PAIR[(l + 1) % NL][1])
                        softmax(n, l, j)
                        if j == 4:
                            split_hi(n)
                        if j == 3 and not (tail and l == NL - 1):
                            lay_values(g * 2 + (hh + b), (l + 1) % NL)

            act.wait_ge(kb_ok, 2)
            act.wait_ge(alibi_ok, 1)
            for hh in range(2):
                head_bias(hh, hh)
            act.wait_ge(v_free, NT + 4)
            lay_values(0, 0)
            rows_under_q(0, 0)
            with act.Fori(0, H // 2 - 1) as g:
                four_heads(g, False)
            four_heads(H // 2 - 1, True)

            def take_block(b, s):
                act.wait_ge(tp2, b + 3)
                act.wait_ge(gu_ok, b + 1)
                act.activation(xb[s].rearrange("p c q -> p (c q)"), bank[:, s, :].bitcast(F16), ACT.Copy).then_inc(xb_ok, 1)

            def tanh_gate(b, s):
                act.wait_ge(gu_ok, b + 3)
                act.wait_ge(hf_ok, b + 2)
                act.activation(tA, bank[:, 2 + s, 0:I], ACT.Tanh, scale=0.5 * UNSCALE).then_inc(tanh_ok, 1)

            def hidden_hi(b, s):
                act.wait_ge(hf_ok, b + 3)
                act.wait_ge(t2, b + 1)
                act.activation(h16[s][:, 0, :], h_f[:, 0:IA], ACT.Copy)
                act.activation(h16[s][:, 2, 0:IB], h_f[:, IA:I], ACT.Copy).then_inc(h_hi, 1)

            def step(b, s, blocks, hiddens):
                if blocks:
                    take_block(b + 3, 1 - s)
                if hiddens:
                    tanh_gate(b + 2, s)
                    hidden_hi(b + 2, s)

            act.wait_ge(o_out, HEADS + 1)
            take_block(0, 0)
            take_block(1, 1)
            tanh_gate(0, 0)
            hidden_hi(0, 0)
            take_block(2, 0)
            tanh_gate(1, 1)
            hidden_hi(1, 1)
            with act.Fori(0, NB // 2 - 2) as g:
                for s in range(2):
                    step(g * 2 + s, s, True, True)
            for b in range(NB - 4, NB):
                step(b, b % 2, b + 3 < NB, b + 2 < NB)

            with act.Fori(0, NT // 2) as g:
                for s in range(2):
                    act.wait_ge(on_ok, g * 2 + (s + 3))
                    act.wait_ge(s_out, g * 2 + 2)
                    act.activation(oT[s][0], on[s], ACT.Copy, scale=SX).then_inc(ot_hi, 1)
                for s in range(2):
                    act.wait_ge(fin_ok, g * 2 + 2)
                    act.wait_ge(ya_ok, g * 2 + (s + 3))
                    act.activation(th[s], ya[s], ACT.Tanh, scale=0.5).then_inc(th_ok, 1)

        @block.vector
        def _(dve):
            dve.sem_inc(tp_lo, 2)
            dve.sem_inc(proj_free, 4)
            dve.sem_inc(s_free, 1)
            dve.sem_inc(o_out, 1)
            dve.sem_inc(v_free, 4)
            dve.sem_inc(y_ok, 2)
            dve.sem_inc(on_ok, 2)
            dve.sem_inc(ht_ok, 2)
            dve.sem_inc(ya_ok, 2)
            dve.sem_inc(hf_ok, 2)
            dve.sem_inc(ot_lo, 2)
            dve.sem_inc(fin_ok, 2)

            def bank4(n):
                return bank[:, n, :].rearrange("p (c q) -> p c q", c=C)

            for i in range(4):
                dve.wait_ge(x_ld[i], 16)
                for t in range(4 * i, 4 * i + 4):
                    ins = dve.bn_stats(stats[:, t, :], o_all[:, t, :])
            ins.then_inc(dch, 1)
            dve.wait_ge(dch, 1)
            for t in range(NT):
                ins = dve.bn_aggr(mvs[:, t, :], stats[:, t, :])
            ins.then_inc(dch, 1)
            dve.wait_ge(dch, 2)
            dve.tensor_scalar(small[:, 1, :], mvs[:, :, 1], EPS, None, ALU.add).then_inc(var_ok, 1)
            dve.wait_ge(std_ok, 1)
            dve.reciprocal(rstd[:, :], small[:, 0, :]).then_inc(dch, 1)
            dve.wait_ge(dch, 3)
            dve.wait_ge(const_ld[3], 16)
            dve.tensor_copy(slope1[:, :], slope[:, :])
            dve.tensor_scalar(slope[:, :], slope[:, :], SS, None, ALU.mult).then_inc(rstd_ok, 1)
            dve.wait_ge(kb_ok, 1)
            dve.wait_ge(rstd_ok, 1)
            dve.tensor_tensor(k_bias[:, :], k_bias[:, :], slope1[:, :], ALU.mult).then_inc(kb_ok, 1)
            dve.memset(qk_scale[:, 0:4], UNSCALE * SX * HD ** -0.5)
            dve.memset(qk_scale[:, 4:8], UNSCALE * SX)
            dve.wait_ge(const_ld[0], 16)
            dve.tensor_scalar(qk_bias[:, 0:4], qk_bias[:, 0:4], SX * HD ** -0.5, None, ALU.mult)
            dve.tensor_scalar(qk_bias[:, 4:8], qk_bias[:, 4:8], SX, None, ALU.mult).then_inc(dch, 1)
            dve.wait_ge(dch, 4)

            with dve.Fori(0, (RQ + RO) // 4) as g:
                for s in range(4):
                    hi, lo = (wT[i][:, :, bass.ds(g * 4 + s, 1), :].rearrange("p c r q -> p c (r q)") for i in range(2))
                    dve.wait_ge(tp_hi, g * 4 + (s + 1))
                    dve.scalar_tensor_tensor(out=lo, in0=bank4(s % 2), scalar=SW, in1=hi,
                                             op0=ALU.mult, op1=ALU.subtract).then_inc(tp_lo, 1)
            dve.wait_ge(tp_hi, NI_R)
            dve.scalar_tensor_tensor(out=rT[1][:, :, :], in0=bank4(0)[:, :, 0:E], scalar=SW, in1=rT[0][:, :, :],
                                     op0=ALU.mult, op1=ALU.subtract).then_inc(tp_lo, 1)

            def normalise(t, s):
                dve.wait_ge(tp_full, t + (NI_R - 1))
                dve.wait_ge(x_lo_ok, t + 1)
                dve.tensor_scalar(xn[s], o_all[:, bass.ds(t, 1), :].rearrange("p t d -> p (t d)"),
                                  mvs[:, bass.ds(t, 1), 0:1].rearrange("p t d -> p (t d)"), rstd[:, bass.ds(t, 1)],
                                  ALU.subtract, ALU.mult).then_inc(xn_ok, 1)

            def x_lo(t, s):
                hi, lo = (xT[i][:, :, bass.ds(t, 1), :].rearrange("p c t q -> p c (t q)") for i in range(2))
                dve.wait_ge(tp_hi, t + (NI_R + 1))
                dve.scalar_tensor_tensor(out=lo, in0=bank4((1 + s) % 2), scalar=1.0, in1=hi,
                                         op0=ALU.mult, op1=ALU.subtract).then_inc(tp_lo, 1)

            normalise(0, 0)
            with dve.Fori(0, NT // 2 - 1) as g:
                for s in range(2):
                    normalise(g * 2 + (s + 1), (s + 1) % 2)
                    x_lo(g * 2 + s, s)
            normalise(NT - 1, 1)
            x_lo(NT - 2, 0)
            x_lo(NT - 1, 1)
            dve.wait_ge(logits_ok, 1)
            lg = bank[:, 4, :].rearrange("p (t e) -> p t e", e=E)
            dve.tensor_scalar(rl, lg, UNSCALE, None, ALU.mult).then_inc(rt, 1)
            dve.wait_ge(rt, 1)
            dve.tensor_reduce(small[:, 2, :], rl, AX_X, ALU.max).then_inc(rt, 1)
            dve.wait_ge(rt, 2)
            dve.tensor_tensor(rr, rl, small[:, 2, :].unsqueeze(2).broadcast_to([P, NT, E]), ALU.subtract)\
                .then_inc(rstd_ok, 1)
            dve.wait_ge(ev_act, 1)
            for t in range(NT):
                ins = dve.max(top8[:, t, :], rl[:, t, :])
            ins.then_inc(rt, 1)
            dve.wait_ge(rt, 3)
            for t in range(NT):
                ins = dve.match_replace(rr[:, t, :], top8[:, t, :], rl[:, t, :], -1.0)
            ins.then_inc(rt, 1)
            dve.tensor_reduce(small[:, 3, :], top8[:, :, :], AX_X, ALU.add).then_inc(rt, 1)
            dve.wait_ge(rt, 5)
            dve.tensor_scalar(mask16, rr, 0.0, None, ALU.is_lt).then_inc(mask_ok, 1)
            dve.reciprocal(small[:, 2, :], small[:, 3, :]).then_inc(rt, 1)
            dve.memset(carry[:, 0, :], 0.0).then_inc(rt, 1)
            dve.wait_ge(mask_ok, 1)
            dve.tensor_tensor(rr, rl, mask16, ALU.mult).then_inc(rt, 1)
            dve.wait_ge(rt, 8)
            dve.tensor_tensor(route[:, :, :], rr, small[:, 2, :].unsqueeze(2).broadcast_to([P, NT, E]), ALU.mult)\
                .then_inc(rt, 1)
            dve.wait_ge(cnt_ok, 1)
            for t in range(NT):
                dve.wait_ge(rt, 9 + t)
                dve.tensor_tensor(carry[:, t + 1, :], carry[:, t, :], bank[:, 6, t * E:(t + 1) * E], ALU.add)\
                    .then_inc(rt, 1)
            R = 9 + NT
            dve.wait_ge(rt, R)
            dve.tensor_tensor(over, carry[:, NT, :].unsqueeze(2).broadcast_to([P, E, NT]),
                              thr.unsqueeze(1).broadcast_to([P, E, NT]), ALU.is_gt).then_inc(rt, 1)
            dve.wait_ge(rt, R + 1)
            dve.tensor_reduce(nblk, over, AX_X, ALU.add).then_inc(rt, 1)
            dve.wait_ge(rt, R + 2)
            dve.tensor_scalar(nblk, nblk, 1.0, None, ALU.max).then_inc(rt, 1)
            dve.wait_ge(rt, R + 3)
            dve.wait_ge(pch, 4)
            dve.tensor_tensor(below, below, nblk.unsqueeze(1).broadcast_to([P, E, E]), ALU.mult).then_inc(rt, 1)
            dve.wait_ge(rt, R + 4)
            dve.tensor_reduce(first, below, AX_X, ALU.add).then_inc(rt, 1)
            dve.tensor_tensor(val, carry[:, 0:NT, :], bank[:, 5, :].rearrange("p (t e) -> p t e", e=E), ALU.add)\
                .then_inc(rt, 1)
            dve.wait_ge(rt, R + 6)
            dve.tensor_scalar(base, first, float(P), 1.0, ALU.mult, ALU.add).then_inc(rt, 1)
            dve.wait_ge(rt, R + 7)
            dve.tensor_tensor(val, val, base.unsqueeze(1).broadcast_to([P, NT, E]), ALU.add).then_inc(rt, 1)
            dve.wait_ge(rt, R + 8)
            dve.tensor_tensor(val, val, mask16, ALU.mult).then_inc(rt, 1)
            dve.wait_ge(rt, R + 9)
            for t in range(NT):
                ins = dve.max(s8f[:, t, :], val[:, t, :])
            ins.then_inc(rt, 1)
            dve.wait_ge(rt, R + 10)
            dve.tensor_tensor(eq, val.unsqueeze(2).broadcast_to([P, NT, K, E]),
                              s8f.unsqueeze(3).broadcast_to([P, NT, K, E]), ALU.is_equal).then_inc(rt, 1)
            dve.wait_ge(rt, R + 11)
            dve.tensor_tensor(eq, eq, route[:, :, :].unsqueeze(2).broadcast_to([P, NT, K, E]), ALU.mult)\
                .then_inc(rt, 1)
            dve.tensor_scalar(slot_idx[:, :, :], s8f, -1.0, None, ALU.add).then_inc(rt, 1)
            dve.wait_ge(rt, R + 13)
            dve.tensor_reduce(w8, eq, AX_X, ALU.add).then_inc(rt, 1)
            si = slot_idx[:, :, :].rearrange("p t k -> p (t k)")
            dve.tensor_scalar(blk_i, si, 7, None, ALU.arith_shift_right).then_inc(rt, 1)
            dve.tensor_scalar(low_i, si, P - 1, None, ALU.bitwise_and).then_inc(rt, 1)
            dve.wait_ge(rt, R + 16)
            dve.tensor_copy(low_f, low_i)
            dve.tensor_copy(blk_f, blk_i).then_inc(rt, 1)
            pay = payload.rearrange("p (t k) j -> p t k j", t=NT)
            dve.tensor_copy(pay[:, :, :, 0], tok_id.unsqueeze(2).broadcast_to([P, NT, K])).then_inc(rt, 1)
            dve.tensor_scalar(pay[:, :, :, 1], w8, SROUTE, None, ALU.mult).then_inc(rt, 1)
            dve.wait_ge(rt, R + 19)
            dve.scalar_tensor_tensor(out=pay[:, :, :, 2], in0=w8, scalar=SROUTE, in1=pay[:, :, :, 1],
                                     op0=ALU.mult, op1=ALU.subtract).then_inc(rt, 1)
            dve.tensor_tensor(cmp_e, first[0:1, 1:E].unsqueeze(1).broadcast_to([1, NB, E - 1]),
                              iota3[0:1, 0, :].unsqueeze(2).broadcast_to([1, NB, E - 1]), ALU.is_le).then_inc(rt, 1)
            dve.wait_ge(rt, R + 21)
            dve.tensor_reduce(tab_f[0:1, :], cmp_e, AX_X, ALU.add).then_inc(rt, 1)
            dve.tensor_scalar(slot_wait[0:1, 0:1], first[0:1, 0:1], 1.0, None, ALU.add)
            dve.tensor_scalar(slot_wait[0:1, 1:E], first[0:1, 0:E - 1], 2.0, None, ALU.add).then_inc(rt, 1)
            dve.wait_ge(rt, R + 23)
            dve.tensor_copy(expert_of[0:1, :], tab_f[0:1, :]).then_inc(rt, 1)
            dve.wait_ge(rt, R + 24)
            dve.sem_inc(go_list, 1)

            def list_step(i, s):
                dve.wait_ge(lst_used, i + 1)
                dve.tensor_tensor(oh[s], iota3[:, 0, 0:P].unsqueeze(1).broadcast_to([P, 4, P]),
                                  low_f[:, bass.ds(i * 4, 4)].unsqueeze(2).broadcast_to([P, 4, P]), ALU.is_equal)\
                    .then_inc(oh_ok, 1)
                for q in range(4):
                    ins = dve.scalar_tensor_tensor(
                        out=rhs[s][:, q, :].rearrange("p (j b) -> p j b", j=3), in0=iota3,
                        scalar=blk_f[:, bass.ds(i * 4 + q, 1)],
                        in1=payload[:, bass.ds(i * 4 + q, 1), :].rearrange("p a j -> p (a j)").unsqueeze(2)
                        .broadcast_to([P, 3, NB]), op0=ALU.is_equal, op1=ALU.mult)
                ins.then_inc(rhs_ok, 1)

            with dve.Fori(0, NT // 2) as g:
                for s in range(2):
                    list_step(g * 2 + s, s)
            dve.wait_ge(const_ld[1], 16)
            with dve.Fori(0, NT // 4) as g:
                for s in range(4):
                    list_step(g * 4 + (NT + s), s % 2)
                    dve.wait_ge(pq, g * 4 + (s + 1))
                    dve.scalar_tensor_tensor(
                        out=v_sb[:, bass.ds(g * 4 + s, 1), :, 0:HD].rearrange("p t h d -> p (t h) d"),
                        in0=bank[:, s, :].rearrange("p (h d) -> p h d", h=H), scalar=UNSCALE,
                        in1=v_bias[:, :].rearrange("p (h d) -> p h d", h=H),
                        op0=ALU.mult, op1=ALU.add).then_inc(v_free, 1)
            dve.wait_ge(cnt_ok, 2)
            dve.tensor_copy(tok_idx[:, :], bank[:, 7, 0:NB])
            dve.tensor_scalar(slot_wl[:, :], bank[:, 7, 2 * NB:3 * NB], UNSCALE / SROUTE, None, ALU.mult)\
                .then_inc(rt, 1)
            dve.wait_ge(rt, R + 25)
            dve.scalar_tensor_tensor(out=slot_w[:, :], in0=bank[:, 7, NB:2 * NB], scalar=UNSCALE / SROUTE,
                                     in1=slot_wl[:, :], op0=ALU.mult, op1=ALU.add).then_inc(rstd_ok, 1)

            def row_max(n, k, hh):
                i = QT - 1 - k
                keys = (i + 1) * P
                if k == 0:
                    dve.wait_ge(alibi_ok, n[1] + 2)
                dve.wait_ge(s_full, n[0] * QT + (k + 1))
                dve.sem_inc(scores_seen, 1)
                dve.tensor_tensor_reduce(tb[:, 0:keys], bank[:, 0:2, :].rearrange("p a k -> p (a k)")[:, 0:keys],
                                         alibi[hh][:, S - keys:S], -1.0 / SS, 3.0e38, ALU.add, ALU.min,
                                         mn[:, i:i + 1]).then_inc(s_free, 1)

            def make_rows(n, h, l):
                dve.wait_ge(s_free, n * QT + (QT + 1))
                dve.wait_ge(rows_t, n + 1)
                dve.tensor_scalar(k_bias4[:, l:l + 1], k_bias[:, bass.ds(h, 1)], 1.0, None, ALU.mult)
                dve.scalar_tensor_tensor(out=rows_f[:, :, :], in0=q_off[:, :, :], scalar=slope1[:, bass.ds(h, 1)],
                                         in1=mn[:, :].unsqueeze(2).broadcast_to([P, QT, QT]),
                                         op0=ALU.mult, op1=ALU.add).then_inc(rch, 1)
                dve.wait_ge(rch, n * 4 + 1)
                dve.tensor_copy(rows16[:, :, :, 0], rows_f[:, :, :]).then_inc(rch, 1)
                dve.wait_ge(rch, n * 4 + 2)
                dve.tensor_tensor(rows_f[:, :, :], rows_f[:, :, :], rows16[:, :, :, 0], ALU.subtract).then_inc(rch, 1)
                dve.wait_ge(rch, n * 4 + 3)
                dve.tensor_copy(rows16[:, :, :, 1], rows_f[:, :, :]).then_inc(rch, 1)
                dve.wait_ge(rch, n * 4 + 4)
                dve.tensor_tensor(rows16[:, :, :, 2], rows_f[:, :, :], rows16[:, :, :, 1], ALU.subtract)\
                    .then_inc(rows_ok, 1)

            def split_lo(e):
                dve.wait_ge(w16_hi, e + 1)
                hi, lo = w16_gu[:, :, 0, :], w16_gu[:, :, 1, :]
                for a, raw in ((0, wg_raw), (I, wu_raw)):
                    dve.scalar_tensor_tensor(out=lo[:, :, a:a + I], in0=raw, scalar=SW, in1=hi[:, :, a:a + I],
                                             op0=ALU.mult, op1=ALU.subtract)
                for a, raw in ((0, wda_raw), (1, wdb_raw)):
                    ins = dve.scalar_tensor_tensor(out=w16_d[:, a, 1, :], in0=raw, scalar=SW, in1=w16_d[:, a, 0, :],
                                                   op0=ALU.mult, op1=ALU.subtract)
                ins.then_inc(w16_lo, 1)

            def take_output(n, h, b):
                dve.wait_ge(pv_done, n * QT + (QT + 2))
                dve.wait_ge(o_st[b], h * 32 + 32)
                dve.tensor_copy(o_sb[b][0:HD + 1, :], bank[0:HD + 1, 6:8, :].rearrange("p a k -> p (a k)"))\
                    .then_inc(o_out, 1)

            def four_heads(g, tail):
                for l, (hh, b) in enumerate(PAIR):
                    n = g * NL + l
                    if not (tail and l == NL - 1):
                        nh = g * 2 + (hh + b)
                        for k in range(QT):
                            row_max((n + 1, nh), k, PAIR[(l + 1) % NL][0])
                        make_rows(n + 1, nh, (l + 1) % NL)
                    split_lo(n)
                    take_output(n, g * 2 + hh, b)

            dve.wait_ge(kb_ok, 2)
            for k in range(QT):
                row_max((0, 0), k, 0)
            make_rows(0, 0, 0)
            with dve.Fori(0, H // 2 - 1) as g:
                four_heads(g, False)
            four_heads(H // 2 - 1, True)

            def hidden(b, s):
                dve.wait_ge(tanh_ok, b + 1)
                dve.scalar_tensor_tensor(out=tA, in0=tA, scalar=1.0, in1=bank[:, 2 + s, 0:I],
                                         op0=ALU.add, op1=ALU.mult).then_inc(a_ok, 1)
                dve.wait_ge(a_ok, b + 1)
                dve.scalar_tensor_tensor(out=h_f, in0=bank[:, 2 + s, I:2 * I], scalar=0.5 * UNSCALE * UNSCALE * SX,
                                         in1=tA, op0=ALU.mult, op1=ALU.mult).then_inc(hf_ok, 1)

            def hidden_lo(b, s):
                dve.wait_ge(h_hi, b + 1)
                dve.tensor_tensor(h16[s][:, 1, :], h_f[:, 0:IA], h16[s][:, 0, :], ALU.subtract)
                dve.tensor_tensor(h16[s][:, 2, IB:P], h_f[:, IA:I], h16[s][:, 2, 0:IB], ALU.subtract).then_inc(h_lo, 1)

            def take_hidden(b, s):
                dve.wait_ge(t2, b + 3)
                dve.wait_ge(y_full, b + 1)
                dve.tensor_copy(hT[s].rearrange("p m q -> p (m q)"), bank[:, 6 + s, :].bitcast(F16)[:, 0:3 * P])\
                    .then_inc(ht_ok, 1)

            def weigh(g2, s, first_pair):
                dve.wait_ge(y_full, g2 * 2 + (s + 3))
                if not first_pair:
                    dve.wait_ge(y_st[s], g2 * 16)
                dve.tensor_scalar(ysb[s], bank[:, 4 + s, :], slot_w[:, bass.ds(g2 * 2 + s, 1)], None, ALU.mult)\
                    .then_inc(y_ok, 1)

            def block_pair(g, tail=False, first_pair=False):
                for s in range(2):
                    if not tail:
                        hidden(g * 2 + (s + 2), s)
                    if not (tail and s == 1):
                        take_hidden(g * 2 + (s + 1), 1 - s)
                    if not tail:
                        hidden_lo(g * 2 + (s + 2), s)
                    weigh(g, s, first_pair)

            dve.wait_ge(den_ld, 16)
            dve.reciprocal(rden[:, :], rden[:, :]).then_inc(rden_ok, 1)
            hidden(0, 0)
            hidden_lo(0, 0)
            hidden(1, 1)
            hidden_lo(1, 1)
            take_hidden(0, 0)
            block_pair(0, first_pair=True)
            with dve.Fori(0, NB // 2 - 2) as g:
                block_pair(g + 1)
            block_pair(NB // 2 - 1, tail=True)

            dve.wait_ge(const_ld[2], 16)
            dve.wait_ge(ot_ld, 16)
            dve.wait_ge(y_ok, NB + 2)
            for s in range(2):
                dve.wait_ge(y_st[s], NB // 2 * 16)
            DB = 4
            with dve.Fori(0, NT // 2) as g:
                for s in range(2):
                    dve.wait_ge(rb_ld[s], g * 64 + 64)
                    dve.tensor_tensor(on[s], o_T[:, :, bass.ds((g * 2 + s) * P, P)], rb[s], ALU.mult)\
                        .then_inc(on_ok, 1)
                for s in range(2):
                    dve.wait_ge(ot_hi, g * 2 + (s + 1))
                    dve.scalar_tensor_tensor(out=oT[s][1], in0=on[s], scalar=SX, in1=oT[s][0],
                                             op0=ALU.mult, op1=ALU.subtract).then_inc(ot_lo, 1)
                for s in range(2):
                    dve.wait_ge(yg_ld[s], g * 128 + 128)
                    dve.tensor_reduce(ya[s], yg[s].rearrange("p k d -> p d k"), AX_X, ALU.add).then_inc(ya_ok, 1)
                    dve.wait_ge(th_ok, g * 2 + (s + 1))
                    dve.wait_ge(out_st[s], g * 16 + 16)
                    dve.scalar_tensor_tensor(out=ga[s], in0=th[s], scalar=1.0, in1=ya[s], op0=ALU.add, op1=ALU.mult)\
                        .then_inc(dch, 1)
                    dve.wait_ge(s_out, g * 2 + (s + 3))
                    dve.scalar_tensor_tensor(out=fin[s], in0=bank[:, 2 + s, :], scalar=UNSCALE, in1=o_bias[:, :],
                                             op0=ALU.mult, op1=ALU.add).then_inc(dch, 1)
                    dve.wait_ge(dch, g * 6 + (DB + 3 * s + 2))
                    dve.scalar_tensor_tensor(out=ga[s], in0=ga[s], scalar=0.5, in1=fin[s], op0=ALU.mult,
                                             op1=ALU.mult).then_inc(dch, 1)
                    dve.wait_ge(dch, g * 6 + (DB + 3 * s + 3))
                    dve.wait_ge(xr_ld[s], g * 16 + 16)
                    dve.tensor_tensor(fin[s], ga[s], xr[s], ALU.add).then_inc(fin_ok, 1)

        @block.gpsimd
        def _(pool):
            pool.sem_inc(qkf_free, 4)
            pool.sem_inc(x_lo_ok, 2)
            pool.memset(ident[:, :], 0.0).then_inc(pch, 1)
            pool.wait_ge(pch, 1)
            pool.affine_select(out=ident[:, :], in_=ident[:, :], compare_op=ALU.not_equal, fill=1.0,
                               base=0, pattern=[[-1, P]], channel_multiplier=1).then_inc(ident_ok, 1)
            pool.memset(ident16[:, :], 0.0)
            pool.memset(identh[:, :], 0.0)
            pool.memset(later[:, :], 0.0).then_inc(pch, 1)
            pool.iota(q_off[:, :, :], pattern=[[-P, QT], [P, QT]], base=0, channel_multiplier=-1,
                      allow_small_or_imprecise_dtypes=True)
            pool.iota(k_bias[:, :], pattern=[[0, H]], base=0, channel_multiplier=1,
                      allow_small_or_imprecise_dtypes=True).then_inc(kb_ok, 1)
            pool.wait_ge(pch, 2)
            pool.affine_select(out=ident16[:, :], in_=ident16[:, :], compare_op=ALU.not_equal, fill=SS,
                               base=0, pattern=[[-1, P]], channel_multiplier=1)
            pool.affine_select(out=identh[:, :], in_=identh[:, :], compare_op=ALU.not_equal, fill=1.0,
                               base=0, pattern=[[-1, P]], channel_multiplier=1)
            pool.affine_select(out=later[:, :], in_=later[:, :], compare_op=ALU.is_ge, fill=-60000.0,
                               base=0, pattern=[[1, P]], channel_multiplier=-1).then_inc(pch, 1)
            pool.wait_ge(pch, 3)
            pool.memset(below, 1.0)
            pool.memset(zero16, 0.0)
            pool.memset(ones16, 1.0)
            pool.memset(tri16, 1.0).then_inc(kch, 1)
            pool.iota(iota3, pattern=[[0, 3], [1, NB]], base=0, channel_multiplier=0, allow_small_or_imprecise_dtypes=True)
            pool.iota(thr, pattern=[[P, NT]], base=0, channel_multiplier=0, allow_small_or_imprecise_dtypes=True)
            pool.iota(tok_id, pattern=[[P, NT]], base=0, channel_multiplier=1, allow_small_or_imprecise_dtypes=True)
            pool.wait_ge(kch, 1)
            pool.affine_select(out=below, in_=below, compare_op=ALU.is_gt, fill=0.0, base=0,
                               pattern=[[1, E], [-1, E]], channel_multiplier=0)
            pool.affine_select(out=tri16, in_=tri16, compare_op=ALU.is_gt, fill=0.0, base=0,
                               pattern=[[1, P]], channel_multiplier=-1).then_inc(pch, 1)
            with pool.Fori(0, NT // 2) as g:
                for s in range(2):
                    pool.wait_ge(x_hi, g * 2 + (s + 1))
                    pool.tensor_tensor(x16[s][:, 1, :], xn[s], x16[s][:, 0, :], ALU.subtract).then_inc(x_lo_ok, 1)

            def qk_lo(r, s):
                pool.wait_ge(qk_hi, r * 4 + (s + 1))
                pool.tensor_tensor(qk_p[1][s], qk_f[s], qk_p[0][s], ALU.subtract).then_inc(qkf_free, 1)

            with pool.Fori(0, 8) as r:
                for s in range(TG):
                    qk_lo(r, s)
            pool.wait_ge(go_list, 1)
            pool.memset(v_sb[:, :, :, HD:HD + 1], 1.0).then_inc(pch, 1)
            pool.wait_ge(pch, 5)

            pool.wait_ge(rstd_ok, 3)
            for s in range(TG):
                pool.wait_ge(qk_st[s], 8 * 2 * 16 + 16)
            for b in range(B):
                r = ks[b][AUG:KR, :]
                v = r.rearrange("p (j k) -> p j k", j=QT)
                pool.memset(r, SS).then_inc(kch, 1)
                pool.wait_ge(kch, 3 * b + 2)
                pool.affine_select(out=v, in_=v, compare_op=ALU.is_ge, fill=0.0, base=0,
                                   pattern=[[-3, QT], [0, P]], channel_multiplier=1).then_inc(kch, 1)
                pool.wait_ge(kch, 3 * b + 3)
                pool.affine_select(out=v, in_=v, compare_op=ALU.is_ge, fill=0.0, base=2,
                                   pattern=[[3, QT], [0, P]], channel_multiplier=-1).then_inc(kch, 1)
            pool.wait_ge(kch, 3 * B + 1)
            pool.sem_inc(consts_ok, 1)
            pool.iota(rel, pattern=[[1, S]], base=P - S, channel_multiplier=-1,
                      allow_small_or_imprecise_dtypes=True).then_inc(alibi_ok, 1)
            pool.wait_ge(alibi_ok, 1)
            pool.wait_ge(const_ld[3], 16)

            no_key = pool.to_reg(-1.0e9 * SS)
            with pool.Fori(0, H // 2) as g:
                for hh in range(2):
                    pool.wait_ge(slope_rel, g * 2 + (hh + 1))
                    pool.sem_inc(slope_seen, 1)
                    pool.affine_select(out=alibi[hh], in_=alibi[hh], compare_op=ALU.is_ge, fill=no_key,
                                       base=S - P, pattern=[[-1, S]], channel_multiplier=1).then_inc(alibi_ok, 1)

            def gather(g4, q):
                if g4 is not FIRST:
                    pool.wait_ge(tp2, g4 * 4 + (q - 1))
                    pool.sem_inc(pl_seen, 1)
                b = q if g4 is FIRST else g4 * 4 + q
                pool.tensor_copy(idx1[q][:, :], tok_idx[:, bass.ds(b, 1)]).then_inc(ix_ok, 1)
                pool.wait_ge(ix_ok, b + 1)
                pool.sem_inc(pl_seen, 1)
                pool.indirect_dma_start(xg[q], None, x_tab,
                                        bass.IndirectOffsetOnAxis(ap=idx1[q][:, :].bitcast(U32), axis=0))\
                    .then_inc(xg_ld[q], 16)

            def store(b, s):
                pool.wait_ge(y_ok, b + 3)
                pool.sem_inc(pl_seen, 1)
                pool.dma_start(y_tab[bass.ds(b * P, P), :], ysb[s]).then_inc(y_st[s], 16)

            FIRST = None

            def four_blocks(g, gathers):
                for q in range(4):
                    if q < gathers:
                        gather(g + (q + 7) // 4, (q + 7) % 4)
                    store(g * 4 + q, q % 2)

            pool.wait_ge(o_out, HEADS + 1)
            for q in range(4):
                gather(FIRST, q)
            for q in range(3):
                gather(1, q)
            with pool.Fori(0, NB // 4 - 2) as g:
                four_blocks(g, 4)
            four_blocks(NB // 4 - 2, 1)
            four_blocks(NB // 4 - 1, 0)
            for s in range(2):
                pool.wait_ge(y_st[s], NB // 2 * 16)

            def fetch_outputs(g2, s):
                pool.wait_ge(ya_ok, g2 * 2 + (s + 1))
                pool.sem_inc(pl_seen, 1)
                pool.tensor_copy(idx8[s][:, :], slot_idx[:, bass.ds(g2 * 2 + s, 1), :].rearrange("p t k -> p (t k)"))\
                    .then_inc(ix_ok, 1)
                pool.wait_ge(ix_ok, g2 * 2 + (NB + s + 1))
                pool.sem_inc(pl_seen, 1)
                for k in range(K):
                    pool.indirect_dma_start(yg[s][:, k, :], None, y_tab,
                                            bass.IndirectOffsetOnAxis(ap=idx8[s][:, k:k + 1].bitcast(U32), axis=0))\
                        .then_inc(yg_ld[s], 16)

            with pool.Fori(0, NT // 2) as g:
                for s in range(2):
                    fetch_outputs(g, s)


_INS = ['L0_attn_hidden_states', 'L0_attn_qkv_w', 'L0_attn_qkv_b', 'L0_attn_out_w', 'L0_attn_out_b',
        'L0_attn_alibi_slopes', 'L0_ffn_router_w', 'L0_ffn_w_gate', 'L0_ffn_w_up', 'L0_ffn_w_down']
_OUTS = [((2, 1024, 512), 'float32')]


def kernel(**inputs):
    import numpy as _np
    import concourse.bacc as _bacc
    from concourse import mybir as _mybir
    from concourse.bass_utils import run_bass_kernel_spmd as _run

    nc = _bacc.Bacc("TRN2", target_bir_lowering=False, num_devices=1)
    arrays, args = {}, []
    for name in _INS:
        a = _np.ascontiguousarray(inputs[name])
        arrays[f"in_{name}_dram"] = a
        args.append(nc.dram_tensor(f"in_{name}_dram", a.shape, _mybir.dt.from_np(a.dtype), kind="ExternalInput").ap())
    for i, (shape, dtype) in enumerate(_OUTS):
        dt = _mybir.dt.from_np(_np.dtype(dtype))
        args.append(nc.dram_tensor(f"out_{i}_dram", shape, dt, kind="ExternalOutput").ap())
    attention_times_moe_kernel(nc, *args)
    r = _run(nc, [arrays], core_ids=[0])
    got = tuple(r.results[0][f"out_{i}_dram"] for i in range(len(_OUTS)))
    return got[0]
```

```python
from contextlib import ExitStack

import concourse.bass as bass
from concourse import mybir

ALU = mybir.AluOpType
ACT = mybir.ActivationFunctionType
AX_X = mybir.AxisListType.X
F32 = mybir.dt.float32
F16 = mybir.dt.float16
I32 = mybir.dt.int32
U32 = mybir.dt.uint32

SX = 16.0
SW = 64.0
UNSCALE = 1.0 / (SX * SW)
SROUTE = 4096.0


def attention_times_moe_kernel(nc, x, qkv_w, qkv_b, out_w, out_b, slopes, router_w, w_gate, w_up, w_down, out):
    B, S, D = x.shape
    H = slopes.shape[0]
    HD = D // H
    E, _, I = w_gate.shape
    P = 128
    T = B * S
    NT = T // P
    C = D // P
    QT = S // P
    RQ = 3 * D // P
    RO = D // P
    NTOK = 512
    TG = T // NTOK
    SUB = NTOK // P
    IA, IB = P, I - P
    EPS = 1e-5
    SS = SX * SX
    SCRATCH = 12800
    K = 8
    NB = T * K // P + E
    assert NB % 4 == 0 and NB * 3 <= 512
    NW = C * 2 * 2 * I + 4 * D
    WSLOTS = 3
    WD = C * 2 * 2 * I
    assert IB == 64 and TG == 4 and C == 4 and QT == 8 and B == 2

    x_t = x.rearrange("b (t p) d -> p (b t) d", p=P)
    out_t = out.rearrange("b (t p) d -> p (b t) d", p=P)
    qkvw_t = qkv_w.rearrange("(r p) d -> p r d", p=P)
    outw_t = out_w.rearrange("(r p) d -> p r d", p=P)
    qk_dram = nc.dram_tensor("qk_parts", [2, 2 * D, T], F16, kind="Internal").ap()

    o_dram = nc.dram_tensor("o_sums", [D, T], F32, kind="Internal").ap()
    den_dram = nc.dram_tensor("o_dens", [H, T], F32, kind="Internal").ap()
    rden_dram = nc.dram_tensor("o_rdens", [H, T], F32, kind="Internal").ap()

    x_tab = nc.dram_tensor("x_parts", [T, 2 * D], F16, kind="Internal").ap()
    w_tab = nc.dram_tensor("w_parts", [E, P, NW], F16, kind="Internal").ap()
    y_sum = [nc.dram_tensor(f"y_sum{i}", [T + P, D], F32, kind="Internal").ap() for i in range(2)]

    with ExitStack() as ctx:
        def sb(name, shape, dt=F32):
            return ctx.enter_context(nc.sbuf_tensor(name, shape, dt))

        def sem(name):
            return ctx.enter_context(nc.semaphore(name))

        bank = ctx.enter_context(nc.psum_tensor("bank", [P, 8, 512], F32))

        ident = sb("ident", [P, P])
        wT = [sb(f"wT{i}", [P, C, RQ + RO, P], F16) for i in range(2)]
        rT = [sb(f"rT{i}", [P, C, E], F16) for i in range(2)]
        xT_all = sb("xT_all", [P, 2, C, NT, P], F16)
        xT = [xT_all[:, i, :, :, :] for i in range(2)]
        wbuf = xT_all[:, :, :, :, :].rearrange("p i c t q -> p (i c t q)")
        wraw = wbuf[:, 0:8192].bitcast(F32)
        wg_raw, wu_raw = (wraw[:, i * C * I:(i + 1) * C * I].rearrange("p (c i) -> p c i", c=C) for i in range(2))
        wda_raw, wdb_raw = (wraw[:, 2 * C * I + i * D:2 * C * I + (i + 1) * D] for i in range(2))
        w16 = wbuf[:, 8192:8192 + NW]
        w16_gu = w16[:, 0:WD].rearrange("p (c j q) -> p c j q", c=C, j=2)
        w16_d = w16[:, WD:NW].rearrange("p (a j d) -> p a j d", a=2, j=2)
        wslot = wbuf[:, 0:WSLOTS * NW].rearrange("p (s f) -> p s f", s=WSLOTS)
        v_sb = sb("v_sb", [P, NT, H, HD + 1])
        v_flat = v_sb[:, :, :, :].rearrange("p t h d -> p (t h d)")
        o_all = sb("o_all", [P, NT, D])
        o_T = o_all[:, :, :].rearrange("p t d -> p (t d)").rearrange("p (c k) -> p c k", c=C)
        route = sb("route", [P, NT, E])
        qk_scale = sb("qk_scale", [P, 8])
        qk_bias = sb("qk_bias", [P, 8])
        v_bias = sb("v_bias", [P, D])
        o_bias = sb("o_bias", [P, D])
        slope1 = sb("slope1", [P, H])
        slope = sb("slope", [P, H])
        rwst = sb("rwst", [E, D])
        scratch = sb("scratch", [P, SCRATCH])
        mvs = sb("mvs", [P, NT, 2])
        stats = sb("stats", [P, NT, 6])
        rstd = sb("rstd", [P, NT])
        small = sb("small", [P, 4, NT])
        top8 = sb("top8", [P, NT, 8])
        mn = sb("mn", [P, QT])
        NR = H * T // P
        rden = sb("rden", [P, NR])
        ident16 = sb("ident16", [P, P], F16)
        identh = sb("identh", [P, P], F16)
        later = sb("later", [P, P], F16)
        q_off = sb("q_off", [P, QT, QT])
        k_bias4 = sb("k_bias4", [P, 4])
        k_bias = sb("k_bias", [P, H])
        rows_f = sb("rows_f", [P, QT, QT])
        rows16 = sb("rows16", [P, QT, QT, 3], F16)

        slot_idx = sb("slot_idx", [P, NT, K], I32)
        row_idx = sb("row_idx", [P, NB], I32)
        idx_y = [sb(f"idx_y{i}", [P, 1], I32) for i in range(2)]
        blank = sb("blank", [P, NB])
        tok_idx = sb("tok_idx", [P, NB], I32)
        idx1 = [sb(f"idx1_{i}", [P, 1], I32) for i in range(4)]
        slot_w = sb("slot_w", [P, NB])
        slot_wl = sb("slot_wl", [P, NB])
        expert_of = sb("expert_of", [1, NB], I32)
        slot_wait = sb("slot_wait", [1, E], I32)

        def carve(at, shape, dt=F32):
            n = 1
            for d in shape[1:]:
                n *= d
            words = n if dt == F32 else n // 2
            v = scratch[:, at:at + words]
            if dt != F32:
                v = v.bitcast(dt)
            if len(shape) == 3:
                v = v.rearrange("p (a b) -> p a b", a=shape[1])
            return v, at + words

        at = 0
        wst, xn, qk_f, qk_p = [], [], [], [[], []]
        for i in range(4):
            v, at = carve(at, [P, D]); wst.append(v)
        for i in range(2):
            v, at = carve(at, [P, D]); xn.append(v)
        for i in range(4):
            v, at = carve(at, [P, NTOK]); qk_f.append(v)
        for j in range(2):
            for i in range(4):
                v, at = carve(at, [P, NTOK], F16); qk_p[j].append(v)
        rl, at = carve(at, [P, NT, E])
        rr, at = carve(at, [P, NT, E])
        x16 = []
        for i in range(2):
            v, at = carve(at, [P, 2, D], F16); x16.append(v)
        below, at = carve(at, [P, E, E])
        iota3, at = carve(at, [P, 3, NB])
        thr, at = carve(at, [P, NT])
        tok_id, at = carve(at, [P, NT])
        own_row, at = carve(at, [P, 1])
        zero16, at = carve(at, [P, 512], F16)
        tri16, at = carve(at, [P, P], F16)
        ones16, at = carve(at, [P, P], F16)
        assert at <= SCRATCH - S - S // 2, at
        rel, at = carve(SCRATCH - S - S // 2, [P, S])
        k_rows, at = carve(at, [P, S], F16)
        xfree = o_all[:, :, :].rearrange("p t d -> p (t d)")
        at = 0

        def carve_x(at, shape, dt=F32):
            n = 1
            for d in shape[1:]:
                n *= d
            words = n if dt != F16 else n // 2
            v = xfree[:, at:at + words]
            if dt != F32:
                v = v.bitcast(dt)
            if len(shape) == 3:
                v = v.rearrange("p (a b) -> p a b", a=shape[1])
            return v, at + words

        mask16, at = carve_x(at, [P, NT, E], F16)
        carry, at = carve_x(at, [P, NT + 1, E])
        val, at = carve_x(at, [P, NT, E])
        over, at = carve_x(at, [P, E, NT])
        nblk, at = carve_x(at, [P, E])
        first, at = carve_x(at, [P, E])
        base, at = carve_x(at, [P, E])
        s8f, at = carve_x(at, [P, NT, K])
        w8, at = carve_x(at, [P, NT, K])
        blk_i, at = carve_x(at, [P, NT * K], I32)
        low_i, at = carve_x(at, [P, NT * K], I32)
        blk_f, at = carve_x(at, [P, NT * K])
        low_f, at = carve_x(at, [P, NT * K])
        tab_f, at = carve_x(at, [P, NB])
        payload, at = carve_x(at, [P, NT * K, 3], F16)
        rhs, oh = [], []
        for i in range(2):
            v, at = carve_x(at, [P, 4, 3 * NB], F16); rhs.append(v)
            v, at = carve_x(at, [P, 4, P], F16); oh.append(v)
        assert at <= NT * D
        eq = v_flat[:, 0:NT * K * E].rearrange("p (t k e) -> p t k e", t=NT, k=K)
        cmp_e = v_flat[0:1, 0:NB * (E - 1)].rearrange("p (b e) -> p b e", b=NB)
        at = 0
        qs, ks, pr, alibi = [], [], [], []
        for i in range(2):
            v, at = carve(at, [P, S], F16); qs.append(v)
            v, at = carve(at, [P, S], F16); ks.append(v)
        for i in range(2):
            qs.append(wbuf[:, (5 + i) * S:(6 + i) * S])
            ks.append(wbuf[:, 8192 + (5 + i) * S:8192 + (6 + i) * S])
        assert 5 * S >= 4 * (C * I + D) and 5 * S >= NW
        tb, at = carve(at, [P, S])
        for i in range(2):
            v, at = carve(at, [P, S]); pr.append(v)
        for i in range(2):
            v, at = carve(at, [P, S]); alibi.append(v)
        o_sb, v_cur = [], []
        for i in range(2):
            v, at = carve(at, [P, S]); o_sb.append(v)
        for i in range(2):
            v, at = carve(at, [P, QT, HD + 1]); v_cur.append(v)
        assert at <= SCRATCH - S - S // 2, at
        at = 0
        xg, xb, ysb, h16, hT = [], [], [], [], []
        for i in range(4):
            v, at = carve(at, [P, 2 * D], F16); xg.append(v)
        for i in range(2):
            v, at = carve(at, [P, 2 * C, P], F16); xb.append(v)
            v, at = carve(at, [P, D]); ysb.append(v)
            v, at = carve(at, [P, 3, P], F16); h16.append(v)
            v, at = carve(at, [P, 3, P], F16); hT.append(v)
        tA, at = carve(at, [P, I])
        h_f, at = carve(at, [P, I])
        assert at <= SCRATCH, at
        rb = [v_flat[:, i * D:(i + 1) * D].rearrange("p (c k) -> p c k", c=C) for i in range(4)]
        xr = [v_flat[:, i * D:(i + 1) * D] for i in range(4, 8)]
        at = 0
        ya = []
        oT, on, th, ga, fin = [], [], [], [], []
        for i in range(2):
            v, at = carve(at, [P, C, P], F16)
            w, at = carve(at, [P, C, P], F16); oT.append([v, w])
            v, at = carve(at, [P, C, P]); on.append(v)
            v, at = carve(at, [P, D]); th.append(v)
            v, at = carve(at, [P, D]); ga.append(v)
            v, at = carve(at, [P, D]); fin.append(v)
        for i in range(4):
            v, at = carve(at, [P, 2, D]); ya.append(v)
        assert at <= SCRATCH, at

        const_ld = [sem(f"const_ld{i}") for i in range(6)]
        x_ld = [sem(f"x_ld{i}") for i in range(4)]
        wst_ld = [sem(f"wst_ld{i}") for i in range(4)]
        ident_ok = sem("ident_ok")
        tp_full = sem("tp_full")
        tp_hi = sem("tp_hi")
        tp_lo = sem("tp_lo")
        var_ok = sem("var_ok")
        std_ok = sem("std_ok")
        rstd_ok = sem("rstd_ok")
        xn_ok = sem("xn_ok")
        proj_full = sem("proj_full")
        proj_free = sem("proj_free")
        qkf_free = sem("qkf_free")
        qk_hi = sem("qk_hi")
        qk_st = [sem(f"qk_st{i}") for i in range(4)]
        logits_ok = sem("logits_ok")
        ev_act = sem("ev_act")
        rch = sem("rch")
        consts_ok = sem("consts_ok")
        kb_ok = sem("kb_ok")
        dch = sem("dch")
        pch = sem("pch")
        kch = sem("kch")
        qk_in = [sem(f"qk_in{i}") for i in range(4)]
        slope_rel = sem("slope_rel")
        alibi_ok = sem("alibi_ok")
        s_full = sem("s_full")
        scores_seen = sem("scores_seen")
        slope_seen = sem("slope_seen")
        maxima_seen = sem("maxima_seen")
        s_free = sem("s_free")
        rows_ok = sem("rows_ok")
        rows_t = sem("rows_t")
        rows_in = sem("rows_in")
        st_full = sem("st_full")
        p_ok = sem("p_ok")
        pv_done = sem("pv_done")
        o_out = sem("o_out")
        v_ok = sem("v_ok")
        o_st = [sem(f"o_st{i}") for i in range(2)]
        ot_ld = sem("ot_ld")
        den_ld = sem("den_ld")
        rden_ok = sem("rden_ok")
        rden_st = sem("rden_st")
        wraw_ld = sem("wraw_ld")
        w16_hi = sem("w16_hi")
        w16_lo = sem("w16_lo")
        w_st = sem("w_st")
        x_hi = sem("x_hi")
        x_lo_ok = sem("x_lo_ok")
        x16_st = [sem(f"x16_st{i}") for i in range(2)]
        rt = sem("rt")
        mask_ok = sem("mask_ok")
        cnt_ok = sem("cnt_ok")
        go_list = sem("go_list")
        oh_ok = sem("oh_ok")
        rhs_ok = sem("rhs_ok")
        lst_used = sem("lst_used")
        v_free = sem("v_free")
        pq = sem("pq")
        w_ld = sem("w_ld")
        sp_seen = sem("sp_seen")
        ix_ok = sem("ix_ok")
        iy_ok = sem("iy_ok")
        pl_seen = sem("pl_seen")
        xg_ld = [sem(f"xg_ld{i}") for i in range(4)]
        tp2 = sem("tp2")
        xb_ok = sem("xb_ok")
        gu_ok = sem("gu_ok")
        tanh_ok = sem("tanh_ok")
        a_ok = sem("a_ok")
        hf_ok = sem("hf_ok")
        h_hi = sem("h_hi")
        t2 = sem("t2")
        ht_ok = sem("ht_ok")
        h_lo = sem("h_lo")
        y_full = sem("y_full")
        y_ok = sem("y_ok")
        y_st = [sem(f"y_st{i}") for i in range(2)]
        rb_ld = [sem(f"rb_ld{i}") for i in range(4)]
        ya_ld = [sem(f"ya_ld{i}") for i in range(4)]
        z_st = sem("z_st")
        ya_ok = sem("ya_ok")
        on_ok = sem("on_ok")
        ot_hi = sem("ot_hi")
        ot_lo = sem("ot_lo")
        s_out = sem("s_out")
        th_ok = sem("th_ok")
        fin_ok = sem("fin_ok")
        xr_ld = [sem(f"xr_ld{i}") for i in range(4)]
        out_st = [sem(f"out_st{i}") for i in range(2)]

        block = ctx.enter_context(nc.Block())

        NI_W = RQ + RO
        NI_R = NI_W + 1
        NI = NI_R + NT
        NPROJ = 8 * TG
        HEADS = B * H
        PAIR = [(hh, b) for hh in range(2) for b in range(B)]
        NL = len(PAIR)
        AUG = 3 * HD
        KR = AUG + 3 * QT

        @block.sync
        def _(sp):
            for s in range(TG):
                sp.sem_inc(qk_st[s], 16)
            for s in range(2):
                sp.sem_inc(out_st[s], 16)
                sp.sem_inc(o_st[s], 32)
                sp.sem_inc(x16_st[s], 16)
            sp.sem_inc(w_st, 16)
            for i in range(4):
                sp.dma_start(o_all[:, 4 * i:4 * i + 4, :], x_t[:, 4 * i:4 * i + 4, :]).then_inc(x_ld[i], 16)
            sp.dma_start(qk_bias[:, :], qkv_b[0:2 * D].rearrange("(r p) -> p r", p=P),
                         allow_slow_non_contiguous=True).then_inc(const_ld[0], 16)
            sp.dma_start(v_bias[:, :], qkv_b[2 * D:3 * D].partition_broadcast(P)).then_inc(const_ld[1], 16)
            sp.dma_start(o_bias[:, :], out_b.partition_broadcast(P)).then_inc(const_ld[2], 16)
            sp.dma_start(slope[:, :], slopes.partition_broadcast(P)).then_inc(const_ld[3], 16)
            sp.dma_start(rwst[:, :], router_w).then_inc(const_ld[4], 16)
            for s in range(4):
                sp.dma_start(wst[s], qkvw_t[:, s, :]).then_inc(wst_ld[s], 16)
            with sp.Fori(0, RQ // 4 - 1) as g:
                for s in range(4):
                    sp.wait_ge(tp_full, g * 4 + (s + 1))
                    sp.dma_start(wst[s], qkvw_t[:, bass.ds(g * 4 + (s + 4), 1), :].rearrange("p r d -> p (r d)"))\
                        .then_inc(wst_ld[s], 16)
            for s in range(RO):
                sp.wait_ge(tp_full, RQ + s - 3)
                sp.dma_start(wst[s], outw_t[:, s, :]).then_inc(wst_ld[s], 16)
            with sp.Fori(0, NT // 2) as g:
                for s in range(2):
                    sp.wait_ge(x_lo_ok, g * 2 + (s + 3))
                    sp.dma_start(x_tab[bass.ds((g * 2 + s) * P, P), :], x16[s].rearrange("p j d -> p (j d)"))\
                        .then_inc(x16_st[s], 16)
            for s in range(2):
                sp.wait_ge(x16_st[s], NT // 2 * 16 + 16)
            sp.wait_ge(pch, 4)
            zeros = zero16.bitcast(F32)
            for i in range(2):
                for half in range(2):
                    sp.dma_start(y_sum[i].rearrange("(t p) d -> p t d", p=P)[:, :, half * D // 2:(half + 1) * D // 2],
                                 zeros.unsqueeze(1).broadcast_to([P, NT + 1, D // 2])).then_inc(z_st, 16)
            with sp.Fori(0, 8) as r:
                for s in range(TG):
                    sp.wait_ge(qkf_free, r * 4 + (s + 5))
                    for j in range(2):
                        sp.dma_start(qk_dram[j, bass.ds(r * P, P), s * NTOK:(s + 1) * NTOK],
                                     qk_p[j][s]).then_inc(qk_st[s], 16)
            for s in range(TG):
                sp.wait_ge(qk_st[s], 8 * 2 * 16 + 16)
            sp.wait_ge(rstd_ok, 3)
            sp.wait_ge(v_free, NT + 4)
            sp.wait_ge(kch, 4)

            def load_head(g, l):
                row, b = (g * 2 + PAIR[l][0]) * HD, PAIR[l][1]
                tok = slice(b * S, (b + 1) * S)
                for k, j in enumerate((0, 0, 1)):
                    sp.dma_start(qs[l][HD * k:HD * (k + 1), :],
                                 qk_dram[j, bass.ds(row, HD), tok]).then_inc(qk_in[l], 16)
                for k, j in enumerate((0, 1, 0)):
                    sp.dma_start(ks[l][HD * k:HD * (k + 1), :],
                                 qk_dram[j, bass.ds(row + D, HD), tok]).then_inc(qk_in[l], 16)

            def store_head(h, b):
                tok = slice(b * S, (b + 1) * S)
                sp.wait_ge(o_out, h * 2 + (b + 2))
                sp.dma_start(o_dram[bass.ds(h * HD, HD), tok], o_sb[b][0:HD, :]).then_inc(o_st[b], 16)
                sp.dma_start(den_dram[bass.ds(h, 1), tok], o_sb[b][HD:HD + 1, :]).then_inc(o_st[b], 16)

            def load_weights(e):
                sp.dma_start(wg_raw, w_gate[bass.ds(e, 1), :, :].rearrange("e (c p) i -> p (e c) i", p=P))\
                    .then_inc(wraw_ld, 16)
                sp.dma_start(wu_raw, w_up[bass.ds(e, 1), :, :].rearrange("e (c p) i -> p (e c) i", p=P))\
                    .then_inc(wraw_ld, 16)
                sp.dma_start(wda_raw, w_down[bass.ds(e, 1), 0:IA, :].rearrange("e p d -> p (e d)"))\
                    .then_inc(wraw_ld, 16)
                for k in range(2):
                    sp.dma_start(wdb_raw[IB * k:IB * (k + 1), :],
                                 w_down[bass.ds(e, 1), IA:I, :].rearrange("e p d -> p (e d)"))\
                        .then_inc(wraw_ld, 16)

            def store_weights(e):
                sp.wait_ge(w16_lo, e + 1)
                sp.dma_start(w_tab[bass.ds(e, 1), :, :].rearrange("e p f -> p (e f)"), w16).then_inc(w_st, 16)

            def four_heads(g, tail):
                for l, (hh, b) in enumerate(PAIR):
                    if not tail:
                        sp.wait_ge(st_full, g * (NL * QT) + (l + 1) * QT)
                        load_head(g + 1, l)
                    store_weights(g * NL + l)
                    if not (tail and l == NL - 1):
                        load_weights(g * NL + (l + 1))
                    else:
                        sp.wait_ge(w_st, E * 16)
                        sp.dma_start(wslot[:, 0, :], w_tab[0:1, :, :].rearrange("e p f -> p (e f)")).then_inc(w_ld, 16)
                    store_head(g * 2 + hh, b)

            load_head(0, 0)
            for l in range(NL):
                sp.dma_start(ks[l][AUG:KR, :], k_rows[AUG:KR, :]).then_inc(consts_ok, 16)
            for l in range(1, NL):
                load_head(0, l)
            load_weights(0)
            with sp.Fori(0, H // 2 - 1) as g:
                four_heads(g, False)
            four_heads(H // 2 - 1, True)
            for b in range(B):
                sp.wait_ge(o_st[b], 32 * H + 32)
            sp.dma_start(o_T, o_dram.rearrange("(c p) t -> p c t", p=P)).then_inc(ot_ld, 16)
            sp.dma_start(rden[:, :], den_dram.rearrange("h (a k) -> (h a) k", k=NR)).then_inc(den_ld, 16)
            sp.wait_ge(o_out, HEADS + 1)
            sp.wait_ge(w_st, E * 16 + 16)

            def load_slot(g, s):
                e = g * WSLOTS + s
                sp.wait_ge(w_ld, g * (16 * WSLOTS) + 16 * s)
                sp.sem_inc(sp_seen, 1)
                free_at = sp.value_load(slot_wait[0:1, bass.ds(e, 1)], min_val=1, max_val=NB + 2)
                sp.wait_ge(y_full, free_at)
                sp.sem_inc(sp_seen, 1)
                sp.dma_start(wslot[:, s, :], w_tab[bass.ds(e, 1), :, :].rearrange("e p f -> p (e f)"))\
                    .then_inc(w_ld, 16)

            for s in range(1, WSLOTS):
                load_slot(0, s)
            with sp.Fori(0, E // WSLOTS - 1) as g:
                for s in range(WSLOTS):
                    load_slot(g + 1, s)
            for s in range(E % WSLOTS):
                load_slot(E // WSLOTS, s)
            sp.wait_ge(rden_ok, 1)
            sp.dma_start(rden_dram.rearrange("h (a k) -> (h a) k", k=NR), rden[:, :]).then_inc(rden_st, 16)
            sp.wait_ge(rden_st, 16)

            def load_early(g, q):
                t = g * 4 + q
                for k in range(P // HD):
                    rows = rden_dram.rearrange("(c q) t -> q c t", c=C)[k:k + 1, :, bass.ds(t * P, P)]\
                        .broadcast_to([HD, C, P])
                    sp.dma_start(rb[q][k * HD:(k + 1) * HD, :, :], rows).then_inc(rb_ld[q], 16)
                sp.dma_start(xr[q], x_t[:, bass.ds(t, 1), :].rearrange("p t d -> p (t d)")).then_inc(xr_ld[q], 16)

            def load_sums(g, q):
                for i in range(2):
                    sp.dma_start(ya[q][:, i, :], y_sum[i][bass.ds((g * 4 + q) * P, P), :]).then_inc(ya_ld[q], 16)

            def store_tile(g, q):
                sp.wait_ge(fin_ok, g * 4 + (q + 3))
                sp.dma_start(out_t[:, bass.ds(g * 4 + q, 1), :].rearrange("p t d -> p (t d)"), fin[q % 2])\
                    .then_inc(out_st[q % 2], 16)

            for q in range(4):
                load_early(0, q)
            sp.wait_ge(y_ok, NB + 2)
            for s in range(2):
                sp.wait_ge(y_st[s], NB // 2 * 16)
            for q in range(4):
                load_sums(0, q)
            with sp.Fori(0, NT // 4 - 1) as g:
                for q in range(4):
                    store_tile(g, q)
                    load_early(g + 1, q)
                    load_sums(g + 1, q)
            for q in range(4):
                store_tile(NT // 4 - 1, q)
            for s in range(2):
                sp.wait_ge(out_st[s], NT // 2 * 16 + 16)

        @block.tensor
        def _(pe):
            pe.sem_inc(rows_t, 1)
            pe.sem_inc(pv_done, 2)
            for given in (y_full, tp2, gu_ok, lst_used, t2):
                pe.sem_inc(given, 2)
            pe.sem_inc(s_out, 2)
            pe.wait_ge(ident_ok, 1)

            def turn(src, rows, n_bank):
                view = bank[:, n_bank, :].rearrange("p (c q) -> p c q", c=C)
                for c in range(C):
                    last = pe.transpose(view[:, c, 0:rows], src[0:rows, c * P:(c + 1) * P], ident[0:rows, 0:rows])
                return last.then_inc(tp_full, 1)

            with pe.Fori(0, RQ // 4) as g:
                for s in range(4):
                    pe.wait_ge(wst_ld[s], g * 16 + 16)
                    pe.wait_ge(tp_lo, g * 4 + (s + 1))
                    turn(wst[s], P, s % 2)
            for s in range(RO):
                pe.wait_ge(wst_ld[s], (RQ // 4 + 1) * 16)
                pe.wait_ge(tp_lo, RQ + s + 1)
                turn(wst[s], P, s % 2)
            pe.wait_ge(const_ld[4], 16)
            pe.wait_ge(tp_lo, NI_W + 1)
            turn(rwst, E, 0)
            with pe.Fori(0, NT // 2) as g:
                for s in range(2):
                    pe.wait_ge(xn_ok, g * 2 + (s + 1))
                    pe.wait_ge(tp_lo, g * 2 + (NI_R + s + 1))
                    turn(xn[s], P, (1 + s) % 2)
            pe.wait_ge(tp_lo, NI + 2)

            def three(o, aT, b, first=True, last=True, **kw):
                for k, (i, j) in enumerate(((0, 0), (0, 1), (1, 0))):
                    ins = pe.matmul(o, aT(i), b(j), start=first and k == 0, stop=last and k == 2, **kw)
                return ins

            for t in range(NT):
                for c in range(C):
                    ins = three(bank[:, 4, t * E:(t + 1) * E], lambda i: xT[i][:, c, t, :],
                                lambda j: rT[j][:, c, :], c == 0, c == C - 1)
            ins.then_inc(logits_ok, 1)

            def qk_tile(r, s):
                pe.wait_ge(proj_free, r * 4 + (s + 1))
                for c in range(C):
                    ins = three(bank[:, s, :],
                                lambda i: wT[i][:, c, bass.ds(r, 1), :].rearrange("p r q -> p (r q)"),
                                lambda j: xT[j][:, c, SUB * s:SUB * (s + 1), :].rearrange("p t q -> p (t q)"),
                                c == 0, c == C - 1)
                ins.then_inc(proj_full, 1)

            def list_step(i, s):
                pe.wait_ge(oh_ok, i + 1)
                pe.wait_ge(rhs_ok, i + 1)
                for q in range(4):
                    ins = pe.matmul(bank[:, 7, 0:3 * NB], oh[s][:, q, :], rhs[s][:, q, :], start=False, stop=False)
                ins.then_inc(lst_used, 1)

            for s in range(TG):
                qk_tile(0, s)
            pe.wait_ge(pch, 4)
            pe.wait_ge(mask_ok, 1)
            m16 = mask16.rearrange("p t e -> p (t e)")
            pe.matmul(bank[:, 5, :], tri16, m16, start=True, stop=True)
            pe.matmul(bank[:, 6, :], ones16, m16, start=True, stop=True).then_inc(cnt_ok, 1)
            pe.matmul(bank[:, 7, :], zero16[:, 0:P], zero16, start=True, stop=False)
            with pe.Fori(0, 3) as r:
                for s in range(TG):
                    qk_tile(r + 1, s)
            with pe.Fori(0, 4) as r:
                for s in range(TG):
                    qk_tile(r + 4, s)
                    list_step(r * 4 + s, s % 2)
            pe.wait_ge(proj_free, NPROJ + 4)
            with pe.Fori(0, NT // 4) as g:
                for s in range(4):
                    pe.wait_ge(v_free, g * 4 + (s + 1))
                    for c in range(C):
                        ins = three(bank[:, s, :],
                                    lambda i: xT[i][:, c, bass.ds(g * 4 + s, 1), :].rearrange("p t q -> p (t q)"),
                                    lambda j: wT[j][:, c, 8:12, :].rearrange("p r q -> p (r q)"),
                                    c == 0, c == C - 1)
                    ins.then_inc(pq, 1)
                    list_step(g * 4 + (NT + s), s % 2)
            pe.matmul(bank[:, 7, :], zero16[:, 0:P], zero16, start=False, stop=True).then_inc(cnt_ok, 1)
            pe.wait_ge(v_free, NT + 4)

            def scores(n, g, l, k):
                i = QT - 1 - k
                if k == 0:
                    pe.wait_ge(qk_in[l], g * 96 + 96)
                pe.wait_ge(s_free, n * QT + (k if k > QT // 2 else k + 1))
                if k == 0:
                    pe.wait_ge(rows_in, n + 1)
                keys = (i + 1) * P
                for a in range(0, keys, 512):
                    w = min(512, keys - a)
                    ins = pe.matmul(bank[:, a // 512 if k < QT // 2 else k % 2, 0:w], qs[l][0:AUG, i * P:(i + 1) * P],
                                    ks[l][0:AUG, a:a + w], start=True, stop=True)
                ins.then_inc(s_full, 1)

            def shift_rows(n):
                pe.wait_ge(rows_ok, n + 1)
                t = bank[:, 0, :].bitcast(F16)
                for i in range(QT):
                    ins = pe.transpose(t[0:3 * QT, i * P:(i + 1) * P],
                                       rows16[:, i, :, :].rearrange("p j r -> p (j r)"), identh[:, :])
                ins.then_inc(rows_t, 1)

            def scores_t(n, l, j):
                if j == 0:
                    pe.wait_ge(rows_in, n + 2)
                pe.wait_ge(p_ok, n * QT + (j + 1))
                queries = S - j * P
                for a in range(0, queries, 512):
                    w = min(512, queries - a)
                    ins = pe.matmul(bank[:, 2 + 2 * (j % 2) + a // 512, 0:w], ks[l][0:KR, j * P:(j + 1) * P],
                                    qs[l][0:KR, j * P + a:j * P + a + w], start=True, stop=a > 0)
                    if a == 0:
                        ins = pe.matmul(bank[:, 2 + 2 * (j % 2), 0:P], ident16[:, :], later[:, :],
                                        start=False, stop=True)
                ins.then_inc(st_full, 1)

            def values(n, l, j):
                pe.wait_ge(p_ok, n * QT + (j + 3))
                if j == 0:
                    pe.wait_ge(v_ok, n + 1)
                    pe.wait_ge(o_out, n + 1)
                for half in range(2):
                    a, z = max(j * P, half * 512), (half + 1) * 512
                    if a < z:
                        ins = pe.matmul(bank[0:HD + 1, 6 + half, a - half * 512:512], v_cur[l % 2][:, j, :],
                                        pr[j % 2][:, a - j * P:z - j * P], start=(j == 0),
                                        stop=(j == 4 * half + 3))
                ins.then_inc(pv_done, 1)

            def four_heads(g, tail):
                for l, (hh, b) in enumerate(PAIR):
                    n = g * NL + l
                    more = not (tail and l == NL - 1)
                    g1, l1 = g + (l + 1) // NL, (l + 1) % NL
                    for j in range(QT):
                        if more and j == 0:
                            scores(n + 1, g1, l1, 0)
                        if more and j == 6:
                            shift_rows(n + 1)
                        scores_t(n, l, j)
                        if more and 0 < 2 * j <= QT:
                            scores(n + 1, g1, l1, 2 * j - 1)
                        if j:
                            values(n, l, j - 1)
                        if more and 0 < 2 * j < QT:
                            scores(n + 1, g1, l1, 2 * j)
                    values(n, l, QT - 1)

            pe.wait_ge(consts_ok, 16 * NL)
            for k in range(QT):
                scores(0, 0, 0, k)
            shift_rows(0)
            with pe.Fori(0, H // 2 - 1) as g:
                four_heads(g, False)
            four_heads(H // 2 - 1, True)
            pe.wait_ge(o_out, HEADS + 1)

            def turn_block(g4, q):
                s = q % 2
                pe.wait_ge(xg_ld[q], g4 * 16 + 16)
                pe.wait_ge(xb_ok, g4 * 4 + (q + 1))
                t = bank[:, s, :].bitcast(F16).rearrange("p (c q) -> p c q", c=2 * C)
                for c in range(2 * C):
                    ins = pe.transpose(t[:, c, :], xg[q][:, c * P:(c + 1) * P], identh[:, :])
                ins.then_inc(tp2, 1)

            def gate_up(b, s, e):
                pe.wait_ge(w_ld, e * 16 + 16)
                pe.wait_ge(xb_ok, b + 3)
                pe.wait_ge(hf_ok, b + 1)
                for c in range(C):
                    ins = three(bank[:, 2 + s, 0:2 * I], lambda i: xb[s][:, i * C + c, :],
                                lambda j: wslot[:, bass.ds(e % WSLOTS, 1), (c * 2 + j) * 2 * I:(c * 2 + j + 1) * 2 * I]
                                .rearrange("p s q -> p (s q)"), c == 0, c == C - 1)
                ins.then_inc(gu_ok, 1)

            def turn_hidden(b, s):
                pe.wait_ge(h_lo, b + 1)
                pe.wait_ge(ht_ok, b + 1)
                t = bank[:, 6 + s, :].bitcast(F16).rearrange("p (c q) -> p c q", q=P)
                for m in range(3):
                    ins = pe.transpose(t[:, m, :], h16[s][:, m, :], identh[:, :])
                ins.then_inc(t2, 1)

            def down(b, s, e):
                def wd(a, j, rows):
                    at_ = WD + (a * 2 + j) * D
                    return wslot[0:rows, bass.ds(e % WSLOTS, 1), at_:at_ + D].rearrange("p s d -> p (s d)")
                pe.wait_ge(ht_ok, b + 3)
                pe.wait_ge(y_ok, b + 1)
                y = bank[:, 4 + s, :]
                three(y, lambda i: hT[s][:, i, :], lambda j: wd(0, j, P), True, False)
                pe.matmul(y, hT[s][:, 2, :], wd(1, 0, P), start=False, stop=False)
                pe.matmul(y, hT[s][0:IB, 2, :], wd(1, 1, IB), start=False, stop=True).then_inc(y_full, 1)

            def expert(b):
                return pe.value_load(expert_of[0:1, bass.ds(b, 1)], min_val=0, max_val=E - 1)

            def four_blocks(g, tail):
                e = {}
                for q in range(4):
                    b = g * 4 + q
                    if q < 2 or not tail:
                        e[q + 2] = expert(b + 2)
                    if q == 0:
                        turn_block(g, 3)
                    elif not tail:
                        turn_block(g + 1, q - 1)
                    if q < 2 or not tail:
                        gate_up(b + 2, q % 2, e[q + 2])
                    if q < 2:
                        e[q] = expert(b)
                    if q < 3 or not tail:
                        turn_hidden(b + 1, (q + 1) % 2)
                    down(b, q % 2, e[q])

            turn_block(0, 0)
            turn_block(0, 1)
            gate_up(0, 0, expert(0))
            turn_block(0, 2)
            gate_up(1, 1, expert(1))
            turn_hidden(0, 0)
            with pe.Fori(0, NB // 4 - 1) as g:
                four_blocks(g, False)
            four_blocks(NB // 4 - 1, True)
            pe.wait_ge(y_ok, NB + 2)

            with pe.Fori(0, NT // 2) as g:
                for s in range(2):
                    pe.wait_ge(ot_lo, g * 2 + (s + 3))
                    pe.wait_ge(fin_ok, g * 2 + (s + 1))
                    for c in range(C):
                        ins = three(bank[:, 2 + s, :], lambda i: oT[s][i][:, c, :],
                                    lambda j: wT[j][:, c, 12:16, :].rearrange("p r q -> p (r q)"),
                                    c == 0, c == C - 1)
                    ins.then_inc(s_out, 1)

        @block.scalar
        def _(act):
            act.sem_inc(rows_in, 1)
            act.sem_inc(p_ok, 2)
            act.sem_inc(xb_ok, 2)
            act.wait_ge(var_ok, 1)
            act.activation(small[:, 0, :], small[:, 1, :], ACT.Sqrt, scale=1.0 / (SX * SX)).then_inc(std_ok, 1)

            def bank4(n):
                return bank[:, n, :].rearrange("p (c q) -> p c q", c=C)

            with act.Fori(0, (RQ + RO) // 4) as g:
                for s in range(4):
                    act.wait_ge(tp_full, g * 4 + (s + 1))
                    act.activation(wT[0][:, :, bass.ds(g * 4 + s, 1), :].rearrange("p c r q -> p c (r q)"),
                                   bank4(s % 2), ACT.Copy, scale=SW).then_inc(tp_hi, 1)
            act.wait_ge(tp_full, NI_R)
            act.activation(rT[0][:, :, :], bank4(0)[:, :, 0:E], ACT.Copy, scale=SW).then_inc(tp_hi, 1)
            with act.Fori(0, NT // 2) as g:
                for s in range(2):
                    act.wait_ge(tp_full, g * 2 + (NI_R + s + 1))
                    act.activation(xT[0][:, :, bass.ds(g * 2 + s, 1), :].rearrange("p c t q -> p c (t q)"),
                                   bank4((1 + s) % 2), ACT.Copy).then_inc(tp_hi, 1)
                    act.wait_ge(x16_st[s], g * 16 + 16)
                    act.activation(x16[s][:, 0, :], xn[s], ACT.Copy).then_inc(x_hi, 1)
            act.wait_ge(rstd_ok, 2)
            act.activation(rl, rr, ACT.Exp).then_inc(ev_act, 1)
            with act.Fori(0, 8) as r:
                for s in range(TG):
                    act.wait_ge(proj_full, r * 4 + (s + 1))
                    act.sem_inc(maxima_seen, 1)
                    act.wait_ge(qkf_free, r * 4 + (s + 1))
                    act.sem_inc(maxima_seen, 1)
                    act.activation(qk_f[s], bank[:, s, :], ACT.Identity, scale=qk_scale[:, bass.ds(r, 1)],
                                   bias=qk_bias[:, bass.ds(r, 1)]).then_inc(proj_free, 1)
                    act.wait_ge(proj_free, r * 4 + (s + 5))
                    act.wait_ge(qk_st[s], r * 32 + 16)
                    act.activation(qk_p[0][s], qk_f[s], ACT.Copy).then_inc(qk_hi, 1)

            def head_bias(h, hh):
                act.activation(alibi[hh], rel, ACT.Copy, scale=slope[:, bass.ds(h, 1)]).then_inc(slope_rel, 1)

            def rows_under_q(n, l):
                act.wait_ge(rows_t, n + 2)
                act.activation(qs[l][AUG:KR, :], bank[0:3 * QT, 0, :].bitcast(F16), ACT.Copy).then_inc(rows_in, 1)

            def lay_values(h, l):
                b = PAIR[l][1]
                act.activation(v_cur[l % 2], v_sb[:, b * QT:(b + 1) * QT, bass.ds(h, 1), :]
                               .rearrange("p j h d -> p j (h d)"), ACT.Copy).then_inc(v_ok, 1)

            def split_hi(e, k):
                if k == 0:
                    act.wait_ge(wraw_ld, e * 80 + 80)
                    act.sem_inc(maxima_seen, 1)
                    act.wait_ge(w_st, e * 16 + 16)
                    act.sem_inc(maxima_seen, 1)
                to, raw = ((w16_gu[:, :, 0, 0:I], wg_raw), (w16_gu[:, :, 0, I:2 * I], wu_raw),
                           (w16_d[:, 0, 0, :], wda_raw), (w16_d[:, 1, 0, :], wdb_raw))[k]
                act.activation(to, raw, ACT.Copy, scale=SW).then_inc(w16_hi, 1)

            def softmax(n, l, j):
                act.wait_ge(st_full, n * QT + (j + 1))
                act.wait_ge(pv_done, n * QT + (j + 1))
                act.activation(pr[j % 2][:, 0:S - j * P],
                               bank[:, 2 + 2 * (j % 2):4 + 2 * (j % 2), :].rearrange("p a k -> p (a k)")[:, 0:S - j * P],
                               ACT.Exp, scale=1.0 / SS, bias=k_bias4[:, l:l + 1]).then_inc(p_ok, 1)

            def four_heads(g, tail):
                for l, (hh, b) in enumerate(PAIR):
                    n = g * NL + l
                    if b == 1 and not tail:
                        act.wait_ge(s_free, n * QT + (QT + 1))
                        act.sem_inc(maxima_seen, 1)
                        head_bias(g * 2 + (hh + 2), hh)
                    for j in range(QT):
                        if j == 6 and not (tail and l == NL - 1):
                            rows_under_q(n + 1, (l + 1) % NL)
                        softmax(n, l, j)
                        if 3 <= j < 7:
                            split_hi(n, j - 3)
                        if j == 3 and not (tail and l == NL - 1):
                            lay_values(g * 2 + (hh + b), (l + 1) % NL)

            act.wait_ge(kb_ok, 2)
            act.wait_ge(alibi_ok, 1)
            act.wait_ge(rstd_ok, 3)
            act.wait_ge(qkf_free, NPROJ + 4)
            act.wait_ge(pch, 5)
            for s in range(TG):
                act.wait_ge(qk_st[s], 8 * 2 * 16 + 16)
            for hh in range(2):
                head_bias(hh, hh)
            act.wait_ge(v_free, NT + 4)
            lay_values(0, 0)
            rows_under_q(0, 0)
            with act.Fori(0, H // 2 - 1) as g:
                four_heads(g, False)
            four_heads(H // 2 - 1, True)

            def take_block(b, s):
                act.wait_ge(tp2, b + 3)
                act.wait_ge(gu_ok, b + 1)
                act.activation(xb[s].rearrange("p c q -> p (c q)"), bank[:, s, :].bitcast(F16), ACT.Copy).then_inc(xb_ok, 1)

            def tanh_gate(b, s):
                act.wait_ge(gu_ok, b + 3)
                act.wait_ge(hf_ok, b + 2)
                act.activation(tA, bank[:, 2 + s, 0:I], ACT.Tanh, scale=0.5 * UNSCALE).then_inc(tanh_ok, 1)

            def hidden_hi(b, s):
                act.wait_ge(hf_ok, b + 3)
                act.wait_ge(t2, b + 1)
                act.activation(h16[s][:, 0, :], h_f[:, 0:IA], ACT.Copy)
                act.activation(h16[s][:, 2, 0:IB], h_f[:, IA:I], ACT.Copy).then_inc(h_hi, 1)

            def step(b, s, blocks, hiddens):
                if blocks:
                    take_block(b + 3, 1 - s)
                if hiddens:
                    tanh_gate(b + 2, s)
                    hidden_hi(b + 2, s)

            act.wait_ge(o_out, HEADS + 1)
            take_block(0, 0)
            take_block(1, 1)
            tanh_gate(0, 0)
            hidden_hi(0, 0)
            take_block(2, 0)
            tanh_gate(1, 1)
            hidden_hi(1, 1)
            with act.Fori(0, NB // 2 - 2) as g:
                for s in range(2):
                    step(g * 2 + s, s, True, True)
            for b in range(NB - 4, NB):
                step(b, b % 2, b + 3 < NB, b + 2 < NB)

            with act.Fori(0, NT // 4) as g:
                for q in range(4):
                    act.wait_ge(on_ok, g * 4 + (q + 3))
                    act.wait_ge(s_out, g * 4 + (q + 1))
                    act.activation(oT[q % 2][0], on[q % 2], ACT.Copy, scale=SX).then_inc(ot_hi, 1)
                    act.wait_ge(fin_ok, g * 4 + (q + 1))
                    act.wait_ge(ya_ok, g * 4 + (q + 3))
                    act.activation(th[q % 2], ya[q][:, 0, :], ACT.Tanh, scale=0.5).then_inc(th_ok, 1)

        @block.vector
        def _(dve):
            dve.sem_inc(tp_lo, 2)
            dve.sem_inc(proj_free, 4)
            dve.sem_inc(s_free, 1)
            dve.sem_inc(o_out, 1)
            dve.sem_inc(v_free, 4)
            dve.sem_inc(y_ok, 2)
            dve.sem_inc(on_ok, 2)
            dve.sem_inc(ht_ok, 2)
            dve.sem_inc(ya_ok, 2)
            dve.sem_inc(hf_ok, 2)
            dve.sem_inc(ot_lo, 2)
            dve.sem_inc(fin_ok, 2)

            def bank4(n):
                return bank[:, n, :].rearrange("p (c q) -> p c q", c=C)

            for i in range(4):
                dve.wait_ge(x_ld[i], 16)
                for t in range(4 * i, 4 * i + 4):
                    ins = dve.bn_stats(stats[:, t, :], o_all[:, t, :])
            ins.then_inc(dch, 1)
            dve.wait_ge(dch, 1)
            for t in range(NT):
                ins = dve.bn_aggr(mvs[:, t, :], stats[:, t, :])
            ins.then_inc(dch, 1)
            dve.wait_ge(dch, 2)
            dve.tensor_scalar(small[:, 1, :], mvs[:, :, 1], EPS, None, ALU.add).then_inc(var_ok, 1)
            dve.wait_ge(std_ok, 1)
            dve.reciprocal(rstd[:, :], small[:, 0, :]).then_inc(dch, 1)
            dve.wait_ge(dch, 3)
            dve.wait_ge(const_ld[3], 16)
            dve.tensor_copy(slope1[:, :], slope[:, :])
            dve.tensor_scalar(slope[:, :], slope[:, :], SS, None, ALU.mult).then_inc(rstd_ok, 1)
            dve.wait_ge(kb_ok, 1)
            dve.wait_ge(rstd_ok, 1)
            dve.tensor_tensor(k_bias[:, :], k_bias[:, :], slope1[:, :], ALU.mult).then_inc(kb_ok, 1)
            dve.memset(qk_scale[:, 0:4], UNSCALE * SX * HD ** -0.5)
            dve.memset(qk_scale[:, 4:8], UNSCALE * SX)
            dve.wait_ge(const_ld[0], 16)
            dve.tensor_scalar(qk_bias[:, 0:4], qk_bias[:, 0:4], SX * HD ** -0.5, None, ALU.mult)
            dve.tensor_scalar(qk_bias[:, 4:8], qk_bias[:, 4:8], SX, None, ALU.mult).then_inc(dch, 1)
            dve.wait_ge(dch, 4)

            with dve.Fori(0, (RQ + RO) // 4) as g:
                for s in range(4):
                    hi, lo = (wT[i][:, :, bass.ds(g * 4 + s, 1), :].rearrange("p c r q -> p c (r q)") for i in range(2))
                    dve.wait_ge(tp_hi, g * 4 + (s + 1))
                    dve.scalar_tensor_tensor(out=lo, in0=bank4(s % 2), scalar=SW, in1=hi,
                                             op0=ALU.mult, op1=ALU.subtract).then_inc(tp_lo, 1)
            dve.wait_ge(tp_hi, NI_R)
            dve.scalar_tensor_tensor(out=rT[1][:, :, :], in0=bank4(0)[:, :, 0:E], scalar=SW, in1=rT[0][:, :, :],
                                     op0=ALU.mult, op1=ALU.subtract).then_inc(tp_lo, 1)

            def normalise(t, s):
                dve.wait_ge(tp_full, t + (NI_R - 1))
                dve.wait_ge(x_lo_ok, t + 1)
                dve.tensor_scalar(xn[s], o_all[:, bass.ds(t, 1), :].rearrange("p t d -> p (t d)"),
                                  mvs[:, bass.ds(t, 1), 0:1].rearrange("p t d -> p (t d)"), rstd[:, bass.ds(t, 1)],
                                  ALU.subtract, ALU.mult).then_inc(xn_ok, 1)

            def x_lo(t, s):
                hi, lo = (xT[i][:, :, bass.ds(t, 1), :].rearrange("p c t q -> p c (t q)") for i in range(2))
                dve.wait_ge(tp_hi, t + (NI_R + 1))
                dve.scalar_tensor_tensor(out=lo, in0=bank4((1 + s) % 2), scalar=1.0, in1=hi,
                                         op0=ALU.mult, op1=ALU.subtract).then_inc(tp_lo, 1)

            normalise(0, 0)
            with dve.Fori(0, NT // 2 - 1) as g:
                for s in range(2):
                    normalise(g * 2 + (s + 1), (s + 1) % 2)
                    x_lo(g * 2 + s, s)
            normalise(NT - 1, 1)
            x_lo(NT - 2, 0)
            x_lo(NT - 1, 1)
            dve.wait_ge(logits_ok, 1)
            lg = bank[:, 4, :].rearrange("p (t e) -> p t e", e=E)
            dve.tensor_scalar(rl, lg, UNSCALE, None, ALU.mult).then_inc(rt, 1)
            dve.wait_ge(rt, 1)
            dve.tensor_reduce(small[:, 2, :], rl, AX_X, ALU.max).then_inc(rt, 1)
            dve.wait_ge(rt, 2)
            dve.tensor_tensor(rr, rl, small[:, 2, :].unsqueeze(2).broadcast_to([P, NT, E]), ALU.subtract)\
                .then_inc(rstd_ok, 1)
            dve.wait_ge(ev_act, 1)
            for t in range(NT):
                ins = dve.max(top8[:, t, :], rl[:, t, :])
            ins.then_inc(rt, 1)
            dve.wait_ge(rt, 3)
            for t in range(NT):
                ins = dve.match_replace(rr[:, t, :], top8[:, t, :], rl[:, t, :], -1.0)
            ins.then_inc(rt, 1)
            dve.tensor_reduce(small[:, 3, :], top8[:, :, :], AX_X, ALU.add).then_inc(rt, 1)
            dve.wait_ge(rt, 5)
            dve.tensor_scalar(mask16, rr, 0.0, None, ALU.is_lt).then_inc(mask_ok, 1)
            dve.reciprocal(small[:, 2, :], small[:, 3, :]).then_inc(rt, 1)
            dve.memset(carry[:, 0, :], 0.0).then_inc(rt, 1)
            dve.wait_ge(mask_ok, 1)
            dve.tensor_tensor(rr, rl, mask16, ALU.mult).then_inc(rt, 1)
            dve.wait_ge(rt, 8)
            dve.tensor_tensor(route[:, :, :], rr, small[:, 2, :].unsqueeze(2).broadcast_to([P, NT, E]), ALU.mult)\
                .then_inc(rt, 1)
            dve.wait_ge(cnt_ok, 1)
            for t in range(NT):
                dve.wait_ge(rt, 9 + t)
                dve.tensor_tensor(carry[:, t + 1, :], carry[:, t, :], bank[:, 6, t * E:(t + 1) * E], ALU.add)\
                    .then_inc(rt, 1)
            R = 9 + NT
            dve.wait_ge(rt, R)
            dve.tensor_tensor(over, carry[:, NT, :].unsqueeze(2).broadcast_to([P, E, NT]),
                              thr.unsqueeze(1).broadcast_to([P, E, NT]), ALU.is_gt).then_inc(rt, 1)
            dve.wait_ge(rt, R + 1)
            dve.tensor_reduce(nblk, over, AX_X, ALU.add).then_inc(rt, 1)
            dve.wait_ge(rt, R + 2)
            dve.tensor_scalar(nblk, nblk, 1.0, None, ALU.max).then_inc(rt, 1)
            dve.wait_ge(rt, R + 3)
            dve.wait_ge(pch, 4)
            dve.tensor_tensor(below, below, nblk.unsqueeze(1).broadcast_to([P, E, E]), ALU.mult).then_inc(rt, 1)
            dve.wait_ge(rt, R + 4)
            dve.tensor_reduce(first, below, AX_X, ALU.add).then_inc(rt, 1)
            dve.tensor_tensor(val, carry[:, 0:NT, :], bank[:, 5, :].rearrange("p (t e) -> p t e", e=E), ALU.add)\
                .then_inc(rt, 1)
            dve.wait_ge(rt, R + 6)
            dve.tensor_scalar(base, first, float(P), 1.0, ALU.mult, ALU.add).then_inc(rt, 1)
            dve.wait_ge(rt, R + 7)
            dve.tensor_tensor(val, val, base.unsqueeze(1).broadcast_to([P, NT, E]), ALU.add).then_inc(rt, 1)
            dve.wait_ge(rt, R + 8)
            dve.tensor_tensor(val, val, mask16, ALU.mult).then_inc(rt, 1)
            dve.wait_ge(rt, R + 9)
            for t in range(NT):
                ins = dve.max(s8f[:, t, :], val[:, t, :])
            ins.then_inc(rt, 1)
            dve.wait_ge(rt, R + 10)
            dve.tensor_tensor(eq, val.unsqueeze(2).broadcast_to([P, NT, K, E]),
                              s8f.unsqueeze(3).broadcast_to([P, NT, K, E]), ALU.is_equal).then_inc(rt, 1)
            dve.wait_ge(rt, R + 11)
            dve.tensor_tensor(eq, eq, route[:, :, :].unsqueeze(2).broadcast_to([P, NT, K, E]), ALU.mult)\
                .then_inc(rt, 1)
            dve.tensor_scalar(slot_idx[:, :, :], s8f, -1.0, None, ALU.add).then_inc(rt, 1)
            dve.wait_ge(rt, R + 13)
            dve.tensor_reduce(w8, eq, AX_X, ALU.add).then_inc(rt, 1)
            si = slot_idx[:, :, :].rearrange("p t k -> p (t k)")
            dve.tensor_scalar(blk_i, si, 7, None, ALU.arith_shift_right).then_inc(rt, 1)
            dve.tensor_scalar(low_i, si, P - 1, None, ALU.bitwise_and).then_inc(rt, 1)
            dve.wait_ge(rt, R + 16)
            dve.tensor_copy(low_f, low_i)
            dve.tensor_copy(blk_f, blk_i).then_inc(rt, 1)
            pay = payload.rearrange("p (t k) j -> p t k j", t=NT)
            dve.tensor_copy(pay[:, :, :, 0], tok_id.unsqueeze(2).broadcast_to([P, NT, K])).then_inc(rt, 1)
            dve.tensor_scalar(pay[:, :, :, 1], w8, SROUTE, None, ALU.mult).then_inc(rt, 1)
            dve.wait_ge(rt, R + 19)
            dve.scalar_tensor_tensor(out=pay[:, :, :, 2], in0=w8, scalar=SROUTE, in1=pay[:, :, :, 1],
                                     op0=ALU.mult, op1=ALU.subtract).then_inc(rt, 1)
            dve.tensor_tensor(cmp_e, first[0:1, 1:E].unsqueeze(1).broadcast_to([1, NB, E - 1]),
                              iota3[0:1, 0, :].unsqueeze(2).broadcast_to([1, NB, E - 1]), ALU.is_le).then_inc(rt, 1)
            dve.wait_ge(rt, R + 21)
            dve.tensor_reduce(tab_f[0:1, :], cmp_e, AX_X, ALU.add).then_inc(rt, 1)
            dve.tensor_scalar(slot_wait[0:1, 0:WSLOTS], first[0:1, 0:WSLOTS], 0.0, 1.0, ALU.mult, ALU.add)
            dve.tensor_scalar(slot_wait[0:1, WSLOTS:E], first[0:1, 1:E - WSLOTS + 1], 2.0, None, ALU.add)\
                .then_inc(rt, 1)
            dve.wait_ge(rt, R + 23)
            dve.tensor_copy(expert_of[0:1, :], tab_f[0:1, :]).then_inc(rt, 1)
            dve.wait_ge(rt, R + 24)
            dve.sem_inc(go_list, 1)

            def list_step(i, s):
                dve.wait_ge(lst_used, i + 1)
                dve.tensor_tensor(oh[s], iota3[:, 0, 0:P].unsqueeze(1).broadcast_to([P, 4, P]),
                                  low_f[:, bass.ds(i * 4, 4)].unsqueeze(2).broadcast_to([P, 4, P]), ALU.is_equal)\
                    .then_inc(oh_ok, 1)
                for q in range(4):
                    ins = dve.scalar_tensor_tensor(
                        out=rhs[s][:, q, :].rearrange("p (j b) -> p j b", j=3), in0=iota3,
                        scalar=blk_f[:, bass.ds(i * 4 + q, 1)],
                        in1=payload[:, bass.ds(i * 4 + q, 1), :].rearrange("p a j -> p (a j)").unsqueeze(2)
                        .broadcast_to([P, 3, NB]), op0=ALU.is_equal, op1=ALU.mult)
                ins.then_inc(rhs_ok, 1)

            with dve.Fori(0, NT // 2) as g:
                for s in range(2):
                    list_step(g * 2 + s, s)
            dve.wait_ge(const_ld[1], 16)
            with dve.Fori(0, NT // 4) as g:
                for s in range(4):
                    list_step(g * 4 + (NT + s), s % 2)
                    dve.wait_ge(pq, g * 4 + (s + 1))
                    dve.scalar_tensor_tensor(
                        out=v_sb[:, bass.ds(g * 4 + s, 1), :, 0:HD].rearrange("p t h d -> p (t h) d"),
                        in0=bank[:, s, :].rearrange("p (h d) -> p h d", h=H), scalar=UNSCALE,
                        in1=v_bias[:, :].rearrange("p (h d) -> p h d", h=H),
                        op0=ALU.mult, op1=ALU.add).then_inc(v_free, 1)
            dve.wait_ge(cnt_ok, 2)
            dve.tensor_scalar(tok_idx[:, :], bank[:, 7, 0:NB], -1.0, 0.0, ALU.add, ALU.max)
            dve.tensor_scalar(blank[:, :], bank[:, 7, 0:NB], 0.0, own_row, ALU.is_equal, ALU.mult)
            dve.tensor_scalar(slot_wl[:, :], bank[:, 7, 2 * NB:3 * NB], UNSCALE / SROUTE, None, ALU.mult)\
                .then_inc(rt, 1)
            dve.wait_ge(rt, R + 25)
            dve.scalar_tensor_tensor(out=row_idx[:, :], in0=bank[:, 7, 0:NB], scalar=-1.0, in1=blank[:, :],
                                     op0=ALU.add, op1=ALU.add)
            dve.scalar_tensor_tensor(out=slot_w[:, :], in0=bank[:, 7, NB:2 * NB], scalar=UNSCALE / SROUTE,
                                     in1=slot_wl[:, :], op0=ALU.mult, op1=ALU.add).then_inc(rstd_ok, 1)

            def row_max(n, k, hh):
                i = QT - 1 - k
                keys = (i + 1) * P
                if k == 0:
                    dve.wait_ge(alibi_ok, n[1] + 2)
                dve.wait_ge(s_full, n[0] * QT + (k + 1))
                dve.sem_inc(scores_seen, 1)
                s_ = bank[:, 0:2, :].rearrange("p a k -> p (a k)") if k < QT // 2 else bank[:, k % 2, :]
                at_ = 0 if k < QT // 2 else k % 2 * 512
                dve.tensor_tensor_reduce(tb[:, at_:at_ + keys], s_[:, 0:keys],
                                         alibi[hh][:, S - keys:S], -1.0 / SS, 3.0e38, ALU.add, ALU.min,
                                         mn[:, i:i + 1]).then_inc(s_free, 1)

            def make_rows(n, h, l):
                dve.wait_ge(s_free, n * QT + (QT + 1))
                dve.wait_ge(rows_t, n + 1)
                dve.tensor_scalar(k_bias4[:, l:l + 1], k_bias[:, bass.ds(h, 1)], 1.0, None, ALU.mult)
                dve.scalar_tensor_tensor(out=rows_f[:, :, :], in0=q_off[:, :, :], scalar=slope1[:, bass.ds(h, 1)],
                                         in1=mn[:, :].unsqueeze(2).broadcast_to([P, QT, QT]),
                                         op0=ALU.mult, op1=ALU.add).then_inc(rch, 1)
                dve.wait_ge(rch, n * 4 + 1)
                dve.tensor_copy(rows16[:, :, :, 0], rows_f[:, :, :]).then_inc(rch, 1)
                dve.wait_ge(rch, n * 4 + 2)
                dve.tensor_tensor(rows_f[:, :, :], rows_f[:, :, :], rows16[:, :, :, 0], ALU.subtract).then_inc(rch, 1)
                dve.wait_ge(rch, n * 4 + 3)
                dve.tensor_copy(rows16[:, :, :, 1], rows_f[:, :, :]).then_inc(rch, 1)
                dve.wait_ge(rch, n * 4 + 4)
                dve.tensor_tensor(rows16[:, :, :, 2], rows_f[:, :, :], rows16[:, :, :, 1], ALU.subtract)\
                    .then_inc(rows_ok, 1)

            def split_lo(e):
                hi, lo = w16_gu[:, :, 0, :], w16_gu[:, :, 1, :]
                for k, (to, h, raw) in enumerate(((lo[:, :, 0:I], hi[:, :, 0:I], wg_raw),
                                                  (lo[:, :, I:2 * I], hi[:, :, I:2 * I], wu_raw),
                                                  (w16_d[:, 0, 1, :], w16_d[:, 0, 0, :], wda_raw),
                                                  (w16_d[:, 1, 1, :], w16_d[:, 1, 0, :], wdb_raw))):
                    dve.wait_ge(w16_hi, e * 4 + (k + 1))
                    ins = dve.scalar_tensor_tensor(out=to, in0=raw, scalar=SW, in1=h, op0=ALU.mult, op1=ALU.subtract)
                ins.then_inc(w16_lo, 1)

            def take_output(n, h, b):
                dve.wait_ge(pv_done, n * QT + (QT + 2))
                dve.wait_ge(o_st[b], h * 32 + 32)
                dve.tensor_copy(o_sb[b][0:HD + 1, :], bank[0:HD + 1, 6:8, :].rearrange("p a k -> p (a k)"))\
                    .then_inc(o_out, 1)

            def four_heads(g, tail):
                for l, (hh, b) in enumerate(PAIR):
                    n = g * NL + l
                    if not (tail and l == NL - 1):
                        nh = g * 2 + (hh + b)
                        for k in range(1, QT):
                            row_max((n + 1, nh), k, PAIR[(l + 1) % NL][0])
                        make_rows(n + 1, nh, (l + 1) % NL)
                    split_lo(n)
                    if not (tail and l >= NL - 2):
                        row_max((n + 2, g * 2 + (l + 2) // 2), 0, PAIR[(l + 2) % NL][0])
                    take_output(n, g * 2 + hh, b)

            dve.wait_ge(kb_ok, 2)
            for k in range(QT):
                row_max((0, 0), k, 0)
            make_rows(0, 0, 0)
            row_max((1, 0), 0, 0)
            with dve.Fori(0, H // 2 - 1) as g:
                four_heads(g, False)
            four_heads(H // 2 - 1, True)

            def hidden(b, s):
                dve.wait_ge(tanh_ok, b + 1)
                dve.scalar_tensor_tensor(out=tA, in0=tA, scalar=1.0, in1=bank[:, 2 + s, 0:I],
                                         op0=ALU.add, op1=ALU.mult).then_inc(a_ok, 1)
                dve.wait_ge(a_ok, b + 1)
                dve.scalar_tensor_tensor(out=h_f, in0=bank[:, 2 + s, I:2 * I], scalar=0.5 * UNSCALE * UNSCALE * SX,
                                         in1=tA, op0=ALU.mult, op1=ALU.mult).then_inc(hf_ok, 1)

            def hidden_lo(b, s):
                dve.wait_ge(h_hi, b + 1)
                dve.tensor_tensor(h16[s][:, 1, :], h_f[:, 0:IA], h16[s][:, 0, :], ALU.subtract)
                dve.tensor_tensor(h16[s][:, 2, IB:P], h_f[:, IA:I], h16[s][:, 2, 0:IB], ALU.subtract).then_inc(h_lo, 1)

            def take_hidden(b, s):
                dve.wait_ge(t2, b + 3)
                dve.wait_ge(y_full, b + 1)
                dve.tensor_copy(hT[s].rearrange("p m q -> p (m q)"), bank[:, 6 + s, :].bitcast(F16)[:, 0:3 * P])\
                    .then_inc(ht_ok, 1)

            def weigh(g2, s, first_pair):
                dve.wait_ge(y_full, g2 * 2 + (s + 3))
                if not first_pair:
                    dve.wait_ge(y_st[s], g2 * 16)
                dve.tensor_scalar(ysb[s], bank[:, 4 + s, :], slot_w[:, bass.ds(g2 * 2 + s, 1)], None, ALU.mult)\
                    .then_inc(y_ok, 1)

            def block_pair(g, tail=False, first_pair=False):
                for s in range(2):
                    if not tail:
                        hidden(g * 2 + (s + 2), s)
                    if not (tail and s == 1):
                        take_hidden(g * 2 + (s + 1), 1 - s)
                    if not tail:
                        hidden_lo(g * 2 + (s + 2), s)
                    weigh(g, s, first_pair)

            hidden(0, 0)
            hidden_lo(0, 0)
            hidden(1, 1)
            hidden_lo(1, 1)
            take_hidden(0, 0)
            block_pair(0, first_pair=True)
            dve.wait_ge(den_ld, 16)
            dve.reciprocal(rden[:, :], rden[:, :]).then_inc(rden_ok, 1)
            with dve.Fori(0, NB // 2 - 2) as g:
                block_pair(g + 1)
            block_pair(NB // 2 - 1, tail=True)

            dve.wait_ge(const_ld[2], 16)
            dve.wait_ge(ot_ld, 16)
            dve.wait_ge(y_ok, NB + 2)
            for s in range(2):
                dve.wait_ge(y_st[s], NB // 2 * 16)
            DB = 4

            def prepare(g, q):
                t, s = g * 4 + q, q % 2
                dve.wait_ge(rb_ld[q], g * 64 + 64)
                dve.tensor_tensor(on[s], o_T[:, :, bass.ds(t * P, P)], rb[q], ALU.mult).then_inc(on_ok, 1)
                dve.wait_ge(ya_ld[q], g * 32 + 32)
                dve.tensor_tensor(ya[q][:, 0, :], ya[q][:, 0, :], ya[q][:, 1, :], ALU.add).then_inc(ya_ok, 1)
                dve.wait_ge(ot_hi, t + 1)
                dve.scalar_tensor_tensor(out=oT[s][1], in0=on[s], scalar=SX, in1=oT[s][0],
                                         op0=ALU.mult, op1=ALU.subtract).then_inc(ot_lo, 1)

            def finish(g, q):
                t, s = g * 4 + q, q % 2
                dve.wait_ge(th_ok, t + 1)
                dve.scalar_tensor_tensor(out=ga[s], in0=th[s], scalar=1.0, in1=ya[q][:, 0, :],
                                         op0=ALU.add, op1=ALU.mult).then_inc(dch, 1)
                dve.wait_ge(s_out, t + 3)
                dve.wait_ge(out_st[s], g * 32 + (q // 2 * 16 + 16))
                dve.scalar_tensor_tensor(out=fin[s], in0=bank[:, 2 + s, :], scalar=UNSCALE, in1=o_bias[:, :],
                                         op0=ALU.mult, op1=ALU.add).then_inc(dch, 1)
                dve.wait_ge(dch, t * 3 + (DB + 2))
                dve.scalar_tensor_tensor(out=ga[s], in0=ga[s], scalar=0.5, in1=fin[s], op0=ALU.mult,
                                         op1=ALU.mult).then_inc(dch, 1)
                dve.wait_ge(dch, t * 3 + (DB + 3))
                dve.wait_ge(xr_ld[q], g * 16 + 16)
                dve.tensor_tensor(fin[s], ga[s], xr[q], ALU.add).then_inc(fin_ok, 1)

            prepare(0, 0)
            with dve.Fori(0, NT // 4 - 1) as g:
                for q in range(4):
                    prepare(g + (q + 1) // 4, (q + 1) % 4)
                    finish(g, q)
            for q in range(4):
                if q < 3:
                    prepare(NT // 4 - 1, q + 1)
                finish(NT // 4 - 1, q)

        @block.gpsimd
        def _(pool):
            pool.sem_inc(qkf_free, 4)
            pool.sem_inc(x_lo_ok, 2)
            pool.memset(ident[:, :], 0.0).then_inc(pch, 1)
            pool.wait_ge(pch, 1)
            pool.affine_select(out=ident[:, :], in_=ident[:, :], compare_op=ALU.not_equal, fill=1.0,
                               base=0, pattern=[[-1, P]], channel_multiplier=1).then_inc(ident_ok, 1)
            pool.memset(ident16[:, :], 0.0)
            pool.memset(identh[:, :], 0.0)
            pool.memset(later[:, :], 0.0).then_inc(pch, 1)
            pool.iota(q_off[:, :, :], pattern=[[-P, QT], [P, QT]], base=0, channel_multiplier=-1,
                      allow_small_or_imprecise_dtypes=True)
            pool.iota(k_bias[:, :], pattern=[[0, H]], base=0, channel_multiplier=1,
                      allow_small_or_imprecise_dtypes=True).then_inc(kb_ok, 1)
            pool.wait_ge(pch, 2)
            pool.affine_select(out=ident16[:, :], in_=ident16[:, :], compare_op=ALU.not_equal, fill=SS,
                               base=0, pattern=[[-1, P]], channel_multiplier=1)
            pool.affine_select(out=identh[:, :], in_=identh[:, :], compare_op=ALU.not_equal, fill=1.0,
                               base=0, pattern=[[-1, P]], channel_multiplier=1)
            pool.affine_select(out=later[:, :], in_=later[:, :], compare_op=ALU.is_ge, fill=-60000.0,
                               base=0, pattern=[[1, P]], channel_multiplier=-1).then_inc(pch, 1)
            pool.wait_ge(pch, 3)
            pool.memset(below, 1.0)
            pool.memset(zero16, 0.0)
            pool.memset(ones16, 1.0)
            pool.memset(tri16, 1.0).then_inc(kch, 1)
            pool.iota(iota3, pattern=[[0, 3], [1, NB]], base=0, channel_multiplier=0, allow_small_or_imprecise_dtypes=True)
            pool.iota(thr, pattern=[[P, NT]], base=0, channel_multiplier=0, allow_small_or_imprecise_dtypes=True)
            pool.iota(tok_id, pattern=[[P, NT]], base=1, channel_multiplier=1, allow_small_or_imprecise_dtypes=True)
            pool.iota(own_row, pattern=[[0, 1]], base=T + 1, channel_multiplier=1, allow_small_or_imprecise_dtypes=True)
            pool.wait_ge(kch, 1)
            pool.affine_select(out=below, in_=below, compare_op=ALU.is_gt, fill=0.0, base=0,
                               pattern=[[1, E], [-1, E]], channel_multiplier=0)
            pool.affine_select(out=tri16, in_=tri16, compare_op=ALU.is_gt, fill=0.0, base=0,
                               pattern=[[1, P]], channel_multiplier=-1).then_inc(pch, 1)
            kr = k_rows[AUG:KR, :]
            kv = kr.rearrange("p (j k) -> p j k", j=QT)
            pool.wait_ge(pch, 4)
            pool.memset(kr, SS).then_inc(kch, 1)
            pool.wait_ge(kch, 2)
            pool.affine_select(out=kv, in_=kv, compare_op=ALU.is_ge, fill=0.0, base=0,
                               pattern=[[-3, QT], [0, P]], channel_multiplier=1).then_inc(kch, 1)
            pool.wait_ge(kch, 3)
            pool.affine_select(out=kv, in_=kv, compare_op=ALU.is_ge, fill=0.0, base=2,
                               pattern=[[3, QT], [0, P]], channel_multiplier=-1).then_inc(kch, 1)
            pool.wait_ge(kch, 4)
            pool.iota(rel, pattern=[[1, S]], base=P - S, channel_multiplier=-1,
                      allow_small_or_imprecise_dtypes=True).then_inc(alibi_ok, 1)
            pool.wait_ge(alibi_ok, 1)
            with pool.Fori(0, NT // 2) as g:
                for s in range(2):
                    pool.wait_ge(x_hi, g * 2 + (s + 1))
                    pool.tensor_tensor(x16[s][:, 1, :], xn[s], x16[s][:, 0, :], ALU.subtract).then_inc(x_lo_ok, 1)

            def qk_lo(r, s):
                pool.wait_ge(qk_hi, r * 4 + (s + 1))
                pool.tensor_tensor(qk_p[1][s], qk_f[s], qk_p[0][s], ALU.subtract).then_inc(qkf_free, 1)

            with pool.Fori(0, 8) as r:
                for s in range(TG):
                    qk_lo(r, s)
            pool.wait_ge(go_list, 1)
            pool.memset(v_sb[:, :, :, HD:HD + 1], 1.0).then_inc(pch, 1)
            pool.wait_ge(pch, 5)

            no_key = pool.to_reg(-1.0e9 * SS)
            with pool.Fori(0, H // 2) as g:
                for hh in range(2):
                    pool.wait_ge(slope_rel, g * 2 + (hh + 1))
                    pool.sem_inc(slope_seen, 1)
                    pool.affine_select(out=alibi[hh], in_=alibi[hh], compare_op=ALU.is_ge, fill=no_key,
                                       base=S - P, pattern=[[-1, S]], channel_multiplier=1).then_inc(alibi_ok, 1)

            def gather(g4, q):
                if g4 is not FIRST:
                    pool.wait_ge(tp2, g4 * 4 + (q - 1))
                    pool.sem_inc(pl_seen, 1)
                b = q if g4 is FIRST else g4 * 4 + q
                pool.tensor_copy(idx1[q][:, :], tok_idx[:, bass.ds(b, 1)]).then_inc(ix_ok, 1)
                pool.wait_ge(ix_ok, b + 1)
                pool.sem_inc(pl_seen, 1)
                pool.indirect_dma_start(xg[q], None, x_tab,
                                        bass.IndirectOffsetOnAxis(ap=idx1[q][:, :].bitcast(U32), axis=0))\
                    .then_inc(xg_ld[q], 16)

            def store(g, q):
                b, s = g * 4 + q, q % 2
                if not (isinstance(g, int) and g == 0 and q < 2):
                    pool.wait_ge(y_st[s], g * 32 + q // 2 * 16)
                    pool.sem_inc(pl_seen, 1)
                pool.tensor_copy(idx_y[s][:, :], row_idx[:, bass.ds(b, 1)]).then_inc(iy_ok, 1)
                pool.wait_ge(iy_ok, b + 1)
                pool.sem_inc(pl_seen, 1)
                pool.wait_ge(y_ok, b + 3)
                pool.sem_inc(pl_seen, 1)
                pool.indirect_dma_start(y_sum[s], bass.IndirectOffsetOnAxis(ap=idx_y[s][:, :].bitcast(U32), axis=0),
                                        ysb[s], None, compute_op=ALU.add).then_inc(y_st[s], 16)

            FIRST = None

            def four_blocks(g, gathers):
                for q in range(4):
                    if q < gathers:
                        gather(g + (q + 7) // 4, (q + 7) % 4)
                    store(g, q)

            pool.wait_ge(z_st, 64)
            pool.wait_ge(st_full, (HEADS - 2) * QT)
            for q in range(4):
                gather(FIRST, q)
            for q in range(3):
                gather(1, q)
            four_blocks(0, 4)
            with pool.Fori(0, NB // 4 - 3) as g:
                four_blocks(g + 1, 4)
            four_blocks(NB // 4 - 2, 1)
            four_blocks(NB // 4 - 1, 0)
            for s in range(2):
                pool.wait_ge(y_st[s], NB // 2 * 16)


_INS = ['L0_attn_hidden_states', 'L0_attn_qkv_w', 'L0_attn_qkv_b', 'L0_attn_out_w', 'L0_attn_out_b',
        'L0_attn_alibi_slopes', 'L0_ffn_router_w', 'L0_ffn_w_gate', 'L0_ffn_w_up', 'L0_ffn_w_down']
_OUTS = [((2, 1024, 512), 'float32')]


def kernel(**inputs):
    import numpy as _np
    import concourse.bacc as _bacc
    from concourse import mybir as _mybir
    from concourse.bass_utils import run_bass_kernel_spmd as _run

    nc = _bacc.Bacc("TRN2", target_bir_lowering=False, num_devices=1)
    arrays, args = {}, []
    for name in _INS:
        a = _np.ascontiguousarray(inputs[name])
        arrays[f"in_{name}_dram"] = a
        args.append(nc.dram_tensor(f"in_{name}_dram", a.shape, _mybir.dt.from_np(a.dtype), kind="ExternalInput").ap())
    for i, (shape, dtype) in enumerate(_OUTS):
        dt = _mybir.dt.from_np(_np.dtype(dtype))
        args.append(nc.dram_tensor(f"out_{i}_dram", shape, dt, kind="ExternalOutput").ap())
    attention_times_moe_kernel(nc, *args)
    r = _run(nc, [arrays], core_ids=[0])
    got = tuple(r.results[0][f"out_{i}_dram"] for i in range(len(_OUTS)))
    return got[0]
```
